# Optimizing a Trainium2 kernel written in Bass

```python
import numpy as np
import jax
import jax.numpy as jnp

def _softmax(x, axis=-1):
    return jax.nn.softmax(x, axis=axis)

def _gelu(x):
    return jax.nn.gelu(x, approximate=True)

def _silu(x):
    return jax.nn.silu(x)

def _sigmoid(x):
    return jax.nn.sigmoid(x)

def _layernorm(x, axis=-1, eps=1e-05):
    m = jnp.mean(x, axis=axis, keepdims=True)
    v = jnp.var(x, axis=axis, keepdims=True)
    return (x - m) / jnp.sqrt(v + eps)

def _scatter_add(tgt, idx, src, axis=0):
    return tgt.at[idx].add(src)

def _segment_sum(src, seg, n):
    return jax.ops.segment_sum(src, seg, n)
kernel_name = 'mk_gnn_ffn_d2_gnn_r8_3f9747'

def setup_inputs(seed: int=0):
    np.random.seed(seed)
    _w = jnp.asarray

    def _rec_inputs():
        import jax
        import jax.numpy as jnp
        _gk = jax.random.key(seed)
        x = -8.776e-05 + 1 * jax.random.normal(jax.random.fold_in(_gk, 1), (6250, 256), jnp.float32)
        src = jax.random.randint(jax.random.fold_in(_gk, 2), (100000,), 0, 6250, jnp.int32)
        dst = jnp.minimum((6250 * jax.random.uniform(jax.random.fold_in(_gk, 3), (100000,)) ** 2.0).astype(jnp.int32), 49999)
        _o = jnp.argsort(dst, stable=True)
        src = src[_o]
        dst = dst[_o]
        edge_attr_64 = -5.16925e-05 + 1.00005 * jax.random.normal(jax.random.fold_in(_gk, 12), (100000, 64), jnp.float32)
        return (x, src, dst, edge_attr_64)
    x, src, dst, edge_attr_64 = _rec_inputs()

    def _L0_gnn_setup():
        import jax, jax.numpy as jnp
        import numpy as np
        N = 2500
        E = 40000
        HID = 256
        H = 4
        D = HID // H
        FF = 4 * HID

        def _layernorm(x, g, b, eps=1e-05):
            mu = jnp.mean(x, axis=-1, keepdims=True)
            var = jnp.var(x, axis=-1, keepdims=True)
            return (x - mu) * jax.lax.rsqrt(var + eps) * g + b

        def _transformer_conv(x, edge_index, Wq, bq, Wk, bk, Wv, bv, Wskip, bskip):
            src, dst = (edge_index[0], edge_index[1])
            n = x.shape[0]
            q = (x @ Wq + bq).reshape(n, H, D)
            k = (x @ Wk + bk).reshape(n, H, D)
            v = (x @ Wv + bv).reshape(n, H, D)
            qi = q[dst]
            kj = k[src]
            vj = v[src]
            alpha = jnp.sum(qi * kj, axis=-1) / jnp.sqrt(jnp.float32(D))
            m = jax.ops.segment_max(alpha, dst, num_segments=n)
            ex = jnp.exp(alpha - m[dst])
            denom = jax.ops.segment_sum(ex, dst, num_segments=n)
            a = ex / (denom[dst] + 1e-16)
            out = jax.ops.segment_sum(a[..., None] * vj, dst, num_segments=n)
            out = out.reshape(n, H * D)
            return out + x @ Wskip + bskip
        key = jax.random.key(seed)
        ks = jax.random.split(key, 20)
        w = lambda i, sh: jax.random.normal(ks[i], sh, dtype=jnp.float32) * 0.02
        return {'x': jax.random.normal(ks[0], (N, HID), dtype=jnp.float32), 'edge_index': jax.random.randint(ks[1], (2, E), 0, N, dtype=jnp.int64), 'Wq': w(2, (HID, HID)), 'bq': jnp.zeros((HID,), jnp.float32), 'Wk': w(3, (HID, HID)), 'bk': jnp.zeros((HID,), jnp.float32), 'Wv': w(4, (HID, HID)), 'bv': jnp.zeros((HID,), jnp.float32), 'Wskip': w(5, (HID, HID)), 'bskip': jnp.zeros((HID,), jnp.float32), 'ln1_g': jnp.ones((HID,), jnp.float32), 'ln1_b': jnp.zeros((HID,), jnp.float32), 'W1': w(6, (HID, FF)), 'b1': jnp.zeros((FF,), jnp.float32), 'W2': w(7, (FF, HID)), 'b2': jnp.zeros((HID,), jnp.float32), 'ln2_g': jnp.ones((HID,), jnp.float32), 'ln2_b': jnp.zeros((HID,), jnp.float32)}
    _L0_gnn_all = _L0_gnn_setup()
    _L0_gnn_in = {k: v for k, v in _L0_gnn_all.items() if k in ('Wq', 'bq', 'Wk', 'bk', 'Wv', 'bv', 'Wskip', 'bskip', 'ln1_g', 'ln1_b', 'W1', 'b1', 'W2', 'b2', 'ln2_g', 'ln2_b')}
    del _L0_gnn_all

    def _L0_ffn_setup():
        import jax, jax.numpy as jnp
        import numpy as np
        BN_EPS = 0.001

        def _bn(h, g, b, m, v):
            return g * (h - m) * jax.lax.rsqrt(v + BN_EPS) + b
        key = jax.random.key(seed)
        ks = jax.random.split(key, 8)
        B, F, Df = (256, 64, 256)
        E, H, D = (8, 256, 256)
        s1 = 1.0 / np.sqrt(Df)
        s2 = 1.0 / np.sqrt(H)
        return {'x': jax.random.normal(ks[0], (B, F, Df), jnp.float32), 'Wr': jax.random.normal(ks[1], (Df, E), jnp.float32) * s1, 'br': jnp.zeros((E,), jnp.float32), 'W1': jax.random.normal(ks[2], (E, Df, H), jnp.float32) * s1, 'b1': jnp.zeros((E, H), jnp.float32), 'g1': jnp.ones((E, H), jnp.float32), 'be1': jnp.zeros((E, H), jnp.float32), 'm1': jnp.zeros((E, H), jnp.float32), 'v1': jnp.ones((E, H), jnp.float32), 'W2': jax.random.normal(ks[3], (E, H, H), jnp.float32) * s2, 'b2': jnp.zeros((E, H), jnp.float32), 'g2': jnp.ones((E, H), jnp.float32), 'be2': jnp.zeros((E, H), jnp.float32), 'm2': jnp.zeros((E, H), jnp.float32), 'v2': jnp.ones((E, H), jnp.float32), 'Wo': jax.random.normal(ks[4], (E, H, D), jnp.float32) * s2, 'bo': jnp.zeros((E, D), jnp.float32)}
    _L0_ffn_all = _L0_ffn_setup()
    _L0_ffn_in = {k: v for k, v in _L0_ffn_all.items() if k in ('Wr', 'br', 'W1', 'b1', 'g1', 'be1', 'm1', 'v1', 'W2', 'b2', 'g2', 'be2', 'm2', 'v2', 'Wo', 'bo')}
    del _L0_ffn_all

    def _L1_gnn_setup():
        import jax, jax.numpy as jnp
        import numpy as np
        N = 6250
        E = 200000
        IN_F = 256
        EDGE_F = 64
        HALF = IN_F // 2
        BASE = IN_F + HALF
        OUT_F = 256
        NEG_SLOPE = 0.01
        key = jax.random.key(seed)
        ks = jax.random.split(key, 10)
        x = jax.random.normal(ks[0], (N, IN_F), dtype=jnp.float32)
        edge_index = jax.random.randint(ks[1], (2, E), 0, N, dtype=jnp.int64)
        edge_attr = jax.random.normal(ks[2], (E, EDGE_F), dtype=jnp.float32)
        batch = jnp.sort(jax.random.randint(ks[3], (N,), 0, 512, dtype=jnp.int64))
        W_edge = jax.random.normal(ks[4], (EDGE_F, HALF), dtype=jnp.float32) * 0.05
        b_edge = jnp.zeros((HALF,), dtype=jnp.float32)
        W_conv = jax.random.normal(ks[5], (BASE, OUT_F), dtype=jnp.float32) * 0.05
        b_conv = jnp.zeros((OUT_F,), dtype=jnp.float32)
        W_res = jax.random.normal(ks[6], (BASE, OUT_F), dtype=jnp.float32) * 0.05
        b_res = jnp.zeros((OUT_F,), dtype=jnp.float32)
        return {'x': x, 'edge_index': edge_index, 'edge_attr': edge_attr, 'batch': batch, 'W_edge': W_edge, 'b_edge': b_edge, 'W_conv': W_conv, 'b_conv': b_conv, 'W_res': W_res, 'b_res': b_res}
    _L1_gnn_all = _L1_gnn_setup()
    _L1_gnn_in = {k: v for k, v in _L1_gnn_all.items() if k in ('W_edge', 'b_edge', 'W_conv', 'b_conv', 'W_res', 'b_res')}
    del _L1_gnn_all

    def _L1_ffn_setup():
        import jax, jax.numpy as jnp
        import numpy as np
        B, N, D = (16, 512, 256)
        NUM_EXPERTS, TOP_K, HEADS = (4, 2, 4)
        N_EDGES = 131072
        LN_EPS = 1e-05

        def _layernorm(x, g, b):
            mu = x.mean(-1, keepdims=True)
            var = ((x - mu) ** 2).mean(-1, keepdims=True)
            return (x - mu) * jax.lax.rsqrt(var + LN_EPS) * g + b

        def _forward(x, edge_index, W_gat, att_src, att_dst, b_gat, ln_gamma, ln_beta, W1, b1, W2, b2):
            Bc, Nc, Dc = x.shape
            M = Bc * Nc
            x_flat = x.reshape(M, Dc)
            h = (x_flat @ W_gat).reshape(M, HEADS, NUM_EXPERTS)
            loops = jnp.arange(M, dtype=edge_index.dtype)
            src = jnp.concatenate([edge_index[0], loops])
            dst = jnp.concatenate([edge_index[1], loops])
            a_src = (h * att_src).sum(-1)
            a_dst = (h * att_dst).sum(-1)
            e = jax.nn.leaky_relu(a_src[src] + a_dst[dst], negative_slope=0.2)
            e_max = jax.ops.segment_max(e, dst, num_segments=M)
            ee = jnp.exp(e - e_max[dst])
            denom = jax.ops.segment_sum(ee, dst, num_segments=M)
            alpha = ee / (denom[dst] + 1e-16)
            msg = h[src] * alpha[:, :, None]
            agg = jax.ops.segment_sum(msg, dst, num_segments=M).reshape(M, HEADS * NUM_EXPERTS) + b_gat
            scores = _layernorm(agg, ln_gamma, ln_beta).reshape(M, HEADS, NUM_EXPERTS).mean(1)
            scores = scores.reshape(Bc, Nc, NUM_EXPERTS)
            topk_s, topk_i = jax.lax.top_k(scores, TOP_K)
            w = jax.nn.softmax(topk_s, axis=-1)
            out = jnp.zeros_like(x)
            for ei in range(NUM_EXPERTS):
                g = jnp.where(topk_i == ei, w, 0.0).sum(-1)
                hh = jax.nn.gelu(x @ W1[ei] + b1[ei], approximate=False)
                out = out + g[..., None] * (hh @ W2[ei] + b2[ei])
            return out
        key = jax.random.key(seed)
        ks = jax.random.split(key, 8)
        s = 0.05
        return {'x': jax.random.normal(ks[0], (B, N, D), jnp.float32), 'W_gat': jax.random.normal(ks[1], (D, HEADS * NUM_EXPERTS), jnp.float32) * s, 'att_src': jax.random.normal(ks[2], (HEADS, NUM_EXPERTS), jnp.float32) * s, 'att_dst': jax.random.normal(ks[3], (HEADS, NUM_EXPERTS), jnp.float32) * s, 'b_gat': jnp.zeros((HEADS * NUM_EXPERTS,), jnp.float32), 'ln_gamma': jnp.ones((HEADS * NUM_EXPERTS,), jnp.float32), 'ln_beta': jnp.zeros((HEADS * NUM_EXPERTS,), jnp.float32), 'W1': jax.random.normal(ks[4], (NUM_EXPERTS, D, 2 * D), jnp.float32) * s, 'b1': jnp.zeros((NUM_EXPERTS, 2 * D), jnp.float32), 'W2': jax.random.normal(ks[5], (NUM_EXPERTS, 2 * D, D), jnp.float32) * s, 'b2': jnp.zeros((NUM_EXPERTS, D), jnp.float32), 'edge_index': jax.random.randint(ks[6], (2, N_EDGES), 0, B * N, jnp.int32)}
    _L1_ffn_all = _L1_ffn_setup()
    _L1_ffn_in = {k: v for k, v in _L1_ffn_all.items() if k in ('W_gat', 'att_src', 'att_dst', 'b_gat', 'ln_gamma', 'ln_beta', 'W1', 'b1', 'W2', 'b2', 'edge_index')}
    del _L1_ffn_all
    return {'x': x, 'src': src, 'dst': dst, 'edge_attr_64': edge_attr_64, 'L0_gnn_Wq': _L0_gnn_in['Wq'], 'L0_gnn_bq': _L0_gnn_in['bq'], 'L0_gnn_Wk': _L0_gnn_in['Wk'], 'L0_gnn_bk': _L0_gnn_in['bk'], 'L0_gnn_Wv': _L0_gnn_in['Wv'], 'L0_gnn_bv': _L0_gnn_in['bv'], 'L0_gnn_Wskip': _L0_gnn_in['Wskip'], 'L0_gnn_bskip': _L0_gnn_in['bskip'], 'L0_gnn_ln1_g': _L0_gnn_in['ln1_g'], 'L0_gnn_ln1_b': _L0_gnn_in['ln1_b'], 'L0_gnn_W1': _L0_gnn_in['W1'], 'L0_gnn_b1': _L0_gnn_in['b1'], 'L0_gnn_W2': _L0_gnn_in['W2'], 'L0_gnn_b2': _L0_gnn_in['b2'], 'L0_gnn_ln2_g': _L0_gnn_in['ln2_g'], 'L0_gnn_ln2_b': _L0_gnn_in['ln2_b'], 'L0_ffn_Wr': _L0_ffn_in['Wr'], 'L0_ffn_br': _L0_ffn_in['br'], 'L0_ffn_W1': _L0_ffn_in['W1'], 'L0_ffn_b1': _L0_ffn_in['b1'], 'L0_ffn_g1': _L0_ffn_in['g1'], 'L0_ffn_be1': _L0_ffn_in['be1'], 'L0_ffn_m1': _L0_ffn_in['m1'], 'L0_ffn_v1': _L0_ffn_in['v1'], 'L0_ffn_W2': _L0_ffn_in['W2'], 'L0_ffn_b2': _L0_ffn_in['b2'], 'L0_ffn_g2': _L0_ffn_in['g2'], 'L0_ffn_be2': _L0_ffn_in['be2'], 'L0_ffn_m2': _L0_ffn_in['m2'], 'L0_ffn_v2': _L0_ffn_in['v2'], 'L0_ffn_Wo': _L0_ffn_in['Wo'], 'L0_ffn_bo': _L0_ffn_in['bo'], 'L1_gnn_W_edge': _L1_gnn_in['W_edge'], 'L1_gnn_b_edge': _L1_gnn_in['b_edge'], 'L1_gnn_W_conv': _L1_gnn_in['W_conv'], 'L1_gnn_b_conv': _L1_gnn_in['b_conv'], 'L1_gnn_W_res': _L1_gnn_in['W_res'], 'L1_gnn_b_res': _L1_gnn_in['b_res'], 'L1_ffn_W_gat': _L1_ffn_in['W_gat'], 'L1_ffn_att_src': _L1_ffn_in['att_src'], 'L1_ffn_att_dst': _L1_ffn_in['att_dst'], 'L1_ffn_b_gat': _L1_ffn_in['b_gat'], 'L1_ffn_ln_gamma': _L1_ffn_in['ln_gamma'], 'L1_ffn_ln_beta': _L1_ffn_in['ln_beta'], 'L1_ffn_W1': _L1_ffn_in['W1'], 'L1_ffn_b1': _L1_ffn_in['b1'], 'L1_ffn_W2': _L1_ffn_in['W2'], 'L1_ffn_b2': _L1_ffn_in['b2'], 'L1_ffn_edge_index': _L1_ffn_in['edge_index']}

def reference(x, src, dst, edge_attr_64, L0_gnn_Wq, L0_gnn_bq, L0_gnn_Wk, L0_gnn_bk, L0_gnn_Wv, L0_gnn_bv, L0_gnn_Wskip, L0_gnn_bskip, L0_gnn_ln1_g, L0_gnn_ln1_b, L0_gnn_W1, L0_gnn_b1, L0_gnn_W2, L0_gnn_b2, L0_gnn_ln2_g, L0_gnn_ln2_b, L0_ffn_Wr, L0_ffn_br, L0_ffn_W1, L0_ffn_b1, L0_ffn_g1, L0_ffn_be1, L0_ffn_m1, L0_ffn_v1, L0_ffn_W2, L0_ffn_b2, L0_ffn_g2, L0_ffn_be2, L0_ffn_m2, L0_ffn_v2, L0_ffn_Wo, L0_ffn_bo, L1_gnn_W_edge, L1_gnn_b_edge, L1_gnn_W_conv, L1_gnn_b_conv, L1_gnn_W_res, L1_gnn_b_res, L1_ffn_W_gat, L1_ffn_att_src, L1_ffn_att_dst, L1_ffn_b_gat, L1_ffn_ln_gamma, L1_ffn_ln_beta, L1_ffn_W1, L1_ffn_b1, L1_ffn_W2, L1_ffn_b2, L1_ffn_edge_index):
    import jax
    import jax.numpy as jnp

    def _L0_gnn_ref(x, edge_index, Wq, bq, Wk, bk, Wv, bv, Wskip, bskip, ln1_g, ln1_b, W1, b1, W2, b2, ln2_g, ln2_b):
        import jax, jax.numpy as jnp
        import numpy as np
        N = 2500
        E = 40000
        HID = 256
        H = 4
        D = HID // H
        FF = 4 * HID

        def _layernorm(x, g, b, eps=1e-05):
            mu = jnp.mean(x, axis=-1, keepdims=True)
            var = jnp.var(x, axis=-1, keepdims=True)
            return (x - mu) * jax.lax.rsqrt(var + eps) * g + b

        def _transformer_conv(x, edge_index, Wq, bq, Wk, bk, Wv, bv, Wskip, bskip):
            src, dst = (edge_index[0], edge_index[1])
            n = x.shape[0]
            q = (x @ Wq + bq).reshape(n, H, D)
            k = (x @ Wk + bk).reshape(n, H, D)
            v = (x @ Wv + bv).reshape(n, H, D)
            qi = q[dst]
            kj = k[src]
            vj = v[src]
            alpha = jnp.sum(qi * kj, axis=-1) / jnp.sqrt(jnp.float32(D))
            m = jax.ops.segment_max(alpha, dst, num_segments=n)
            ex = jnp.exp(alpha - m[dst])
            denom = jax.ops.segment_sum(ex, dst, num_segments=n)
            a = ex / (denom[dst] + 1e-16)
            out = jax.ops.segment_sum(a[..., None] * vj, dst, num_segments=n)
            out = out.reshape(n, H * D)
            return out + x @ Wskip + bskip
        x_new = _transformer_conv(x, edge_index, Wq, bq, Wk, bk, Wv, bv, Wskip, bskip)
        h = _layernorm(x + x_new, ln1_g, ln1_b)
        ffn = jax.nn.gelu(h @ W1 + b1, approximate=False) @ W2 + b2
        return _layernorm(h + ffn, ln2_g, ln2_b)

    def _L0_ffn_ref(x, Wr, br, W1, b1, g1, be1, m1, v1, W2, b2, g2, be2, m2, v2, Wo, bo):
        import jax, jax.numpy as jnp
        import numpy as np
        BN_EPS = 0.001

        def _bn(h, g, b, m, v):
            return g * (h - m) * jax.lax.rsqrt(v + BN_EPS) + b
        feat = jnp.mean(x, axis=0)
        w = jax.nn.softmax(feat @ Wr + br, axis=-1)
        h = jnp.einsum('bfd,edh->bfeh', x, W1) + b1
        h = jax.nn.relu(_bn(h, g1, be1, m1, v1))
        h = jnp.einsum('bfeh,ehk->bfek', h, W2) + b2
        h = jax.nn.relu(_bn(h, g2, be2, m2, v2))
        y = jnp.einsum('bfeh,ehd->bfed', h, Wo) + bo
        return jnp.einsum('bfed,fe->bfd', y, w)

    def _L1_gnn_ref(x, edge_index, edge_attr, batch, W_edge, b_edge, W_conv, b_conv, W_res, b_res):
        import jax, jax.numpy as jnp
        import numpy as np
        N = 6250
        E = 200000
        IN_F = 256
        EDGE_F = 64
        HALF = IN_F // 2
        BASE = IN_F + HALF
        OUT_F = 256
        NEG_SLOPE = 0.01
        n = x.shape[0]
        src, dst = (edge_index[0], edge_index[1])
        per_node = jax.ops.segment_sum(edge_attr, src, num_segments=n)
        per_node = jax.nn.leaky_relu(per_node @ W_edge + b_edge, negative_slope=NEG_SLOPE)
        h = jnp.concatenate([x, per_node], axis=1)
        identity = h
        hw = h @ W_conv
        ones = jnp.ones((src.shape[0],), dtype=hw.dtype)
        deg = jax.ops.segment_sum(ones, dst, num_segments=n) + 1.0
        dinv = jax.lax.rsqrt(deg)
        norm = dinv[src] * dinv[dst]
        agg = jax.ops.segment_sum(norm[:, None] * hw[src], dst, num_segments=n)
        out = agg + (dinv * dinv)[:, None] * hw + b_conv
        out = out + identity @ W_res + b_res
        return jax.nn.relu(out)

    def _L1_ffn_ref(x, W_gat, att_src, att_dst, b_gat, ln_gamma, ln_beta, W1, b1, W2, b2, edge_index):
        import jax, jax.numpy as jnp
        import numpy as np
        B, N, D = (16, 512, 256)
        NUM_EXPERTS, TOP_K, HEADS = (4, 2, 4)
        N_EDGES = 131072
        LN_EPS = 1e-05

        def _layernorm(x, g, b):
            mu = x.mean(-1, keepdims=True)
            var = ((x - mu) ** 2).mean(-1, keepdims=True)
            return (x - mu) * jax.lax.rsqrt(var + LN_EPS) * g + b

        def _forward(x, edge_index, W_gat, att_src, att_dst, b_gat, ln_gamma, ln_beta, W1, b1, W2, b2):
            Bc, Nc, Dc = x.shape
            M = Bc * Nc
            x_flat = x.reshape(M, Dc)
            h = (x_flat @ W_gat).reshape(M, HEADS, NUM_EXPERTS)
            loops = jnp.arange(M, dtype=edge_index.dtype)
            src = jnp.concatenate([edge_index[0], loops])
            dst = jnp.concatenate([edge_index[1], loops])
            a_src = (h * att_src).sum(-1)
            a_dst = (h * att_dst).sum(-1)
            e = jax.nn.leaky_relu(a_src[src] + a_dst[dst], negative_slope=0.2)
            e_max = jax.ops.segment_max(e, dst, num_segments=M)
            ee = jnp.exp(e - e_max[dst])
            denom = jax.ops.segment_sum(ee, dst, num_segments=M)
            alpha = ee / (denom[dst] + 1e-16)
            msg = h[src] * alpha[:, :, None]
            agg = jax.ops.segment_sum(msg, dst, num_segments=M).reshape(M, HEADS * NUM_EXPERTS) + b_gat
            scores = _layernorm(agg, ln_gamma, ln_beta).reshape(M, HEADS, NUM_EXPERTS).mean(1)
            scores = scores.reshape(Bc, Nc, NUM_EXPERTS)
            topk_s, topk_i = jax.lax.top_k(scores, TOP_K)
            w = jax.nn.softmax(topk_s, axis=-1)
            out = jnp.zeros_like(x)
            for ei in range(NUM_EXPERTS):
                g = jnp.where(topk_i == ei, w, 0.0).sum(-1)
                hh = jax.nn.gelu(x @ W1[ei] + b1[ei], approximate=False)
                out = out + g[..., None] * (hh @ W2[ei] + b2[ei])
            return out
        return _forward(x, edge_index, W_gat, att_src, att_dst, b_gat, ln_gamma, ln_beta, W1, b1, W2, b2)
    edge_index = jnp.stack([src, dst])
    batch0 = jnp.zeros((6250,), jnp.int32)
    x = x + _L0_gnn_ref(_layernorm(x, axis=-1), edge_index, L0_gnn_Wq, L0_gnn_bq, L0_gnn_Wk, L0_gnn_bk, L0_gnn_Wv, L0_gnn_bv, L0_gnn_Wskip, L0_gnn_bskip, L0_gnn_ln1_g, L0_gnn_ln1_b, L0_gnn_W1, L0_gnn_b1, L0_gnn_W2, L0_gnn_b2, L0_gnn_ln2_g, L0_gnn_ln2_b)
    x = x + _L0_ffn_ref(_layernorm(x, axis=-1)[None], L0_ffn_Wr, L0_ffn_br, L0_ffn_W1, L0_ffn_b1, L0_ffn_g1, L0_ffn_be1, L0_ffn_m1, L0_ffn_v1, L0_ffn_W2, L0_ffn_b2, L0_ffn_g2, L0_ffn_be2, L0_ffn_m2, L0_ffn_v2, L0_ffn_Wo, L0_ffn_bo)[0]
    x = x + _L1_gnn_ref(_layernorm(x, axis=-1), edge_index, edge_attr_64, batch0, L1_gnn_W_edge, L1_gnn_b_edge, L1_gnn_W_conv, L1_gnn_b_conv, L1_gnn_W_res, L1_gnn_b_res)
    x = x + _L1_ffn_ref(_layernorm(x, axis=-1)[None], L1_ffn_W_gat, L1_ffn_att_src, L1_ffn_att_dst, L1_ffn_b_gat, L1_ffn_ln_gamma, L1_ffn_ln_beta, L1_ffn_W1, L1_ffn_b1, L1_ffn_W2, L1_ffn_b2, L1_ffn_edge_index)[0]
    return x

_drawn_inputs = setup_inputs


def setup_inputs(seed=0):
    import zlib

    import numpy as np

    out = dict(_drawn_inputs(seed))
    spreads = {'L0_gnn_bq': (0.0, 0.8),
     'L0_gnn_bk': (0.0, 0.8),
     'L0_gnn_bv': (0.0, 0.1),
     'L0_gnn_bskip': (0.0, 0.1),
     'L0_gnn_ln1_g': (1.0, 0.2),
     'L0_gnn_ln1_b': (0.0, 0.1),
     'L0_gnn_b1': (0.0, 0.336),
     'L0_gnn_b2': (0.0, 0.1),
     'L0_gnn_ln2_g': (1.0, 0.2),
     'L0_gnn_ln2_b': (0.0, 0.1),
     'L0_ffn_br': (0.0, 0.31),
     'L0_ffn_b1': (0.0, 0.496),
     'L0_ffn_g1': (1.0, 0.2),
     'L0_ffn_be1': (0.0, 0.529),
     'L0_ffn_m1': (0.0, 0.461),
     'L0_ffn_v1': (1.0, 0.6),
     'L0_ffn_b2': (0.0, 0.354),
     'L0_ffn_g2': (1.0, 0.2),
     'L0_ffn_be2': (0.0, 0.36),
     'L0_ffn_m2': (0.0, 0.376),
     'L0_ffn_v2': (1.0, 0.6),
     'L0_ffn_bo': (0.0, 0.1),
     'L1_gnn_b_edge': (0.0, 0.362),
     'L1_gnn_b_conv': (0.0, 0.1),
     'L1_gnn_b_res': (0.0, 0.1),
     'L1_ffn_b_gat': (0.0, 0.1),
     'L1_ffn_ln_gamma': (1.0, 0.2),
     'L1_ffn_ln_beta': (0.0, 0.273),
     'L1_ffn_b1': (0.0, 0.31),
     'L1_ffn_b2': (0.0, 0.1)}
    factors = {'L0_gnn_Wq': 8.0, 'L0_gnn_Wk': 8.0, 'L1_ffn_att_src': 2.889, 'L1_ffn_att_dst': 4.933}
    for name, (base, spread) in spreads.items():
        noise = np.random.default_rng([zlib.crc32(name.encode()), seed]).standard_normal(out[name].shape)
        drawn = base * np.exp(spread * noise) if base else spread * noise
        out[name] = jnp.asarray(drawn.astype(out[name].dtype))
    for name, factor in factors.items():
        out[name] = (out[name] * factor).astype(out[name].dtype)
    return out
```

```python
from contextlib import ExitStack

import concourse.bass as bass
from concourse import mybir

F32 = mybir.dt.float32
BF16 = mybir.dt.bfloat16
I32 = mybir.dt.int32
U16 = mybir.dt.uint16
ALU = mybir.AluOpType
ACT = mybir.ActivationFunctionType
AX = mybir.AxisListType
DVE = mybir.EngineType.DVE

P = 128
N = 6250
D = 256
NT = -(-N // P)
NP = NT * P
LAST = N - (NT - 1) * P
KC = D // P
NB = NT + 1
H = 4
DH = D // H
LN_EPS = 1e-5
PAD_LO = 999
UNROLL = 8


class Stream:

    def __init__(self, name, edges, parts, buckets, tiles):
        self.name = name
        self.edges = edges
        self.buckets = buckets
        self.parts = parts
        self.cols = edges // parts
        self.tiles = tiles
        self.stride = -(-(edges // P + buckets) // UNROLL) * UNROLL
        assert parts * self.cols == edges and tiles <= self.stride


E1 = 100000
E3 = 131072
BY_DST = Stream("dst", E1, 125, NT, 832)
BY_SRC = Stream("src", E1, 125, NT, 832)
GAT = Stream("gat", E3, 128, NB, 1072)
for s in (BY_DST, BY_SRC):
    assert s.tiles >= (s.edges + NT * (P - 1)) // P
assert GAT.tiles >= (E3 + NT * (P - 1)) // P


class Alloc:

    def __init__(self, nc, ctx, stage):
        self.nc, self.ctx, self.stage = nc, ctx, stage
        self.own = []
        ctx.callback(self.give_back)

    def give_back(self):
        if self.own:
            self.nc.clear_and_free_semaphores(self.own)
            self.nc.all_engine_barrier()

    def sb(self, name, shape, dt=F32):
        return self.ctx.enter_context(self.nc.sbuf_tensor(f"{self.stage}_{name}", shape, dt))

    def ps(self, name, shape, dt=F32):
        return self.ctx.enter_context(self.nc.psum_tensor(f"{self.stage}_{name}", shape, dt))

    def sem(self, name):
        self.own.append(self.nc.alloc_semaphore(f"{self.stage}_{name}"))
        return self.own[-1]

    def sems(self, name, n):
        return [self.sem(f"{name}{i}") for i in range(n)]


def wait(eng, sem, value):
    if not isinstance(value, int) or value > 0:
        eng.wait_ge(sem, value)


def wait_alone(eng, sem, value, passed):
    wait(eng, sem, value)
    if not isinstance(value, int):
        eng.sem_inc(passed, 1)


def pipelined(eng, tiles, unroll, stages, top=None, peel=1):
    assert tiles % unroll == 0
    last = max(lag for lag, _ in stages)
    rounds = tiles // unroll
    assert last <= unroll * peel and peel <= rounds

    def steps(i, u):
        for lag, stage in stages:
            if not isinstance(i, int):
                back = -((u - lag) // unroll)
                stage(i * unroll + (u - lag), (u - lag) % unroll, i - back if back else i)
            elif 0 <= i * unroll + u - lag < tiles:
                t = i * unroll + u - lag
                stage(t, t % unroll, t // unroll)
    for i in range(peel):
        if top:
            top(i)
        for u in range(unroll):
            steps(i, u)
    if rounds > peel:
        with eng.Fori(peel, rounds) as i:
            if top:
                top(i)
            for u in range(unroll):
                steps(i, u)
    for k in range(last):
        if k % unroll == 0 and top:
            top(rounds + k // unroll)
        steps(rounds + k // unroll, k % unroll)


def cols(ap, start, n=1):
    return ap[:, bass.ds(start, n)]

def constants(nc, keep):
    c = {}
    c["ident"] = keep.sb("ident", [P, P])
    c["ident_bf"] = keep.sb("ident_bf", [P, P], BF16)
    c["drop4"] = keep.sb("drop4", [P, H * P], BF16)
    c["ones"] = keep.sb("ones", [P, P])
    c["ones_bf"] = keep.sb("ones_bf", [P, P], BF16)
    c["before"] = keep.sb("before", [P, P])
    c["upto"] = keep.sb("upto", [P, P])
    c["iota"] = keep.sb("iota", [P, P])
    c["iota_bf"] = keep.sb("iota_bf", [P, P], BF16)
    with ExitStack() as ctx:
        a = Alloc(nc, ctx, "const")
        filled, made = a.sem("filled"), a.sem("made")
        block = ctx.enter_context(nc.Block())

        @block.gpsimd
        def _(pool):
            for name, value in (("ident", 0.0), ("ident_bf", 0.0), ("drop4", 0.0), ("ones", 1.0), ("ones_bf", 1.0),
                                ("before", 1.0), ("upto", 1.0)):
                nc.gpsimd.memset(c[name][:], value).then_inc(filled, 1)
            pool.wait_ge(filled, 7)
            for name, copies, fill in (("ident", 1, 1.0), ("ident_bf", 1, 1.0), ("drop4", H, -1e30)):
                m = c[name][:].rearrange("p (h n) -> p h n", h=copies)
                nc.gpsimd.affine_select(m, m, [[0, copies], [-1, P]], ALU.not_equal, fill, base=0,
                                        channel_multiplier=1).then_inc(made, 1)
            for name, compare in (("before", ALU.is_gt), ("upto", ALU.is_ge)):
                nc.gpsimd.affine_select(c[name][:], c[name][:], [[1, P]], compare, 0.0, base=0,
                                        channel_multiplier=-1).then_inc(made, 1)
            for name in ("iota", "iota_bf"):
                nc.gpsimd.iota(c[name][:], pattern=[[1, P]], base=0, channel_multiplier=0,
                               allow_small_or_imprecise_dtypes=True).then_inc(made, 1)
            pool.wait_ge(made, 7)
    return c


def place_edges(nc, c, st, key_dram, hi_row, slot_row, lo, src_dram=None, payload=None, fill=()):
    R, C, T = st.parts, st.cols, st.tiles
    with ExitStack() as ctx:
        a = Alloc(nc, ctx, f"place_{st.name}")
        key = a.sb("key", [R, C], I32)
        src = a.sb("src_in", [R, C], I32)
        hi = a.sb("hi", [R, C], BF16)
        hi_i = a.sb("hi_i", [R, C], I32)
        lo_i = a.sb("lo_i", [R, C], I32)
        ones = a.sb("row_ones", [R, C], BF16)
        mask = a.sb("mask", [R, C], U16)
        rank = a.sb("rank", [R, C])
        pos = a.sb("pos", [R, C])
        cnt = a.sb("cnt", [P, NB])
        tot = a.sb("tot", [P, NB])
        tot_i = a.sb("tot_i", [P, NB], I32)
        n_tiles = a.sb("n_tiles", [P, NB])
        end = a.sb("end", [P, NB])
        first = a.sb("first", [P, NB])
        start = a.sb("start", [P, NB])
        ctot = a.sb("ctot", [NB, 2])
        ctot_i = a.sb("ctot_i", [NB, 2], I32)
        ctiles = a.sb("ctiles", [NB, 2])
        cend = a.sb("cend", [NB, 2])
        tile_no = a.sb("tile_no", [NB, T])
        ended = a.sb("ended", [NB, T])
        p_off = a.ps("p_off", [P, 512])
        p_tot = a.ps("p_tot", [P, 512])
        p_col = a.ps("p_col", [P, 512])
        p_end = a.ps("p_end", [P, 512])
        HC = -(-T // 512)
        p_hi = [a.ps(f"p_hi{k}", [P, 512]) for k in range(HC)]
        loaded, filled = a.sem("loaded"), a.sem("filled")
        numbered, counted, tiled = a.sem("numbered"), a.sem("counted"), a.sem("tiled")
        summed, ends, listed, marked = a.sem("summed"), a.sem("ends"), a.sem("listed"), a.sem("marked")
        v_done, loops, passed = a.sem("v_done"), a.sem("loops"), a.sem("passed")
        block = ctx.enter_context(nc.Block())

        @block.sync
        def _(sp):
            sp.dma_start(key[:], key_dram.rearrange("(p c) -> p c", p=R)).then_inc(loaded, 16)
            if src_dram is not None:
                sp.dma_start(src[:], src_dram.rearrange("(p c) -> p c", p=R)).then_inc(loaded, 16)
            for to, from_ in fill:
                sp.dma_start(to, from_).then_inc(filled, 16)
            if fill:
                sp.wait_ge(filled, 16 * len(fill))

        @block.gpsimd
        def _(pool):
            nc.gpsimd.iota(tile_no[:], pattern=[[1, T]], base=0, channel_multiplier=0,
                           allow_small_or_imprecise_dtypes=True).then_inc(numbered, 1)

        @block.tensor
        def _(pe):
            pe.wait_ge(counted, 1)
            nc.tensor.matmul(p_off[:, 0:NB], c["before"][:], cnt[:], start=True, stop=True)
            nc.tensor.matmul(p_tot[:, 0:NB], c["ones"][:], cnt[:], start=True, stop=True)
            nc.tensor.matmul(p_col[0:NB, 0:2], cnt[:], c["ones"][:, 0:2], start=True, stop=True).then_inc(summed, 1)
            pe.wait_ge(tiled, 1)
            nc.tensor.matmul(p_end[0:NB, 0:2], c["upto"][0:NB, 0:NB], ctiles[:], start=True, stop=True).then_inc(ends, 1)
            pe.wait_ge(marked, 1)
            for k in range(HC):
                n = min(512, T - 512 * k)
                last = nc.tensor.matmul(p_hi[k][0:1, 0:n], c["ones"][0:NB, 0:1], ended[:, 512 * k:512 * k + n],
                                        start=True, stop=True)
            last.then_inc(listed, 1)

        @block.vector
        def _(v):
            done = [0]

            def step(ins):
                done[0] += 1
                ins.then_inc(v_done, 1)
                v.wait_ge(v_done, done[0])

            step(nc.vector.memset(cnt[:], 0.0))
            step(nc.vector.memset(ones[:], 1.0))
            step(nc.vector.memset(pos[:], 0.0))
            step(nc.vector.memset(hi_row[:], 0))
            v.wait_ge(loaded, 16 if src_dram is None else 32)
            step(nc.vector.tensor_scalar(hi_i[:], key[:], 7, None, ALU.arith_shift_right))
            step(nc.vector.tensor_scalar(lo_i[:], key[:], P - 1, None, ALU.bitwise_and))
            step(nc.vector.tensor_scalar(hi[:], hi_i[:], float(NT), None, ALU.min))
            if payload is None:
                step(nc.vector.tensor_copy(lo[:], lo_i[:]))
            else:
                step(nc.vector.tensor_scalar(payload[:, :, 0], src[:], float(N - 1), None, ALU.min))
                step(nc.vector.tensor_copy(payload[:, :, 1], lo_i[:]))
            base = done[0]
            with v.Fori(0, NB) as b:
                nc.vector.tensor_scalar(mask[:], hi[:], cols(c["iota"][0:R, :], b), 0.0, ALU.is_equal, ALU.add,
                                        accum_out=cols(cnt[0:R, :], b)).then_inc(loops, 1)
                v.wait_ge(loops, b + 1)
            nc.vector.memset(ctot[:], 0.0).then_inc(counted, 1)
            v.wait_ge(summed, 1)
            step(nc.vector.tensor_copy(ctot[:], p_col[0:NB, 0:2]))
            step(nc.vector.tensor_scalar(ctot_i[:], ctot[:], float(P - 1), None, ALU.add))
            step(nc.vector.tensor_scalar(ctot_i[:], ctot_i[:], 7, None, ALU.arith_shift_right))
            nc.vector.tensor_copy(ctiles[:], ctot_i[:]).then_inc(tiled, 1)
            step(nc.vector.tensor_scalar(tot_i[:], p_tot[:, 0:NB], float(P - 1), None, ALU.add))
            step(nc.vector.tensor_scalar(tot_i[:], tot_i[:], 7, None, ALU.arith_shift_right))
            step(nc.vector.tensor_copy(n_tiles[:], tot_i[:]))
            step(nc.vector.tensor_tensor_scan(end[:], c["ones"][:, 0:NB], n_tiles[:], 0.0, ALU.mult, ALU.add))
            step(nc.vector.tensor_tensor(first[:], end[:], n_tiles[:], ALU.subtract))
            step(nc.vector.scalar_tensor_tensor(start[:], first[:], float(P), p_off[:, 0:NB], ALU.mult, ALU.add))
            step(nc.vector.tensor_scalar(start[:], start[:], -1.0, None, ALU.add))
            v.wait_ge(ends, 1)
            v.wait_ge(numbered, 1)
            step(nc.vector.tensor_copy(cend[:], p_end[0:NB, 0:2]))
            nc.vector.tensor_scalar(ended[:], tile_no[:], cend[:, 0:1], None, ALU.is_ge).then_inc(marked, 1)
            v.wait_ge(listed, 1)
            for k in range(HC):
                n = min(512, T - 512 * k)
                nc.vector.tensor_scalar(hi_row[0:1, UNROLL + 512 * k:UNROLL + 512 * k + n], p_hi[k][0:1, 0:n],
                                        float(st.buckets - 1), None, ALU.min)
            with v.Fori(0, NB) as b:
                nc.vector.tensor_scalar(mask[:], hi[:], cols(c["iota"][0:R, :], b), None,
                                        ALU.is_equal).then_inc(loops, 1)
                v.wait_ge(loops, b * 3 + (NB + 1))
                nc.vector.tensor_tensor_scan(rank[:], ones[:], mask[:], cols(start[0:R, :], b), ALU.mult,
                                             ALU.add).then_inc(loops, 1)
                wait_alone(v, loops, b * 3 + (NB + 2), passed)
                nc.vector.copy_predicated(pos[:], mask[:], rank[:]).then_inc(loops, 1)
                v.wait_ge(loops, b * 3 + (NB + 3))
            step(nc.vector.tensor_copy(hi_i[:], pos[:]))
            step(nc.vector.tensor_scalar(lo_i[:], hi_i[:], P - 1, None, ALU.bitwise_and))
            step(nc.vector.tensor_scalar(hi_i[:], hi_i[:], 7, None, ALU.arith_shift_right))
            step(nc.vector.scalar_tensor_tensor(slot_row[:], lo_i[:], float(st.stride), hi_i[:], ALU.mult, ALU.add))


SCATTER = 16


class Scatter:

    def __init__(self, a, st, slot_row, out, width, dt):
        self.st, self.slot_row, self.out, self.width = st, slot_row, out, width
        self.rows = a.sb(f"{st.name}_rows", [st.parts, 2, SCATTER], I32)
        self.data = a.sb(f"{st.name}_data", [st.parts, 2, SCATTER * width], dt)
        self.copied = a.sem(f"{st.name}_copied")
        self.loaded = a.sems(f"{st.name}_loaded", 2)
        self.landed = a.sems(f"{st.name}_landed", 2)
        self.passed = a.sem(f"{st.name}_passed")
        self.chunks = st.cols // SCATTER

    def on_gpsimd(self, nc, pool, column, source, loads):
        def chunk(t, u, r):
            wait(pool, self.landed[u], r * (16 * SCATTER))
            nc.gpsimd.tensor_copy(self.rows[:, u, :], cols(self.slot_row, t * SCATTER, SCATTER)).then_inc(self.copied, 1)
            data = self.data[:, u, :].rearrange("p (c w) -> p c w", w=self.width)
            if column:
                to = self.data[:, u, column::self.width]
            else:
                to = data
            nc.gpsimd.tensor_copy(to, cols(source, t * SCATTER, SCATTER)).then_inc(self.copied, 1)
            wait_alone(pool, self.copied, t * 2 + 2, self.passed)
            if loads:
                wait_alone(pool, self.loaded[u], r * 16 + 16, self.passed)
            for c in range(SCATTER):
                nc.gpsimd.indirect_dma_start(self.out, bass.IndirectOffsetOnAxis(self.rows[:, u, c:c + 1], 0),
                                             data[:, c, :], None).then_inc(self.landed[u], 16)
        pipelined(pool, self.chunks, 2, [(0, chunk)])

    def drain(self, eng):
        for u in range(2):
            eng.wait_ge(self.landed[u], self.chunks // 2 * 16 * SCATTER)

GROUP = 7
GROUPS = NT // GROUP
GW = GROUP * P
HALF = GW // 2
assert GROUPS * GROUP == NT and HALF <= 512
VW = DH + 1
KVW = D + H * VW


class Normed:

    def __init__(self, a, gamma=None, beta=None, turned=True):
        self.gamma, self.beta = gamma, beta
        self.steps = GROUP * (1 if gamma is None else 3)
        self.stats = a.sb("stats", [P, GROUP, 6])
        self.mv = a.sb("mv", [P, GROUP, 2])
        self.var = a.sb("var", [P, GROUP])
        self.inv = a.sb("inv", [P, GROUP])
        self.rstd = a.sb("rstd", [P, GROUP])
        self.xn = a.sb("xn", [P, GROUP, D])
        if turned:
            self.xnT = a.sb("xnT", [P, KC, GW])
            self.banks = [a.ps(f"turn{b}", [P, 512]) for b in range(2)]
        self.passed = a.sem("passed")
        names = ("counted", "averaged", "added", "inverted", "rooted", "normed", "turned", "copied")
        (self.counted, self.averaged, self.added, self.inverted, self.rooted, self.normed, self.turned,
         self.copied) = (a.sem(n) for n in names)

    BATCHES = [(c, k0, min(4, GROUP - k0)) for c in range(KC) for k0 in range(0, GROUP, 4)]

    def on_vector(self, nc, v, g, x):
        for k in range(GROUP):
            nc.vector.bn_stats(self.stats[:, k, :], x(k)).then_inc(self.counted, 1)
        wait_alone(v, self.counted, g * GROUP + GROUP, self.passed)
        for k in range(GROUP):
            nc.vector.bn_aggr(self.mv[:, k, :], self.stats[:, k, :]).then_inc(self.averaged, 1)
        v.wait_ge(self.averaged, g * GROUP + GROUP)
        nc.vector.tensor_scalar(self.var[:], self.mv[:, :, 1], LN_EPS, None, ALU.add).then_inc(self.added, 1)
        v.wait_ge(self.added, g + 1)
        nc.vector.reciprocal(self.inv[:], self.var[:]).then_inc(self.inverted, 1)
        v.wait_ge(self.rooted, g + 1)
        for k in range(GROUP):
            nc.vector.tensor_scalar(self.xn[:, k, :], x(k), self.mv[:, k, 0:1], self.rstd[:, k:k + 1],
                                    ALU.subtract, ALU.mult).then_inc(self.normed, 1)
        if self.gamma is not None:
            for i, (row, op) in enumerate(((self.gamma, ALU.mult), (self.beta, ALU.add))):
                for k in range(GROUP):
                    v.wait_ge(self.normed, g * self.steps + (i * GROUP + k + 1))
                    nc.vector.tensor_tensor(self.xn[:, k, :], self.xn[:, k, :], row[:], op).then_inc(self.normed, 1)

    def on_scalar(self, nc, act, g):
        act.wait_ge(self.inverted, g + 1)
        nc.scalar.activation(self.rstd[:], self.inv[:], ACT.Sqrt).then_inc(self.rooted, 1)

    def turn(self, nc, pe, g, ident):
        pe.wait_ge(self.normed, g * self.steps + self.steps)
        for b, (c, k0, n) in enumerate(self.BATCHES):
            wait(pe, self.copied, g * len(self.BATCHES) + (b - 1))
            for k in range(n):
                last = nc.tensor.transpose(self.banks[b % 2][:, k * P:k * P + P],
                                           self.xn[:, k0 + k, c * P:c * P + P], ident[:])
            last.then_inc(self.turned, 1)

    def copy(self, nc, act, g):
        for b, (c, k0, n) in enumerate(self.BATCHES):
            act.wait_ge(self.turned, g * len(self.BATCHES) + b + 1)
            nc.scalar.activation(self.xnT[:, c, k0 * P:(k0 + n) * P], self.banks[b % 2][:, 0:n * P],
                                 ACT.Copy).then_inc(self.copied, 1)


def groups(eng, stages):
    pipelined(eng, GROUPS, 1, stages)


def tiled(rows):
    return rows.rearrange("(t p) w -> p t w", p=P)


def tile_of(x, t):
    return x[:, bass.ds(t, 1), :].rearrange("p a d -> p (a d)")


def chunked(w):
    return w.rearrange("(c p) n -> p c n", p=P)


def load_x(nc, x, x_dram):
    with ExitStack() as ctx:
        a = Alloc(nc, ctx, "load")
        cleared, loaded = a.sem("cleared"), a.sem("loaded")
        block = ctx.enter_context(nc.Block())

        @block.vector
        def _(v):
            nc.vector.memset(x[:, NT - 1, :], 0.0).then_inc(cleared, 1)

        @block.sync
        def _(sp):
            full = (NT - 1) * P
            sp.dma_start(x[:, 0:NT - 1, :], x_dram[0:full, :].rearrange("(t p) d -> p t d", p=P)).then_inc(loaded, 16)
            sp.wait_ge(cleared, 1)
            sp.dma_start(x[0:LAST, NT - 1, :], x_dram[full:N, :]).then_inc(loaded, 16)
            sp.wait_ge(loaded, 32)


def project(nc, c, x, w, qT, skip_dram, kv_dram, scatter, scatter_source):
    with ExitStack() as ctx:
        a = Alloc(nc, ctx, "project")
        norm = Normed(Alloc(nc, ctx, f"{a.stage}_n"))
        wq, wk, wv, ws = (a.sb(n, [P, KC, D]) for n in ("wq", "wk", "wv", "ws"))
        bq = a.sb("bq", [P, KC])
        bk, bv, bs = (a.sb(n, [P, D]) for n in ("bk", "bv", "bs"))
        kv = a.sb("kv", [P, GROUP, KVW])
        plus = a.sb("plus", [P, 2, D])
        skip = a.sb("skip", [P, GROUP, D])
        p_q = [a.ps(f"q{i}", [P, 512]) for i in range(2)]
        p_kv = [a.ps(f"kv{i}", [P, 512]) for i in range(2)]
        p_s = [a.ps(f"s{i}", [P, 512]) for i in range(2)]
        loaded, ones = a.sem("loaded"), a.sem("ones")
        q_made, q_read = a.sem("q_made"), a.sem("q_read")
        kvs_made, kv_read, s_read, stored = a.sem("kvs_made"), a.sem("kv_read"), a.sem("s_read"), a.sem("stored")
        loads = [(wq, chunked(w["Wq"])), (wk, chunked(w["Wk"])), (wv, chunked(w["Wv"])), (ws, chunked(w["Wskip"])),
                 (bq, w["bq"].rearrange("(c p) -> p c", p=P)), (bk, w["bk"].partition_broadcast(P)),
                 (bv, w["bv"].partition_broadcast(P)), (bs, w["bskip"].partition_broadcast(P))]
        block = ctx.enter_context(nc.Block())

        @block.sync
        def _(sp):
            for to, from_ in loads:
                sp.dma_start(to[:], from_, allow_slow_non_contiguous=True).then_inc(loaded, 16)

            def store(g, u, r):
                sp.wait_ge(kv_read, g * 3 * GROUP + 3 * GROUP)
                sp.dma_start(tiled(kv_dram)[:, bass.ds(g * GROUP, GROUP), :],
                             kv[:]).then_inc(stored, 16)
                sp.wait_ge(s_read, g * GROUP + GROUP)
                sp.dma_start(tiled(skip_dram)[:, bass.ds(g * GROUP, GROUP), :], skip[:]).then_inc(stored, 16)
            groups(sp, [(0, store)])
            sp.wait_ge(stored, 32 * GROUPS)

        @block.gpsimd
        def _(pool):
            nc.gpsimd.memset(kv[:], 1.0).then_inc(ones, 1)
            scatter.on_gpsimd(nc, pool, 0, scatter_source, False)
            scatter.drain(pool)

        @block.tensor
        def _(pe):
            pe.wait_ge(loaded, 16 * len(loads))

            def group(g, u, r):
                norm.turn(nc, pe, g, c["ident"])
                pe.wait_ge(norm.copied, g * len(norm.BATCHES) + len(norm.BATCHES))
                for m in range(KC):
                    for h in range(2):
                        i = 2 * m + h
                        wait(pe, q_read, g * 4 + (i - 1))
                        for k in range(KC):
                            mm = nc.tensor.matmul(p_q[i % 2][:, 0:HALF], wq[:, k, m * P:m * P + P],
                                                  norm.xnT[:, k, h * HALF:(h + 1) * HALF],
                                                  start=(k == 0), stop=(k == KC - 1))
                        mm.then_inc(q_made, 1)
                for t in range(GROUP):
                    wait(pe, s_read, (g * GROUP + (t - 1)))
                    for out, ww in ((p_kv[t % 2][:, 0:D], wk), (p_kv[t % 2][:, D:2 * D], wv), (p_s[t % 2][:, 0:D], ws)):
                        for k in range(KC):
                            mm = nc.tensor.matmul(out, norm.xnT[:, k, t * P:t * P + P], ww[:, k, :],
                                                  start=(k == 0), stop=(k == KC - 1))
                    mm.then_inc(kvs_made, 1)
            groups(pe, [(0, group)])

        @block.scalar
        def _(act):
            act.wait_ge(loaded, 16 * len(loads))

            def group(g, u, r):
                norm.on_scalar(nc, act, g)
                norm.copy(nc, act, g)
                for m in range(KC):
                    for h in range(2):
                        i = 2 * m + h
                        act.wait_ge(q_made, g * 4 + i + 1)
                        nc.scalar.activation(qT[:, m, bass.ds(g * GW + h * HALF, HALF)], p_q[i % 2][:, 0:HALF],
                                             ACT.Identity, bias=bq[:, m:m + 1]).then_inc(q_read, 1)
            groups(act, [(0, group)])

        @block.vector
        def _(v):
            v.wait_ge(loaded, 16 * len(loads))
            v.wait_ge(ones, 1)

            def group(g, u, r):
                norm.on_vector(nc, v, g, lambda k: tile_of(x, g * GROUP + k))
                wait(v, stored, g * 32)
                for t in range(GROUP):
                    v.wait_ge(kvs_made, g * GROUP + t + 1)
                    nc.vector.tensor_tensor(kv[:, t, 0:D], p_kv[t % 2][:, 0:D], bk[:], ALU.add).then_inc(kv_read, 1)
                    values = kv[:, t, D:].rearrange("p (h w) -> p h w", w=VW)[:, :, 0:DH]
                    nc.vector.tensor_tensor(values, p_kv[t % 2][:, D:2 * D].rearrange("p (h w) -> p h w", w=DH),
                                            bv[:].rearrange("p (h w) -> p h w", w=DH), ALU.add).then_inc(kv_read, 1)
                    nc.vector.tensor_tensor(plus[:, t % 2, :], p_s[t % 2][:, 0:D], norm.xn[:, t, :],
                                            ALU.add).then_inc(kv_read, 1)
                    v.wait_ge(kv_read, (g * GROUP + t) * 3 + 3)
                    nc.vector.tensor_tensor(skip[:, t, :], plus[:, t % 2, :], bs[:], ALU.add).then_inc(s_read, 1)
                v.wait_ge(s_read, g * GROUP + GROUP)
            groups(v, [(0, group)])

def load_edges(nc, st, rows_dram, source, lo, clear=()):
    with ExitStack() as ctx:
        a = Alloc(nc, ctx, f"load_{st.name}")
        both = a.sb("both", [P, st.tiles, 2], I32)
        loaded = a.sem("loaded")
        block = ctx.enter_context(nc.Block())

        @block.sync
        def _(sp):
            sp.dma_start(both[:], rows_dram.rearrange("(p t) w -> p t w", p=P)[:, 0:st.tiles, :]).then_inc(loaded, 16)

        @block.gpsimd
        def _(pool):
            for tile, value in clear:
                nc.gpsimd.memset(tile[:], value)

        @block.vector
        def _(v):
            v.wait_ge(loaded, 16)
            nc.vector.tensor_copy(source[:], both[:, :, 0])
            nc.vector.tensor_copy(lo[:], both[:, :, 1])


RING = UNROLL


def gather_loop(nc, pool, tiles, source, index, staged, passed, rows_dram, ring, gathered, freed):
    def gather(t, u, r):
        if u % UNROLL == 0:
            wait(pool, freed, t - UNROLL)
            nc.gpsimd.tensor_copy(index[:, u // UNROLL, :], cols(source, t, UNROLL)).then_inc(staged, 1)
            wait_alone(pool, staged, r * 2 + (u // UNROLL + 1), passed)
            if isinstance(t, int):
                pool.sem_inc(passed, 1)
        wait_alone(pool, freed, t - (RING - 1), passed)
        pool.indirect_dma_start(ring[:, u % RING, :], None, rows_dram,
                                bass.IndirectOffsetOnAxis(index[:, u // UNROLL, u % UNROLL:u % UNROLL + 1], 0)
                                ).then_inc(gathered[u % RING], 16)
    pipelined(pool, tiles, 2 * UNROLL, [(0, gather)])


def node_tiles(nc, st, hi_row, i, behind, engine=DVE):
    start = i * UNROLL + (UNROLL - behind)
    _, values = nc.values_load_multi_w_load_instructions(
        hi_row[0:1, bass.ds(start, UNROLL + behind)], (engine,), min_val=0, max_val=st.buckets - 1,
        skip_runtime_bounds_check_because="the row is clamped to the last bucket")
    return values


def attend(nc, c, source, lo, hi_row, qT, kv_dram, acc, top_score, no_edges, acc_dram):
    with ExitStack() as ctx:
        a = Alloc(nc, ctx, "attend")
        index = a.sb("index", [P, 2, UNROLL], I32)
        kv = a.sb("kv", [P, RING, KVW])
        kT = a.sb("kT", [P, 2, H, P])
        qs = a.sb("qs", [P, 2, KC, P])
        other = a.sb("other", [P, 4, P], BF16)
        tmax = a.sb("tmax", [P, H])
        new_top = a.sb("new_top", [P, H])
        minus = a.sb("minus", [P, 2, H])
        drop = a.sb("drop", [P, 2, H])
        shrink = a.sb("shrink", [P, 4, H])
        prob = a.sb("prob", [P, 2, H, P])
        probT = a.sb("probT", [P, 2, H, P])
        p_k = [a.ps(f"k{i}", [P, 512]) for i in range(2)]
        p_s = [a.ps(f"s{i}", [P, 512]) for i in range(2)]
        p_t = [a.ps(f"t{i}", [P, 512]) for i in range(2)]
        p_v = [a.ps(f"v{i}", [P, 512]) for i in range(2)]
        gathered = a.sems("gathered", RING)
        staged, passed = a.sem("staged"), a.sem("passed")
        k_turned, k_copied, prepared, scored = a.sem("k_turned"), a.sem("k_copied"), a.sem("prepared"), a.sem("scored")
        reduced, raised, lowered, kept = a.sem("reduced"), a.sem("raised"), a.sem("lowered"), a.sem("kept")
        exped, shrunk, p_turned, p_copied = a.sem("exped"), a.sem("shrunk"), a.sem("p_turned"), a.sem("p_copied")
        valued, summed, zeroed = a.sem("valued"), a.sem("summed"), a.sem("zeroed")
        stored = a.sem("stored")
        block = ctx.enter_context(nc.Block())
        T = BY_DST.tiles
        TURN, SCORE, PTURN, VALUE = 0, 1, 2, 3

        @block.sync
        def _(sp):
            sp.wait_ge(summed, T * 5)
            sp.dma_start(acc_dram, acc[:, 0:NT, :]).then_inc(stored, 16)
            sp.wait_ge(stored, 16)

        @block.gpsimd
        def _(pool):
            nc.gpsimd.memset(kT[:], 0.0).then_inc(zeroed, 1)
            gather_loop(nc, pool, T, source, index, staged, passed, kv_dram, kv, gathered, valued)

        @block.tensor
        def _(pe):
            def turn_keys(t, u, r):
                pe.wait_ge(gathered[u], r * 16 + 16)
                wait(pe, k_copied, t * 2 - 2)
                for k in range(KC):
                    mm = nc.tensor.transpose(p_k[u % 2][:, k * P:k * P + P], kv[:, u, k * P:k * P + P], c["ident"][:])
                mm.then_inc(k_turned, 1)

            def score(t, u, r):
                pe.wait_ge(prepared, t * 2 + 2)
                pe.wait_ge(k_copied, t * 2 + 2)
                wait(pe, exped, t - 1)
                s = p_s[u % 2]
                nc.tensor.matmul(s[:, :], other[:, u % 4, :], c["drop4"][:], start=True, stop=False,
                                 skip_group_check=True)
                for h in range(H):
                    mm = nc.tensor.matmul(s[:, h * P:h * P + P], qs[:, u % 2, h * DH // P, :], kT[:, u % 2, h, :],
                                          start=False, stop=True, skip_group_check=True)
                mm.then_inc(scored, 1)

            def turn_probs(t, u, r):
                pe.wait_ge(exped, t + 1)
                wait(pe, p_copied, t - 1)
                for h in range(H):
                    mm = nc.tensor.transpose(p_t[u % 2][:, h * P:h * P + P], prob[:, u % 2, h, :], c["ident"][:])
                mm.then_inc(p_turned, 1)

            def value(t, u, r):
                pe.wait_ge(p_copied, t + 1)
                wait(pe, summed, t * 5 - 5)
                for h in range(H):
                    nc.tensor.matmul(p_v[u % 2][:, h * VW:h * VW + VW], probT[:, u % 2, h, :],
                                     kv[:, u, D + h * VW:D + h * VW + VW], start=True, stop=True)
                nc.tensor.matmul(p_v[u % 2][:, H * VW:H * VW + 2], other[:, u % 4, :], c["ones_bf"][:, 0:2],
                                 start=True, stop=True).then_inc(valued, 1)
            pipelined(pe, T, UNROLL, [(TURN, turn_keys), (SCORE, score), (PTURN, turn_probs), (VALUE, value)])

        @block.scalar
        def _(act):
            act.wait_ge(zeroed, 1)

            def copy_keys(t, u, r):
                act.wait_ge(k_turned, t + 1)
                wait(act, scored, t - 1)
                for half in range(P // DH):
                    rows = slice(half * DH, half * DH + DH)
                    nc.scalar.activation(kT[rows, u % 2, half::P // DH, :],
                                         p_k[u % 2][rows, 0:D].rearrange("p (c e) -> p c e", e=P),
                                         ACT.Copy).then_inc(k_copied, 1)

            def exponentials(t, u, r):
                act.wait_ge(lowered, t * 2 + 2)
                wait(act, p_turned, t - 1)
                for h in range(H):
                    e = nc.scalar.activation(prob[:, u % 2, h, :], p_s[u % 2][:, h * P:h * P + P], ACT.Exp,
                                             bias=minus[:, u % 2, h:h + 1], scale=DH ** -0.5)
                e.then_inc(exped, 1)
                wait(act, summed, t * 5 - 15)
                nc.scalar.activation(shrink[:, u % 4, :], drop[:, u % 2, :], ACT.Exp, scale=DH ** -0.5).then_inc(shrunk, 1)

            def copy_probs(t, u, r):
                act.wait_ge(p_turned, t + 1)
                wait(act, valued, t - 1)
                nc.scalar.activation(probT[:, u % 2, :, :].rearrange("p h n -> p (h n)"), p_t[u % 2][:, :],
                                     ACT.Copy).then_inc(p_copied, 1)
            pipelined(act, T, UNROLL, [(TURN, copy_keys), (SCORE, exponentials), (PTURN, copy_probs)])

        @block.vector
        def _(v):
            tile_regs = [None]

            def load_tiles(i):
                tile_regs[0] = node_tiles(nc, BY_DST, hi_row, i, VALUE)

            def node_tile(u, lag):
                return tile_regs[0][VALUE + (u if u < UNROLL - lag else u - UNROLL)]

            def prepare(t, u, r):
                wait(v, valued, t - 3)
                nc.vector.tensor_scalar(other[:, u % 4, :], c["iota_bf"][:], cols(lo, t), None,
                                        ALU.not_equal).then_inc(prepared, 1)
                wait(v, scored, t - 1)
                nc.vector.tensor_scalar(qs[:, u % 2, :, :], qT[:, :, bass.ds(node_tile(u, TURN) * P, P)], 1.0, None,
                                        ALU.mult).then_inc(prepared, 1)

            def maxima(t, u, r):
                n = node_tile(u, SCORE)
                top = tile_of(top_score, n)
                v.wait_ge(scored, t + 1)
                nc.vector.tensor_reduce(tmax[:], p_s[u % 2][:, :].rearrange("p (h e) -> p h e", h=H), AX.X,
                                        ALU.max).then_inc(reduced, 1)
                v.wait_ge(reduced, t + 1)
                wait(v, kept, t)
                nc.vector.tensor_tensor(new_top[:], tmax[:], top, ALU.max).then_inc(raised, 1)
                v.wait_ge(raised, t + 1)
                wait(v, exped, t - 1)
                wait(v, shrunk, t - 1)
                nc.vector.tensor_scalar(minus[:, u % 2, :], new_top[:], -(DH ** -0.5), None, ALU.mult).then_inc(lowered, 1)
                nc.vector.tensor_tensor(drop[:, u % 2, :], top, new_top[:], ALU.subtract).then_inc(lowered, 1)
                v.wait_ge(lowered, t * 2 + 2)
                nc.vector.tensor_scalar(top, new_top[:], 1.0, None, ALU.mult).then_inc(kept, 1)

            def add_up(t, u, r):
                n = node_tile(u, VALUE)
                v.wait_ge(valued, t + 1)
                v.wait_ge(shrunk, t + 1)
                wait(v, summed, t * 5)
                sums = tile_of(acc, n)
                for h in range(H):
                    part = sums[:, h * VW:h * VW + VW]
                    nc.vector.scalar_tensor_tensor(part, part, shrink[:, u % 4, h:h + 1],
                                                   p_v[u % 2][:, h * VW:h * VW + VW], ALU.mult, ALU.add).then_inc(summed, 1)
                count = cols(no_edges, n)
                nc.vector.scalar_tensor_tensor(count, p_v[u % 2][:, H * VW:H * VW + 1], -float(P), count, ALU.add,
                                               ALU.add).then_inc(summed, 1)
            pipelined(v, T, UNROLL, [(TURN, prepare), (SCORE, maxima), (VALUE, add_up)], top=load_tiles)

FF = 4 * D
FC = FF // P
EXPERTS = 8
BN_EPS = 1e-3


def feed_forward(nc, c, x, w, acc_dram, skip_dram, side, side_loads):
    with ExitStack() as ctx:
        a = Alloc(nc, ctx, "ff")
        rows = {n: a.sb(n, [P, D]) for n in ("ln1_g", "ln1_b", "ln2_g", "ln2_b", "b2")}
        w1 = a.sb("w1", [P, KC, FF])
        w2 = a.sb("w2", [P, FC, D])
        b1 = a.sb("b1", [P, FC])
        norm1 = Normed(Alloc(nc, ctx, "ff_n1"), rows["ln1_g"], rows["ln1_b"])
        norm2 = Normed(Alloc(nc, ctx, "ff_n2"), rows["ln2_g"], rows["ln2_b"], turned=False)
        sums = a.sb("sums", [P, GROUP, H * VW])
        skip = a.sb("skip", [P, GROUP, D])
        weight = a.sb("weight", [P, GROUP, H])
        y = a.sb("y", [P, GROUP, D])
        h_b2 = a.sb("h_b2", [P, GROUP, D])
        z = a.sb("z", [P, GROUP, D])
        hidden = a.sb("hidden", [P, FC, GW])
        p_1 = [a.ps(f"p1{i}", [P, 512]) for i in range(3)]
        p_2 = [a.ps(f"p2{i}", [P, 512]) for i in range(3)]
        loaded, fetched, used = a.sem("loaded"), a.sem("fetched"), a.sem("used")
        den, inv, att, biased = a.sem("den"), a.sem("inv"), a.sem("att"), a.sem("biased")
        up, gelued, down, evacuated, added = a.sem("up"), a.sem("gelued"), a.sem("down"), a.sem("evacuated"), a.sem("added")
        loads = [(w1, chunked(w["W1"])), (w2, chunked(w["W2"])), (b1, w["b1"].rearrange("(c p) -> p c", p=P))]
        loads += [(t, w[n].partition_broadcast(P)) for n, t in rows.items()]
        block = ctx.enter_context(nc.Block())

        @block.gpsimd
        def _(pool):
            side(pool)

        @block.sync
        def _(sp):
            for to, from_ in loads:
                sp.dma_start(to[:], from_, allow_slow_non_contiguous=True).then_inc(loaded, 16)

            def fetch(g, u, r):
                wait(sp, used, g * GROUP)
                sp.dma_start(sums[:], acc_dram[:, bass.ds(g * GROUP, GROUP), :]).then_inc(fetched, 16)
                sp.dma_start(skip[:], tiled(skip_dram)[:, bass.ds(g * GROUP, GROUP), :]).then_inc(fetched, 16)
            groups(sp, [(0, fetch)])
            side_loads(sp)

        @block.tensor
        def _(pe):
            pe.wait_ge(loaded, 16 * len(loads))

            def group(g, u, r):
                norm1.turn(nc, pe, g, c["ident"])
                pe.wait_ge(norm1.copied, g * len(norm1.BATCHES) + len(norm1.BATCHES))
                for m in range(FC):
                    for h in range(2):
                        i = 2 * m + h
                        wait(pe, gelued, g * 2 * FC + (i - 2))
                        for k in range(KC):
                            mm = nc.tensor.matmul(p_1[i % 3][:, 0:HALF], w1[:, k, m * P:m * P + P],
                                                  norm1.xnT[:, k, h * HALF:(h + 1) * HALF],
                                                  start=(k == 0), stop=(k == KC - 1))
                        mm.then_inc(up, 1)
                pe.wait_ge(gelued, g * 2 * FC + 2 * FC)
                for t in range(GROUP):
                    if t < 3:
                        wait(pe, evacuated, g * GROUP)
                    else:
                        pe.wait_ge(evacuated, g * GROUP + (t - 2))
                    for m in range(FC):
                        mm = nc.tensor.matmul(p_2[t % 3][:, 0:D], hidden[:, m, t * P:t * P + P], w2[:, m, :],
                                              start=(m == 0), stop=(m == FC - 1))
                    mm.then_inc(down, 1)
            groups(pe, [(0, group)])

        @block.scalar
        def _(act):
            act.wait_ge(loaded, 16 * len(loads))

            def first(g, u, r):
                norm1.on_scalar(nc, act, g)
                norm1.copy(nc, act, g)

            def gelu(g, u, r):
                wait(act, down, g * GROUP)
                for m in range(FC):
                    for h in range(2):
                        i = 2 * m + h
                        act.wait_ge(up, g * 2 * FC + i + 1)
                        nc.scalar.activation(hidden[:, m, h * HALF:(h + 1) * HALF], p_1[i % 3][:, 0:HALF], ACT.Gelu,
                                             bias=b1[:, m:m + 1]).then_inc(gelued, 1)

            def second(g, u, r):
                norm2.on_scalar(nc, act, g)
            pipelined(act, GROUPS, 1, [(0, first), (1, second), (0, gelu)])

        @block.vector
        def _(v):
            v.wait_ge(loaded, 16 * len(loads))

            def attention(g, u, r):
                v.wait_ge(fetched, g * 32 + 32)
                heads = [sums[:, t, :].rearrange("p (h w) -> p h w", w=VW) for t in range(GROUP)]
                for t in range(GROUP):
                    nc.vector.tensor_scalar(weight[:, t, :], heads[t][:, :, DH], 1e-16, None, ALU.add).then_inc(den, 1)
                v.wait_ge(den, g * GROUP + GROUP)
                nc.vector.reciprocal(weight[:], weight[:]).then_inc(inv, 1)
                v.wait_ge(inv, g + 1)
                for t in range(GROUP):
                    nc.vector.tensor_tensor(y[:, t, :].rearrange("p (h w) -> p h w", w=DH), heads[t][:, :, 0:DH],
                                            weight[:, t, :].unsqueeze(2).to_broadcast([P, H, DH]),
                                            ALU.mult).then_inc(att, 1)
                for t in range(GROUP):
                    v.wait_ge(att, g * GROUP + t + 1)
                    nc.vector.tensor_tensor(y[:, t, :], y[:, t, :], skip[:, t, :], ALU.add).then_inc(used, 1)
                v.wait_ge(used, g * GROUP + GROUP)
                norm1.on_vector(nc, v, g, lambda k: y[:, k, :])

            def output(g, u, r):
                for t in range(GROUP):
                    v.wait_ge(down, g * GROUP + t + 1)
                    nc.vector.tensor_tensor(z[:, t, :], p_2[t % 3][:, 0:D], h_b2[:, t, :], ALU.add).then_inc(evacuated, 1)
                v.wait_ge(evacuated, g * GROUP + GROUP)
                norm2.on_vector(nc, v, g, lambda k: z[:, k, :])
                v.wait_ge(norm2.normed, g * norm2.steps + norm2.steps)
                for t in range(GROUP):
                    rows_of_x = tile_of(x, g * GROUP + t)
                    nc.vector.tensor_tensor(rows_of_x, rows_of_x, norm2.xn[:, t, :], ALU.add).then_inc(added, 1)

            def keep_h(g, u, r):
                v.wait_ge(norm1.normed, g * norm1.steps + norm1.steps)
                wait(v, evacuated, g * GROUP)
                for t in range(GROUP):
                    nc.vector.tensor_tensor(h_b2[:, t, :], norm1.xn[:, t, :], rows["b2"][:], ALU.add).then_inc(biased, 1)
                wait(v, added, g * GROUP)
                v.wait_ge(biased, g * GROUP + GROUP)
                v.wait_ge(norm1.turned, g * len(norm1.BATCHES) + len(norm1.BATCHES))
            pipelined(v, GROUPS, 1, [(0, attention), (1, output), (0, keep_h)])


def mixture(nc, c, x, w, side):
    E = EXPERTS
    with ExitStack() as ctx:
        a = Alloc(nc, ctx, "moe")
        norm = Normed(Alloc(nc, ctx, f"{a.stage}_n"))
        layers = [a.sb(n, [P, E, KC, D]) for n in ("W1", "W2", "Wo")]
        wr = a.sb("Wr", [P, KC, E])
        br = a.sb("br", [P, E])
        bo = a.sb("bo", [E, D])
        bn = {n: a.sb(n, [P, E, KC]) for i in "12" for n in (f"b{i}", f"g{i}", f"be{i}", f"m{i}", f"v{i}")}
        logits = a.sb("logits", [P, GROUP, E])
        top = a.sb("top", [P, GROUP])
        total = a.sb("total", [P, GROUP])
        share = a.sb("share", [P, GROUP, E])
        shareT = a.sb("shareT", [E, GW])
        h1 = a.sb("h1", [P, KC, GW])
        h2 = a.sb("h2", [P, 2, KC, GW])
        p_r = a.ps("r", [P, 512])
        p_1 = [a.ps(f"p1{i}", [P, 512]) for i in range(3)]
        p_o = [a.ps(f"po{i}", [P, 512]) for i in range(2)]
        loaded, folded, rooted, ready = a.sem("loaded"), a.sem("folded"), a.sem("rooted"), a.sem("ready")
        routed, gated, exped, shared = a.sem("routed"), a.sem("gated"), a.sem("exped"), a.sem("shared")
        folding, summed = a.sem("folding"), a.sem("summed")
        share_turned, share_copied = a.sem("share_turned"), a.sem("share_copied")
        made, activated, out, added = a.sem("made"), a.sem("activated"), a.sem("out"), a.sem("added")
        loads = [(wr[:], chunked(w["Wr"])), (br[:], w["br"].partition_broadcast(P)), (bo[:], w["bo"])]
        loads += [(tile[:, e, :, :], chunked(w[n][e])) for n, tile in zip(("W1", "W2", "Wo"), layers) for e in range(E)]
        loads += [(tile[:, :, k], w[n][:, k * P:k * P + P].rearrange("e p -> p e")) for n, tile in bn.items()
                  for k in range(KC)]
        PER = 2 * 2 * KC * E
        OUT = (E + 1) * GROUP
        block = ctx.enter_context(nc.Block())

        @block.gpsimd
        def _(pool):
            side(pool)

        @block.sync
        def _(sp):
            for to, from_ in loads:
                sp.dma_start(to, from_, allow_slow_non_contiguous=True).then_inc(loaded, 16)

        @block.tensor
        def _(pe):
            pe.wait_ge(loaded, 16 * len(loads))

            def hidden(g, i, weight, moving):
                for m in range(KC):
                    for h in range(2):
                        wait(pe, activated, g * PER + (i - 2))
                        for k in range(KC):
                            mm = nc.tensor.matmul(p_1[i % 3][:, 0:HALF], weight[:, k, m * P:m * P + P],
                                                  moving[:, k, h * HALF:(h + 1) * HALF],
                                                  start=(k == 0), stop=(k == KC - 1))
                        mm.then_inc(made, 1)
                        i += 1
                return i

            def group(g, u, r):
                norm.turn(nc, pe, g, c["ident"])
                pe.wait_ge(norm.copied, g * len(norm.BATCHES) + len(norm.BATCHES))
                wait(pe, share_copied, g * 2)
                for t in range(GROUP):
                    for k in range(KC):
                        mm = nc.tensor.matmul(p_r[:, t * E:t * E + E], norm.xnT[:, k, t * P:t * P + P], wr[:, k, :],
                                              start=(k == 0), stop=(k == KC - 1))
                mm.then_inc(routed, 1)
                i, o = 0, 0

                def output(lhsTs, rhss):
                    nonlocal o
                    for t in range(GROUP):
                        wait(pe, added, g * OUT + (o - 1))
                        for k, rhs in enumerate(rhss):
                            mm = nc.tensor.matmul(p_o[o % 2][:, 0:D], lhsTs[k][:, t * P:t * P + P], rhs,
                                                  start=(k == 0), stop=(k == len(rhss) - 1))
                        mm.then_inc(out, 1)
                        o += 1
                for e in range(E):
                    i = hidden(g, i, layers[0][:, e], norm.xnT)
                    if e == 0:
                        pe.wait_ge(shared, g + 1)
                        for b, (k0, n) in enumerate(((0, 4), (4, GROUP - 4))):
                            wait(pe, share_copied, g * 2 + b)
                            for t in range(n):
                                mm = nc.tensor.transpose(p_r[0:E, t * P:t * P + P], share[:, k0 + t, :], c["ident"][:])
                            mm.then_inc(share_turned, 1)
                    else:
                        output([h2[:, (e - 1) % 2, k, :] for k in range(KC)],
                               [layers[2][:, e - 1, k, :] for k in range(KC)])
                    pe.wait_ge(activated, g * PER + i)
                    i = hidden(g, i, layers[1][:, e], h1)
                    if e == 0:
                        pe.wait_ge(share_copied, g * 2 + 2)
                        output([shareT], [bo[:]])
                pe.wait_ge(activated, g * PER + i)
                output([h2[:, (E - 1) % 2, k, :] for k in range(KC)], [layers[2][:, E - 1, k, :] for k in range(KC)])
            groups(pe, [(0, group)])

        @block.scalar
        def _(act):
            act.wait_ge(folded, 2)
            for i in "12":
                nc.scalar.activation(bn[f"v{i}"][:], bn[f"v{i}"][:], ACT.Sqrt).then_inc(rooted, 1)
            act.wait_ge(ready, 2)

            def group(g, u, r):
                norm.on_scalar(nc, act, g)
                norm.copy(nc, act, g)
                act.wait_ge(gated, g * (2 + GROUP) + 2 + GROUP)
                nc.scalar.activation(share[:], logits[:], ACT.Exp).then_inc(exped, 1)
                i = 0
                for e in range(E):
                    for n, to in (("1", h1), ("2", h2[:, e % 2])):
                        if n == "2" and e == 0:
                            for b, (k0, c0) in enumerate(((0, 4), (4, GROUP - 4))):
                                act.wait_ge(share_turned, g * 2 + b + 1)
                                nc.scalar.activation(shareT[:, k0 * P:(k0 + c0) * P], p_r[0:E, 0:c0 * P],
                                                     ACT.Copy).then_inc(share_copied, 1)
                        if n == "2" and e >= 2:
                            act.wait_ge(out, g * OUT + e * GROUP)
                        elif n == "2":
                            wait(act, out, g * OUT)
                        for m in range(KC):
                            for h in range(2):
                                act.wait_ge(made, g * PER + i + 1)
                                nc.scalar.activation(to[:, m, h * HALF:(h + 1) * HALF], p_1[i % 3][:, 0:HALF], ACT.Relu,
                                                     bias=bn[f"b{n}"][:, e, m:m + 1],
                                                     scale=bn[f"g{n}"][:, e, m:m + 1]).then_inc(activated, 1)
                                i += 1
            groups(act, [(0, group)])

        @block.vector
        def _(v):
            v.wait_ge(loaded, 16 * len(loads))
            done = [0]

            def step(ins):
                done[0] += 1
                ins.then_inc(folding, 1)
                v.wait_ge(folding, done[0])
            for i in "12":
                var = bn[f"v{i}"][:]
                step(nc.vector.tensor_scalar(var, var, BN_EPS, None, ALU.add))
                nc.vector.reciprocal(var, var).then_inc(folded, 1)
            v.wait_ge(rooted, 2)
            for i in "12":
                scale, shift = bn[f"g{i}"][:], bn[f"b{i}"][:]
                step(nc.vector.tensor_tensor(scale, scale, bn[f"v{i}"][:], ALU.mult))
                step(nc.vector.tensor_tensor(shift, shift, bn[f"m{i}"][:], ALU.subtract))
                step(nc.vector.tensor_tensor(shift, shift, scale, ALU.mult))
                nc.vector.tensor_tensor(shift, shift, bn[f"be{i}"][:], ALU.add).then_inc(ready, 1)

            def group(g, u, r):
                wait(v, added, g * OUT)
                norm.on_vector(nc, v, g, lambda k: tile_of(x, g * GROUP + k))
                v.wait_ge(routed, g + 1)
                v.wait_ge(norm.turned, g * len(norm.BATCHES) + len(norm.BATCHES))
                for t in range(GROUP):
                    nc.vector.tensor_tensor(logits[:, t, :], p_r[:, t * E:t * E + E], br[:], ALU.add).then_inc(gated, 1)
                v.wait_ge(gated, g * (2 + GROUP) + GROUP)
                nc.vector.tensor_reduce(top[:], logits[:], AX.X, ALU.max).then_inc(gated, 1)
                v.wait_ge(gated, g * (2 + GROUP) + 1 + GROUP)
                nc.vector.tensor_tensor(logits[:], logits[:], top[:].unsqueeze(2).to_broadcast([P, GROUP, E]),
                                        ALU.subtract).then_inc(gated, 1)
                v.wait_ge(exped, g + 1)
                nc.vector.tensor_reduce(total[:], share[:], AX.X, ALU.add).then_inc(summed, 1)
                v.wait_ge(summed, g * 2 + 1)
                nc.vector.reciprocal(total[:], total[:]).then_inc(summed, 1)
                v.wait_ge(summed, g * 2 + 2)
                nc.vector.tensor_tensor(share[:], share[:], total[:].unsqueeze(2).to_broadcast([P, GROUP, E]),
                                        ALU.mult).then_inc(shared, 1)
                v.wait_ge(shared, g + 1)
                for o in range(OUT):
                    e, t = o // GROUP - 1, o % GROUP
                    v.wait_ge(out, g * OUT + o + 1)
                    if o >= GROUP:
                        v.wait_ge(added, g * OUT + (o + 1 - GROUP))
                    rows_of_x = tile_of(x, g * GROUP + t)
                    if e < 0:
                        nc.vector.tensor_tensor(rows_of_x, p_o[o % 2][:, 0:D], rows_of_x, ALU.add).then_inc(added, 1)
                    else:
                        nc.vector.scalar_tensor_tensor(rows_of_x, p_o[o % 2][:, 0:D], share[:, t, e:e + 1], rows_of_x,
                                                       ALU.mult, ALU.add).then_inc(added, 1)
            groups(v, [(0, group)])

EDGE_F = 64
HALF_F = 128
ATTR_W = EDGE_F + 1
CHUNK = UNROLL // 2


def empty_attributes(nc, ctx, st, n):
    empty = Alloc(nc, ctx, "empty_attr").sb("slots", [P, n, ATTR_W])
    with ExitStack() as bctx:
        zeroed = Alloc(nc, bctx, "empty_attr_zeroed").sem("zeroed")
        block = bctx.enter_context(nc.Block())

        @block.vector
        def _(v):
            nc.vector.memset(empty[:], 0.0).then_inc(zeroed, 1)
            v.wait_ge(zeroed, 1)
            nc.vector.memset(empty[:, :, EDGE_F], float(PAD_LO))
    return empty


def load_attributes(nc, sp, scatter, attr_dram):
    st = scatter.st
    attr = attr_dram.rearrange("(p c) f -> p c f", p=st.parts)

    def load(t, u, r):
        wait(sp, scatter.landed[u], r * (16 * SCATTER))
        data = scatter.data[:, u, :].rearrange("p (c w) -> p c w", w=ATTR_W)
        sp.dma_start(data[:, :, 0:EDGE_F], attr[:, bass.ds(t * SCATTER, SCATTER), :]).then_inc(scatter.loaded[u], 16)
    pipelined(sp, scatter.chunks, 2, [(0, load)])


def segment_sum(nc, c, st, hi_row, width, sums, rows_dram, source=None, lo=None):
    gathers = source is not None
    row_w = width if gathers else width + 1
    with ExitStack() as ctx:
        a = Alloc(nc, ctx, f"sum_{st.name}_{width}")
        ring = a.sb("ring", [P, UNROLL, row_w])
        mine = a.sb("mine", [P, 4, P])
        p_sum = [a.ps(f"sum{i}", [P, 512]) for i in range(4)]
        index = a.sb("index", [P, 2, UNROLL], I32)
        arrived = a.sems("arrived", UNROLL)
        staged, passed = a.sem("staged"), a.sem("passed")
        marked, multiplied, summed = a.sem("marked"), a.sem("multiplied"), a.sem("summed")
        block = ctx.enter_context(nc.Block())
        LAG = 2

        def landed(eng, u, r):
            eng.wait_ge(arrived[u if gathers else u // CHUNK], r * 16 + 16)

        if gathers:
            @block.gpsimd
            def _(pool):
                gather_loop(nc, pool, st.tiles, source, index, staged, passed, rows_dram, ring, arrived, multiplied)
        else:
            @block.sync
            def _(sp):
                rows = rows_dram.rearrange("(p t) w -> p t w", p=P)

                def load(t, u, r):
                    wait(sp, multiplied, t * CHUNK - CHUNK)
                    sp.dma_start(ring[:, u * CHUNK:(u + 1) * CHUNK, :],
                                 rows[:, bass.ds(t * CHUNK, CHUNK), :]).then_inc(arrived[u], 16)
                pipelined(sp, st.tiles // CHUNK, 2, [(0, load)])

        @block.tensor
        def _(pe):
            def product(t, u, r):
                landed(pe, u, r)
                pe.wait_ge(marked, t + 1)
                wait(pe, summed, t - 3)
                nc.tensor.matmul(p_sum[u % 4][:, 0:width], mine[:, u % 4, :], ring[:, u, 0:width], start=True,
                                 stop=True).then_inc(multiplied, 1)
            pipelined(pe, st.tiles, UNROLL, [(0, product)])

        @block.vector
        def _(v):
            tile_regs = [None]

            def load_tiles(i):
                tile_regs[0] = node_tiles(nc, st, hi_row, i, LAG)

            def mark(t, u, r):
                wait(v, multiplied, t - 3)
                if gathers:
                    at = cols(lo, t)
                else:
                    landed(v, u, r)
                    at = ring[:, u, width:width + 1]
                nc.vector.tensor_scalar(mine[:, u % 4, :], c["iota"][:], at, None, ALU.is_equal).then_inc(marked, 1)

            def add_up(t, u, r):
                n = tile_regs[0][LAG + (u if u < UNROLL - LAG else u - UNROLL)]
                v.wait_ge(multiplied, t + 1)
                wait(v, summed, t)
                part = tile_of(sums, n)
                nc.vector.tensor_tensor(part, part, p_sum[u % 4][:, 0:width], ALU.add).then_inc(summed, 1)
            pipelined(v, st.tiles, UNROLL, [(0, mark), (LAG, add_up)], top=load_tiles)


def convolve_dense(nc, c, x, w, per_node, no_edges, dinv, sums, rest, conv_dram):
    with ExitStack() as ctx:
        a = Alloc(nc, ctx, "conv")
        norm = Normed(Alloc(nc, ctx, "conv_n"))
        HC3 = KC + HALF_F // P
        we = a.sb("W_edge", [EDGE_F, HALF_F])
        be = a.sb("b_edge", [P, 1])
        both = a.sb("both", [P, HC3, 2 * D])
        bias = a.sb("bias", [P, D])
        bias2 = a.sb("bias2", [P, D])
        per = a.sb("per", [P, GROUP, EDGE_F])
        pnT = a.sb("pnT", [P, GW])
        perT, z = pnT[0:EDGE_F, :], pnT
        p_e = [a.ps(f"e{i}", [P, 512]) for i in range(2)]
        p_c = [a.ps(f"c{i}", [P, 512]) for i in range(3)]
        loaded, prepared, rooted, ready = a.sem("loaded"), a.sem("prepared"), a.sem("rooted"), a.sem("ready")
        per_staged, passed = a.sem("per_staged"), a.sem("passed")
        per_turned, per_copied, edged, z_made, leaked = (a.sem(n) for n in (
            "per_turned", "per_copied", "edged", "z_made", "leaked"))
        made, scaled, rested, stored = a.sem("made"), a.sem("scaled"), a.sem("rested"), a.sem("stored")
        loads = [(we[:], w["W_edge"]), (be[:], w["b_edge"].rearrange("(p a) -> p a", a=1)),
                 (both[:, :, 0:D], chunked(w["W_conv"])), (both[:, :, D:], chunked(w["W_res"])),
                 (bias[:], w["b_conv"].partition_broadcast(P)), (bias2[:], w["b_res"].partition_broadcast(P))]
        block = ctx.enter_context(nc.Block())
        BATCH = ((0, 4), (4, GROUP - 4))

        @block.sync
        def _(sp):
            for to, from_ in loads:
                sp.dma_start(to, from_, allow_slow_non_contiguous=True).then_inc(loaded, 16)

            def store(g, u, r):
                sp.wait_ge(scaled, g * GROUP + GROUP)
                sp.dma_start(tiled(conv_dram)[:, bass.ds(g * GROUP, GROUP), :],
                             sums[:, bass.ds(g * GROUP, GROUP), :]).then_inc(stored, 16)
            groups(sp, [(0, store)])
            sp.wait_ge(stored, 16 * GROUPS)

        @block.tensor
        def _(pe):
            pe.wait_ge(loaded, 16 * len(loads))

            def group(g, u, r):
                wait(pe, z_made, g * 2)
                wait_alone(pe, per_staged, g + 1, passed)
                for b, (k0, n) in enumerate(BATCH):
                    for t in range(n):
                        mm = nc.tensor.transpose(p_e[b][0:EDGE_F, t * P:t * P + P], per[:, k0 + t, :], c["ident"][:])
                    mm.then_inc(per_turned, 1)
                norm.turn(nc, pe, g, c["ident"])
                pe.wait_ge(per_copied, g * 2 + 2)
                for h in range(2):
                    nc.tensor.matmul(p_e[h][:, 0:HALF], we[:], perT[:, h * HALF:(h + 1) * HALF], start=True,
                                     stop=True).then_inc(edged, 1)
                pe.wait_ge(norm.copied, g * len(norm.BATCHES) + len(norm.BATCHES))
                pe.wait_ge(leaked, g + 1)
                for t in range(GROUP):
                    if t < 3:
                        wait(pe, rested, g * 2 * GROUP)
                    else:
                        pe.wait_ge(rested, g * 2 * GROUP + (t - 2) * 2)
                    for k in range(HC3):
                        lhsT = norm.xnT[:, k, t * P:t * P + P] if k < KC else pnT[:, t * P:t * P + P]
                        mm = nc.tensor.matmul(p_c[t % 3][:, :], lhsT, both[:, k, :], start=(k == 0), stop=(k == HC3 - 1))
                    mm.then_inc(made, 1)
            groups(pe, [(0, group)])

        @block.scalar
        def _(act):
            act.wait_ge(prepared, 3)
            nc.scalar.activation(dinv[:], dinv[:], ACT.Sqrt).then_inc(rooted, 1)

            def group(g, u, r):
                for b, (k0, n) in enumerate(BATCH):
                    act.wait_ge(per_turned, g * 2 + b + 1)
                    nc.scalar.activation(perT[:, k0 * P:(k0 + n) * P], p_e[b][0:EDGE_F, 0:n * P], ACT.Copy).then_inc(per_copied, 1)
                norm.on_scalar(nc, act, g)
                norm.copy(nc, act, g)
            groups(act, [(0, group)])

        @block.vector
        def _(v):
            v.wait_ge(loaded, 16 * len(loads))
            nc.vector.tensor_tensor(bias[:], bias[:], bias2[:], ALU.add).then_inc(prepared, 1)
            nc.vector.tensor_scalar(dinv[:], no_edges[:, 0:NT], -1.0, 1.0, ALU.mult, ALU.add).then_inc(prepared, 1)
            v.wait_ge(prepared, 2)
            nc.vector.reciprocal(dinv[:], dinv[:]).then_inc(prepared, 1)
            v.wait_ge(rooted, 1)

            def group(g, u, r):
                wait(v, per_turned, g * 2)
                nc.vector.tensor_scalar(per[:], per_node[:, bass.ds(g * GROUP, GROUP), :], 1.0, None,
                                        ALU.mult).then_inc(per_staged, 1)
                norm.on_vector(nc, v, g, lambda k: tile_of(x, g * GROUP + k))
                wait(v, made, g * GROUP)
                for h in range(2):
                    v.wait_ge(edged, g * 2 + h + 1)
                    nc.vector.tensor_scalar(z[:, h * HALF:(h + 1) * HALF], p_e[h][:, 0:HALF], be[:, 0:1], None,
                                            ALU.add).then_inc(z_made, 1)
                v.wait_ge(z_made, g * 2 + 2)
                nc.vector.scalar_tensor_tensor(pnT[:], pnT[:], 0.01, pnT[:], ALU.mult, ALU.max).then_inc(leaked, 1)
                v.wait_ge(leaked, g + 1)
                for t in range(GROUP):
                    n = g * GROUP + t
                    v.wait_ge(made, g * GROUP + t + 1)
                    nc.vector.tensor_scalar(tile_of(sums, n), p_c[t % 3][:, 0:D], cols(dinv, n), None,
                                            ALU.mult).then_inc(scaled, 1)
                    nc.vector.tensor_tensor(tile_of(rest, n), p_c[t % 3][:, D:2 * D], bias[:], ALU.add).then_inc(rested, 2)
                v.wait_ge(rested, g * 2 * GROUP + 2 * GROUP)
            groups(v, [(0, group)])


def convolve_end(nc, x, dinv, sums, rest):
    with ExitStack() as ctx:
        a = Alloc(nc, ctx, "conv_end")
        scaled, added = a.sem("scaled"), a.sem("added")
        block = ctx.enter_context(nc.Block())

        @block.vector
        def _(v):
            def scale(t, u, r):
                nc.vector.scalar_tensor_tensor(tile_of(rest, t), tile_of(sums, t), cols(dinv, t), tile_of(rest, t),
                                               ALU.mult, ALU.add).then_inc(scaled, 1)

            def add(t, u, r):
                v.wait_ge(scaled, t + 1)
                nc.vector.scalar_tensor_tensor(tile_of(x, t), tile_of(rest, t), 0.0, tile_of(x, t), ALU.max,
                                               ALU.add).then_inc(added, 1)
            pipelined(v, NT, GROUP, [(0, scale), (1, add)])

E3X = 4
HEADW = H * E3X
SCORES, VECTORS, PARTS = slice(0, H), slice(H, H + HEADW), slice(H + HEADW, H + HEADW + 3 * H)
KEPT = H + HEADW
ROWW = KEPT + 3 * H


def router_rows(nc, c, x, w, rows, target, top, table_dram):
    with ExitStack() as ctx:
        a = Alloc(nc, ctx, "router")
        norm = Normed(Alloc(nc, ctx, "router_n"))
        wg = a.sb("wg", [P, KC, HEADW])
        att = [a.sb(n, [P, HEADW]) for n in ("att_src", "att_dst")]
        row = a.sb("row", [P, GROUP, ROWW])
        prod = [a.sb(f"prod{i}", [P, GROUP, HEADW]) for i in range(2)]
        part = a.sb("part", [P, GROUP, H], BF16)
        left = a.sb("left", [P, GROUP, H])
        p_h = a.ps("h", [P, 512])
        loaded, cleared, made = a.sem("loaded"), a.sem("cleared"), a.sem("made")
        stepped, stored = a.sem("stepped"), a.sem("stored")
        loads = [(wg[:], chunked(w["W_gat"]))]
        loads += [(tile[:], w[n].rearrange("h e -> (h e)").partition_broadcast(P))
                  for n, tile in zip(("att_src", "att_dst"), att)]
        STEPS = 15
        block = ctx.enter_context(nc.Block())

        @block.gpsimd
        def _(pool):
            nc.gpsimd.memset(target[:], 0.0).then_inc(cleared, 1)
            nc.gpsimd.memset(top[:], 0.0).then_inc(cleared, 1)

        @block.sync
        def _(sp):
            for to, from_ in loads:
                sp.dma_start(to, from_, allow_slow_non_contiguous=True).then_inc(loaded, 16)

            def store(g, u, r):
                sp.wait_ge(stepped, g * STEPS + STEPS)
                sp.dma_start(tiled(table_dram)[:, bass.ds(g * GROUP, GROUP), :], row[:]).then_inc(stored, 16)
            groups(sp, [(0, store)])
            sp.wait_ge(stored, 16 * GROUPS)

        @block.tensor
        def _(pe):
            pe.wait_ge(loaded, 16 * len(loads))

            def group(g, u, r):
                norm.turn(nc, pe, g, c["ident"])
                pe.wait_ge(norm.copied, g * len(norm.BATCHES) + len(norm.BATCHES))
                wait(pe, stepped, g * STEPS)
                for t in range(GROUP):
                    for k in range(KC):
                        mm = nc.tensor.matmul(p_h[:, t * HEADW:(t + 1) * HEADW], norm.xnT[:, k, t * P:t * P + P],
                                              wg[:, k, :], start=(k == 0), stop=(k == KC - 1))
                mm.then_inc(made, 1)
            groups(pe, [(0, group)])

        @block.scalar
        def _(act):
            def group(g, u, r):
                norm.on_scalar(nc, act, g)
                norm.copy(nc, act, g)
            groups(act, [(0, group)])

        @block.vector
        def _(v):
            v.wait_ge(loaded, 16 * len(loads))
            v.wait_ge(cleared, 2)

            def group(g, u, r):
                norm.on_vector(nc, v, g, lambda k: tile_of(x, g * GROUP + k))
                done = [0]

                def step(ins):
                    done[0] += 1
                    ins.then_inc(stepped, 1)
                    v.wait_ge(stepped, g * STEPS + done[0])
                here = bass.ds(g * GROUP, GROUP)
                v.wait_ge(norm.turned, g * len(norm.BATCHES) + len(norm.BATCHES))
                wait(v, stored, g * 16)
                v.wait_ge(made, g + 1)
                step(nc.vector.tensor_scalar(row[:, :, VECTORS], p_h[:, 0:GROUP * HEADW].rearrange("p (t w) -> p t w", w=HEADW),
                                             1.0, None, ALU.mult))
                for i in range(2):
                    step(nc.vector.tensor_tensor(prod[i][:], row[:, :, VECTORS],
                                                 att[i][:].unsqueeze(1).to_broadcast([P, GROUP, HEADW]), ALU.mult))
                heads = [p[:].rearrange("p t (h e) -> p t h e", e=E3X) for p in prod]
                step(nc.vector.tensor_reduce(row[:, :, SCORES], heads[0], AX.X, ALU.add))
                step(nc.vector.tensor_reduce(target[:, here, :], heads[1], AX.X, ALU.add))
                step(nc.vector.tensor_scalar(top[:, here, :], row[:, :, SCORES], 1.0, None, ALU.mult))
                parts = row[:, :, PARTS].rearrange("p t (h i) -> p t h i", i=3)
                rest = row[:, :, SCORES]
                for i in range(3):
                    step(nc.vector.tensor_scalar(part[:], rest, 1.0, None, ALU.mult))
                    step(nc.vector.tensor_scalar(parts[:, :, :, i], part[:], 1.0, None, ALU.mult))
                    if i < 2:
                        step(nc.vector.tensor_tensor(left[:], rest, part[:], ALU.subtract))
                        rest = left[:]
                step(nc.vector.tensor_scalar(rows[:, here, :], row[:, :, 0:KEPT], 1.0, None, ALU.mult))
                assert done[0] == STEPS
            groups(v, [(0, group)])


def gather_batches(nc, pool, tiles, source, index, staged, passed, rows_dram, ring, arrived, freed):
    def batch(b, u, r):
        wait(pool, freed, b * 2 - 2)
        nc.gpsimd.tensor_copy(index[:, u, :], cols(source, b * UNROLL, UNROLL)).then_inc(staged, 1)
        wait_alone(pool, staged, b + 1, passed)
        for k in range(UNROLL):
            pool.indirect_dma_start(ring[:, u, k, :], None, rows_dram,
                                    bass.IndirectOffsetOnAxis(index[:, u, k:k + 1], 0)).then_inc(arrived[u], 16)
    pipelined(pool, tiles // UNROLL, 2, [(0, batch)])


def edge_rows(nc, c, source, lo, hi_row, table_dram, edge, top):
    st = GAT
    with ExitStack() as ctx:
        a = Alloc(nc, ctx, "edge_rows")
        W = UNROLL * 3 * H
        index = a.sb("index", [P, 2, UNROLL], I32)
        ring = a.sb("ring", [P, 2, UNROLL, ROWW])
        parts = a.sb("parts", [P, 2, W])
        partsT = a.sb("partsT", [W, 2, P], BF16)
        select = a.sb("select", [W, UNROLL * H, P], BF16)
        other = a.sb("other", [P, 4, P], BF16)
        tmax = a.sb("tmax", [P, 4, H])
        p_t = [a.ps(f"t{i}", [P, 512]) for i in range(2)]
        p_s = [a.ps(f"s{i}", [P, 512]) for i in range(4)]
        arrived = a.sems("arrived", 2)
        staged, passed, freed = a.sem("staged"), a.sem("passed"), a.sem("freed")
        ones_made, selected = a.sem("ones_made"), a.sem("selected")
        parted, turned, copied = a.sem("parted"), a.sem("turned"), a.sem("copied")
        marked, scored, reduced, kept = a.sem("marked"), a.sem("scored"), a.sem("reduced"), a.sem("kept")
        block = ctx.enter_context(nc.Block())
        BATCHES = st.tiles // UNROLL

        @block.gpsimd
        def _(pool):
            nc.gpsimd.memset(select[:], 1.0).then_inc(ones_made, 1)
            pool.wait_ge(ones_made, 1)
            nc.gpsimd.affine_select(select[:], select[:], [[-3, UNROLL * H], [0, P]], ALU.is_ge, 0.0, base=0,
                                    channel_multiplier=1).then_inc(ones_made, 1)
            pool.wait_ge(ones_made, 2)
            nc.gpsimd.affine_select(select[:], select[:], [[3, UNROLL * H], [0, P]], ALU.is_ge, 0.0, base=2,
                                    channel_multiplier=-1).then_inc(selected, 1)
            gather_batches(nc, pool, st.tiles, source, index, staged, passed, table_dram, ring, arrived, freed)

        @block.scalar
        def _(act):
            def take(b, u, r):
                act.wait_ge(arrived[u], r * (16 * UNROLL) + 16 * UNROLL)
                wait(act, turned, b - 1)
                nc.scalar.activation(parts[:, u, :].rearrange("p (t w) -> p t w", w=3 * H), ring[:, u, :, PARTS],
                                     ACT.Copy).then_inc(freed, 1)
                nc.scalar.activation(edge[:, bass.ds(b * UNROLL, UNROLL), :], ring[:, u, :, 0:KEPT],
                                     ACT.Copy).then_inc(freed, 1)

            def copy(b, u, r):
                act.wait_ge(turned, b + 1)
                wait(act, scored, b * UNROLL - UNROLL)
                nc.scalar.activation(partsT[:, u, :], p_t[u][0:W, 0:P], ACT.Copy).then_inc(copied, 1)
            pipelined(act, BATCHES, 2, [(0, take), (0, copy)])

        @block.tensor
        def _(pe):
            pe.wait_ge(selected, 1)

            def turn(b, u, r):
                pe.wait_ge(freed, b * 2 + 2)
                wait(pe, copied, b - 1)
                nc.tensor.transpose(p_t[u][0:W, 0:P], parts[:, u, :], c["ident"][:]).then_inc(turned, 1)

            def score(b, u, r):
                pe.wait_ge(copied, b + 1)
                for k in range(UNROLL):
                    pe.wait_ge(marked, b * UNROLL + k + 1)
                    if isinstance(b, int):
                        wait(pe, reduced, b * UNROLL + k - 3)
                    else:
                        pe.wait_ge(reduced, b * UNROLL + (k - 3))
                    s = p_s[k % 4]
                    nc.tensor.matmul(s[:, :], other[:, k % 4, :], c["drop4"][:], start=True, stop=False,
                                     skip_group_check=True)
                    for h in range(H):
                        mm = nc.tensor.matmul(s[:, h * P:h * P + P], select[:, k * H + h, :], partsT[:, u, :],
                                              start=False, stop=True, skip_group_check=True)
                    mm.then_inc(scored, 1)
            pipelined(pe, BATCHES, 2, [(0, turn), (1, score)])

        @block.vector
        def _(v):
            tile_regs = [None]
            MAXIMA, KEEP = 2, 3

            def load_tiles(i):
                tile_regs[0] = node_tiles(nc, st, hi_row, i, KEEP)

            def mark(t, u, r):
                wait(v, scored, t - 3)
                nc.vector.tensor_scalar(other[:, u % 4, :], c["iota_bf"][:], cols(lo, t), None,
                                        ALU.not_equal).then_inc(marked, 1)

            def maxima(t, u, r):
                v.wait_ge(scored, t + 1)
                wait(v, kept, t - 3)
                nc.vector.tensor_reduce(tmax[:, u % 4, :], p_s[u % 4][:, :].rearrange("p (h e) -> p h e", h=H), AX.X,
                                        ALU.max).then_inc(reduced, 1)

            def keep(t, u, r):
                n = tile_regs[0][KEEP + (u if u < UNROLL - KEEP else u - UNROLL)]
                v.wait_ge(reduced, t + 1)
                wait(v, kept, t)
                nc.vector.tensor_tensor(tile_of(top, n), tmax[:, u % 4, :], tile_of(top, n), ALU.max).then_inc(kept, 1)
            pipelined(v, st.tiles, UNROLL, [(0, mark), (MAXIMA, maxima), (KEEP, keep)], top=load_tiles)


def leaky(nc, out, z, slope):
    return nc.vector.scalar_tensor_tensor(out, z, slope, z, ALU.mult, ALU.max)


def loops_to_self(nc, rows, target, top, bounds, acc):
    with ExitStack() as ctx:
        a = Alloc(nc, ctx, "self")
        z = a.sb("z", [P, NB, H])
        stepped, exped = a.sem("stepped"), a.sem("exped")
        block = ctx.enter_context(nc.Block())
        nodes = slice(0, NT)

        @block.vector
        def _(v):
            done = [0]

            def step(ins):
                done[0] += 1
                ins.then_inc(stepped, 1)
                v.wait_ge(stepped, done[0])
            nc.vector.memset(acc[:], 0.0).then_inc(stepped, 1)
            done[0] += 1
            step(nc.vector.tensor_scalar(bounds[:, :, 0:H], target[:], 1.0, None, ALU.mult))
            step(nc.vector.tensor_tensor(z[:], target[:], top[:], ALU.add))
            step(leaky(nc, bounds[:, :, H:2 * H], z[:], 0.2))
            step(nc.vector.tensor_tensor(z[:, nodes, :], target[:, nodes, :], rows[:, :, SCORES], ALU.add))
            step(leaky(nc, top[:, nodes, :], z[:, nodes, :], 0.2))
            step(nc.vector.tensor_tensor(z[:, nodes, :], top[:, nodes, :], bounds[:, nodes, H:2 * H], ALU.subtract))
            v.wait_ge(exped, 1)
            for h in range(H):
                vectors = acc[:, nodes, h * E3X:(h + 1) * E3X]
                nc.vector.tensor_tensor(vectors, rows[:, :, H + h * E3X:H + (h + 1) * E3X],
                                        acc[:, nodes, HEADW + h:HEADW + h + 1].to_broadcast([P, NT, E3X]), ALU.mult)

        @block.scalar
        def _(act):
            act.wait_ge(stepped, 7)
            nc.scalar.activation(acc[:, nodes, HEADW:], z[:, nodes, :], ACT.Exp).then_inc(exped, 1)


def edge_sums(nc, c, lo, hi_row, edge, bounds, acc):
    st = GAT
    with ExitStack() as ctx:
        a = Alloc(nc, ctx, "edge_sums")
        mine = a.sb("mine", [P, 2, UNROLL, P])
        mineT = a.sb("mineT", [P, 2, UNROLL, P])
        bound = a.sb("bound", [P, 2, UNROLL, 2 * H])
        z = a.sb("z", [P, 2, UNROLL, H])
        y = a.sb("y", [P, 2, UNROLL, H])
        msg = a.sb("msg", [P, 2, UNROLL, KEPT])
        p_t = [a.ps(f"t{i}", [P, 512]) for i in range(4)]
        p_b = [a.ps(f"b{i}", [P, 512]) for i in range(2)]
        p_a = [a.ps(f"a{i}", [P, 512]) for i in range(2)]
        marked, bounded, turned, copied = a.sem("marked"), a.sem("bounded"), a.sem("turned"), a.sem("copied")
        spread, zed, exped, sent = a.sem("spread"), a.sem("zed"), a.sem("exped"), a.sem("sent")
        multiplied, summed, passed = a.sem("multiplied"), a.sem("summed"), a.sem("passed")
        block = ctx.enter_context(nc.Block())
        BATCHES = st.tiles // UNROLL

        @block.gpsimd
        def _(pool):
            def bounds_of(b, u, r):
                regs = node_tiles(nc, st, hi_row, b, 0, mybir.EngineType.Pool)
                wait(pool, spread, b - 1)
                for k in range(UNROLL):
                    nc.gpsimd.tensor_copy(bound[:, u, k, :], tile_of(bounds, regs[k])).then_inc(bounded, 1)
            pipelined(pool, BATCHES, 2, [(0, bounds_of)])

        @block.tensor
        def _(pe):
            def sum_up(b, u, r):
                pe.wait_ge(sent, b + 1)
                wait(pe, summed, (b - 1) * UNROLL)
                for k in range(UNROLL):
                    mm = nc.tensor.matmul(p_a[u][:, k * KEPT:(k + 1) * KEPT], mine[:, u, k, :], msg[:, u, k, :],
                                          start=True, stop=True)
                mm.then_inc(multiplied, 1)

            def spread_bounds(b, u, r):
                pe.wait_ge(bounded, b * UNROLL + UNROLL)
                wait(pe, copied, b * 2 + 2)
                wait(pe, zed, b * 4 - 4)
                for k in range(UNROLL):
                    mm = nc.tensor.matmul(p_b[u][:, k * 2 * H:(k + 1) * 2 * H], mineT[:, u, k, :], bound[:, u, k, :],
                                          start=True, stop=True)
                mm.then_inc(spread, 1)

            def turn(b, u, r):
                for half in range(2):
                    wait(pe, copied, b * 2 - 3 + half)
                    for k in range(4 * half, 4 * half + 4):
                        pe.wait_ge(marked, b * UNROLL + k + 1)
                        mm = nc.tensor.transpose(p_t[2 * u + half][:, k % 4 * P:k % 4 * P + P], mine[:, u, k, :],
                                                 c["ident"][:])
                    mm.then_inc(turned, 1)
            pipelined(pe, BATCHES, 2, [(2, sum_up), (1, spread_bounds), (0, turn)], peel=2)

        @block.scalar
        def _(act):
            def copy(b, u, r):
                wait(act, spread, b - 1)
                for half in range(2):
                    act.wait_ge(turned, b * 2 + half + 1)
                    nc.scalar.activation(mineT[:, u, 4 * half:4 * half + 4, :].rearrange("p k n -> p (k n)"),
                                         p_t[2 * u + half][:, :], ACT.Copy).then_inc(copied, 1)

            def weigh(b, u, r):
                act.wait_ge(zed, b * 4 + 4)
                wait(act, multiplied, b - 1)
                nc.scalar.activation(msg[:, u, :, HEADW:], z[:, u, :, :], ACT.Exp).then_inc(exped, 1)
            pipelined(act, BATCHES, 2, [(1, weigh), (0, copy)])

        @block.vector
        def _(v):
            def mark(b, u, r):
                wait(v, multiplied, b - 1)
                for k in range(UNROLL):
                    nc.vector.tensor_scalar(mine[:, u, k, :], c["iota"][:], cols(lo, b * UNROLL + k), None,
                                            ALU.is_equal).then_inc(marked, 1)

            def message(b, u, r):
                v.wait_ge(spread, b + 1)
                wait(v, exped, b - 1)
                bd = p_b[u][:, 0:UNROLL * 2 * H].rearrange("p (k w) -> p k w", w=2 * H)
                here = bass.ds(b * UNROLL, UNROLL)
                nc.vector.tensor_tensor(z[:, u, :, :], edge[:, here, SCORES], bd[:, :, 0:H], ALU.add).then_inc(zed, 1)
                v.wait_ge(zed, b * 4 + 1)
                leaky(nc, y[:, u, :, :], z[:, u, :, :], 0.2).then_inc(zed, 1)
                v.wait_ge(zed, b * 4 + 2)
                nc.vector.tensor_tensor(z[:, u, :, :], y[:, u, :, :], bd[:, :, H:2 * H], ALU.subtract).then_inc(zed, 1)
                v.wait_ge(zed, b * 4 + 3)
                nc.vector.tensor_scalar(z[:, u, :, :], z[:, u, :, :], 0.0, None, ALU.min).then_inc(zed, 1)
                v.wait_ge(exped, b + 1)
                nc.vector.tensor_tensor(msg[:, u, :, 0:HEADW].rearrange("p k (h e) -> p k h e", e=E3X),
                                        edge[:, here, VECTORS].rearrange("p k (h e) -> p k h e", e=E3X),
                                        msg[:, u, :, HEADW:].unsqueeze(3).to_broadcast([P, UNROLL, H, E3X]),
                                        ALU.mult).then_inc(sent, 1)

            def add_up(b, u, r):
                regs = node_tiles(nc, st, hi_row, b, 0)
                v.wait_ge(multiplied, b + 1)
                for k in range(UNROLL):
                    wait(v, summed, b * UNROLL + k)
                    nc.vector.tensor_tensor(tile_of(acc, regs[k]), tile_of(acc, regs[k]),
                                            p_a[u][:, k * KEPT:(k + 1) * KEPT], ALU.add).then_inc(summed, 1)
            pipelined(v, BATCHES, 2, [(0, mark), (1, message), (2, add_up)], peel=2)


def gates(nc, w, acc, gate):
    with ExitStack() as ctx:
        a = Alloc(nc, ctx, "gates")
        vecs = {n: a.sb(n, [P, HEADW]) for n in ("b_gat", "ln_gamma", "ln_beta")}
        agg = a.sb("agg", [P, NT, HEADW])
        sq = a.sb("sq", [P, NT, HEADW])
        weight = a.sb("weight", [P, NT, H])
        mean = a.sb("mean", [P, NT])
        rstd = a.sb("rstd", [P, NT])
        score = a.sb("score", [P, NT, E3X])
        over = a.sb("over", [P, NT])
        rank = a.sb("rank", [P, NT, E3X])
        best = a.sb("best", [P, NT])
        loaded, stepped, inverted, rooted = a.sem("loaded"), a.sem("stepped"), a.sem("inverted"), a.sem("rooted")
        lowered, exped = a.sem("lowered"), a.sem("exped")
        block = ctx.enter_context(nc.Block())

        @block.sync
        def _(sp):
            for n, tile in vecs.items():
                sp.dma_start(tile[:], w[n].partition_broadcast(P)).then_inc(loaded, 16)

        @block.scalar
        def _(act):
            act.wait_ge(inverted, 1)
            nc.scalar.activation(rstd[:], mean[:], ACT.Sqrt).then_inc(rooted, 1)
            act.wait_ge(lowered, 1)
            nc.scalar.activation(gate[:], score[:], ACT.Exp).then_inc(exped, 1)

        @block.vector
        def _(v):
            done = [0]

            def step(ins):
                done[0] += 1
                ins.then_inc(stepped, 1)
                v.wait_ge(stepped, done[0])

            def per_node(tile, n):
                return tile[:].unsqueeze(2).to_broadcast([P, NT, n])

            def per_feature(name):
                return vecs[name][:].unsqueeze(1).to_broadcast([P, NT, HEADW])
            nodes = slice(0, NT)
            v.wait_ge(loaded, 16 * len(vecs))
            step(nc.vector.tensor_scalar(weight[:], acc[:, nodes, HEADW:], 1e-16, None, ALU.add))
            step(nc.vector.reciprocal(weight[:], weight[:]))
            for h in range(H):
                part = slice(h * E3X, (h + 1) * E3X)
                step(nc.vector.tensor_tensor(agg[:, :, part], acc[:, nodes, part],
                                             weight[:, :, h:h + 1].to_broadcast([P, NT, E3X]), ALU.mult))
            step(nc.vector.tensor_tensor(agg[:], agg[:], per_feature("b_gat"), ALU.add))
            step(nc.vector.tensor_reduce(mean[:], agg[:], AX.X, ALU.add))
            step(nc.vector.tensor_scalar(mean[:], mean[:], 1.0 / HEADW, None, ALU.mult))
            step(nc.vector.tensor_tensor(agg[:], agg[:], per_node(mean, HEADW), ALU.subtract))
            step(nc.vector.tensor_tensor(sq[:], agg[:], agg[:], ALU.mult))
            step(nc.vector.tensor_reduce(mean[:], sq[:], AX.X, ALU.add))
            step(nc.vector.tensor_scalar(mean[:], mean[:], 1.0 / HEADW, LN_EPS, ALU.mult, ALU.add))
            nc.vector.reciprocal(mean[:], mean[:]).then_inc(inverted, 1)
            v.wait_ge(rooted, 1)
            step(nc.vector.tensor_tensor(agg[:], agg[:], per_node(rstd, HEADW), ALU.mult))
            step(nc.vector.tensor_tensor(agg[:], agg[:], per_feature("ln_gamma"), ALU.mult))
            step(nc.vector.tensor_tensor(agg[:], agg[:], per_feature("ln_beta"), ALU.add))
            step(nc.vector.tensor_reduce(score[:], agg[:].rearrange("p t (h e) -> p t e h", e=E3X), AX.X, ALU.add))
            step(nc.vector.tensor_scalar(score[:], score[:], 1.0 / H, None, ALU.mult))
            step(nc.vector.memset(rank[:], 0.0))
            for e in range(E3X):
                for f in range(E3X):
                    if f != e:
                        step(nc.vector.tensor_tensor(over[:], score[:, :, f], score[:, :, e],
                                                     ALU.is_ge if f < e else ALU.is_gt))
                        step(nc.vector.tensor_tensor(rank[:, :, e], rank[:, :, e], over[:], ALU.add))
            step(nc.vector.tensor_scalar(rank[:], rank[:], 2.0, None, ALU.is_lt))
            step(nc.vector.tensor_reduce(best[:], score[:], AX.X, ALU.max))
            nc.vector.tensor_tensor(score[:], score[:], per_node(best, E3X), ALU.subtract).then_inc(lowered, 1)
            v.wait_ge(exped, 1)
            step(nc.vector.tensor_tensor(gate[:], gate[:], rank[:], ALU.mult))
            step(nc.vector.tensor_reduce(best[:], gate[:], AX.X, ALU.add))
            step(nc.vector.reciprocal(best[:], best[:]))
            nc.vector.tensor_tensor(gate[:], gate[:], per_node(best, E3X), ALU.mult)


def experts(nc, c, x, w, gate, out):
    E = E3X
    HID = 2 * D
    FC = HID // P
    with ExitStack() as ctx:
        a = Alloc(nc, ctx, "experts")
        norm = Normed(Alloc(nc, ctx, "experts_n"))
        w1 = a.sb("w1", [P, E, KC, HID])
        w2 = a.sb("w2", [P, E, FC, D])
        b1 = a.sb("b1", [P, E, FC])
        b2 = a.sb("b2", [E, D])
        share = a.sb("share", [P, GROUP, E])
        shareT = a.sb("shareT", [E, GW])
        hidden = a.sb("hidden", [P, 2, FC, GW])
        p_r = a.ps("r", [P, 512])
        p_1 = [a.ps(f"p1{i}", [P, 512]) for i in range(3)]
        p_o = [a.ps(f"po{i}", [P, 512]) for i in range(2)]
        loaded, shared = a.sem("loaded"), a.sem("shared")
        share_turned, share_copied = a.sem("share_turned"), a.sem("share_copied")
        made, activated, down, added, stored = (a.sem(n) for n in ("made", "activated", "down", "added", "stored"))
        loads = [(b2[:], w["b2"])]
        for e in range(E):
            loads += [(w1[:, e], chunked(w["W1"][e])), (w2[:, e], chunked(w["W2"][e])),
                      (b1[:, e, :], w["b1"][e].rearrange("(m p) -> p m", p=P))]
        PER = 2 * FC * E
        OUT = (E + 1) * GROUP
        block = ctx.enter_context(nc.Block())

        @block.sync
        def _(sp):
            for to, from_ in loads:
                sp.dma_start(to, from_, allow_slow_non_contiguous=True).then_inc(loaded, 16)
            for g in range(GROUPS):
                sp.wait_ge(added, g * OUT + OUT)
                full = min(GROUP, NT - 1 - g * GROUP)
                sp.dma_start(out[g * GW:g * GW + full * P, :].rearrange("(t p) d -> p t d", p=P),
                             x[:, g * GROUP:g * GROUP + full, :]).then_inc(stored, 16)
            sp.dma_start(out[(NT - 1) * P:N, :], x[0:LAST, NT - 1, :]).then_inc(stored, 16)
            sp.wait_ge(stored, 16 * (GROUPS + 1))

        @block.tensor
        def _(pe):
            pe.wait_ge(loaded, 16 * len(loads))

            def group(g, u, r):
                norm.turn(nc, pe, g, c["ident"])
                pe.wait_ge(shared, g + 1)
                for b, (k0, n) in enumerate(((0, 4), (4, GROUP - 4))):
                    wait(pe, share_copied, g * 2 + b)
                    for t in range(n):
                        mm = nc.tensor.transpose(p_r[0:E, t * P:t * P + P], share[:, k0 + t, :], c["ident"][:])
                    mm.then_inc(share_turned, 1)
                pe.wait_ge(norm.copied, g * len(norm.BATCHES) + len(norm.BATCHES))
                i, o = 0, 0

                def output(lhsTs, rhss):
                    nonlocal o
                    for t in range(GROUP):
                        wait(pe, added, g * OUT + (o - 1))
                        for k, rhs in enumerate(rhss):
                            mm = nc.tensor.matmul(p_o[o % 2][:, 0:D], lhsTs[k][:, t * P:t * P + P], rhs,
                                                  start=(k == 0), stop=(k == len(rhss) - 1))
                        mm.then_inc(down, 1)
                        o += 1

                def expert_output(e):
                    pe.wait_ge(activated, g * PER + (e + 1) * 2 * FC)
                    output([hidden[:, e % 2, k, :] for k in range(FC)], [w2[:, e, k, :] for k in range(FC)])
                for e in range(E):
                    for m in range(FC):
                        for h in range(2):
                            wait(pe, activated, g * PER + (i - 2))
                            for k in range(KC):
                                mm = nc.tensor.matmul(p_1[i % 3][:, 0:HALF], w1[:, e, k, m * P:m * P + P],
                                                      norm.xnT[:, k, h * HALF:(h + 1) * HALF],
                                                      start=(k == 0), stop=(k == KC - 1))
                            mm.then_inc(made, 1)
                            i += 1
                    if e == 0:
                        pe.wait_ge(share_copied, g * 2 + 2)
                        output([shareT], [b2[:]])
                    else:
                        expert_output(e - 1)
                expert_output(E - 1)
            groups(pe, [(0, group)])

        @block.scalar
        def _(act):
            act.wait_ge(loaded, 16 * len(loads))

            def group(g, u, r):
                norm.on_scalar(nc, act, g)
                norm.copy(nc, act, g)
                for b, (k0, n) in enumerate(((0, 4), (4, GROUP - 4))):
                    act.wait_ge(share_turned, g * 2 + b + 1)
                    wait(act, down, g * OUT)
                    nc.scalar.activation(shareT[:, k0 * P:(k0 + n) * P], p_r[0:E, 0:n * P],
                                         ACT.Copy).then_inc(share_copied, 1)
                i = 0
                for e in range(E):
                    wait(act, down, g * OUT + (e * GROUP if e >= 2 else 0))
                    for m in range(FC):
                        for h in range(2):
                            act.wait_ge(made, g * PER + i + 1)
                            nc.scalar.activation(hidden[:, e % 2, m, h * HALF:(h + 1) * HALF], p_1[i % 3][:, 0:HALF],
                                                 ACT.Gelu, bias=b1[:, e, m:m + 1]).then_inc(activated, 1)
                            i += 1
            groups(act, [(0, group)])

        @block.vector
        def _(v):
            def group(g, u, r):
                wait(v, added, g * OUT)
                nc.vector.tensor_scalar(share[:], gate[:, bass.ds(g * GROUP, GROUP), :], 1.0, None,
                                        ALU.mult).then_inc(shared, 1)
                norm.on_vector(nc, v, g, lambda k: tile_of(x, g * GROUP + k))
                v.wait_ge(shared, g + 1)
                v.wait_ge(norm.turned, g * len(norm.BATCHES) + len(norm.BATCHES))
                v.wait_ge(norm.normed, g * norm.steps + norm.steps)
                for o in range(OUT):
                    e, t = o // GROUP - 1, o % GROUP
                    v.wait_ge(down, g * OUT + o + 1)
                    if o >= GROUP:
                        v.wait_ge(added, g * OUT + (o + 1 - GROUP))
                    rows_of_x = tile_of(x, g * GROUP + t)
                    if e < 0:
                        nc.vector.tensor_tensor(rows_of_x, p_o[o % 2][:, 0:D], rows_of_x, ALU.add).then_inc(added, 1)
                    else:
                        nc.vector.scalar_tensor_tensor(rows_of_x, p_o[o % 2][:, 0:D], share[:, t, e:e + 1], rows_of_x,
                                                       ALU.mult, ALU.add).then_inc(added, 1)
            groups(v, [(0, group)])

def program(nc, t, out):
    def dram(name, shape, dt=F32):
        return nc.dram_tensor(name, shape, dt, kind="Internal").ap()

    def weights(prefix):
        return {n[len(prefix):]: ap for n, ap in t.items() if n.startswith(prefix)}

    kv_dram = dram("kv_rows", (NP, KVW))
    skip_dram = dram("skip_rows", (NP, D))
    sums_dram = dram("attention_sums", (P, NT, H * VW))
    by_src = dram("attributes_by_src", (P * BY_SRC.stride, ATTR_W))
    by_gat = dram("gat_edges_by_dst", (P * GAT.stride, 2), I32)
    hi3_dram = dram("gat_node_tiles", (1, GAT.tiles + 2 * UNROLL), I32)
    conv_dram = dram("conv_rows", (NP, D))
    by_dst = dram("edges_by_dst", (P * BY_DST.stride, 2), I32)
    table_dram = dram("router_rows", (NP, ROWW))
    with ExitStack() as ctx:
        keep = Alloc(nc, ctx, "keep")
        c = constants(nc, keep)
        hi1 = keep.sb("hi1", [1, BY_DST.tiles + 2 * UNROLL], I32)
        x = keep.sb("x", [P, NT, D])
        load_x(nc, x, t["x"])
        src1 = keep.sb("src1", [P, BY_DST.tiles], I32)
        lo1 = keep.sb("lo1", [P, BY_DST.tiles])
        no_edges = keep.sb("no_edges", [P, NB])
        with ExitStack() as actx:
            qT = Alloc(nc, actx, "attend").sb("qT", [P, KC, NP])
            with ExitStack() as sctx:
                b = Alloc(nc, sctx, "by_dst")
                slot = b.sb("slot", [BY_DST.parts, BY_DST.cols], I32)
                pay = b.sb("pay", [BY_DST.parts, BY_DST.cols, 2], I32)
                with ExitStack() as fctx:
                    empty = empty_slots(nc, fctx, BY_DST)
                    place_edges(nc, c, BY_DST, t["dst"], hi1, slot, None, t["src"], pay,
                                fill=[(by_dst.rearrange("(p t) w -> p t w", p=P), empty[:])])
                project(nc, c, x, weights("L0_gnn_"), qT, skip_dram, kv_dram,
                        Scatter(b, BY_DST, slot, by_dst, 2, I32), pay)
            a = Alloc(nc, actx, "sums")
            acc = a.sb("acc", [P, NB, H * VW])
            top_score = a.sb("top_score", [P, NB, H])
            load_edges(nc, BY_DST, by_dst, src1, lo1, [(acc, 0.0), (top_score, -1e20), (no_edges, 0.0)])
            attend(nc, c, src1, lo1, hi1, qT, kv_dram, acc, top_score, no_edges, sums_dram)
        hi2 = keep.sb("hi2", [1, BY_SRC.tiles + 2 * UNROLL], I32)
        with ExitStack() as sctx:
            b = Alloc(nc, sctx, "by_src")
            slot = b.sb("slot", [BY_SRC.parts, BY_SRC.cols], I32)
            lo = b.sb("lo", [BY_SRC.parts, BY_SRC.cols])
            with ExitStack() as fctx:
                n = BY_SRC.stride // 26
                empty = empty_attributes(nc, fctx, BY_SRC, n)
                room = by_src.rearrange("(p t) w -> p t w", p=P)
                place_edges(nc, c, BY_SRC, t["src"], hi2, slot, lo,
                            fill=[(room[:, i * n:(i + 1) * n, :], empty[:]) for i in range(26)])
            scatter = Scatter(b, BY_SRC, slot, by_src, ATTR_W, F32)

            def sort_attributes(pool):
                scatter.on_gpsimd(nc, pool, EDGE_F, lo, True)
                scatter.drain(pool)
            feed_forward(nc, c, x, weights("L0_gnn_"), sums_dram, skip_dram, sort_attributes,
                         lambda sp: load_attributes(nc, sp, scatter, t["edge_attr_64"]))
        with ExitStack() as sctx:
            b = Alloc(nc, sctx, "by_gat")
            hi3 = b.sb("hi3", [1, GAT.tiles + 2 * UNROLL], I32)
            slot = b.sb("slot", [GAT.parts, GAT.cols], I32)
            pay = b.sb("pay", [GAT.parts, GAT.cols, 2], I32)
            with ExitStack() as fctx:
                empty = empty_slots(nc, fctx, GAT)
                place_edges(nc, c, GAT, t["L1_ffn_edge_index"][1], hi3, slot, None, t["L1_ffn_edge_index"][0], pay,
                            fill=[(by_gat.rearrange("(p t) w -> p t w", p=P), empty[:])])
            copy(nc, hi3_dram, hi3[:], "hi3_out")
            scatter3 = Scatter(b, GAT, slot, by_gat, 2, I32)

            def sort_gat(pool):
                scatter3.on_gpsimd(nc, pool, 0, pay, False)
                scatter3.drain(pool)
            mixture(nc, c, x, weights("L0_ffn_"), sort_gat)
        with ExitStack() as cctx:
            a = Alloc(nc, cctx, "conv")
            dinv = a.sb("dinv", [P, NT])
            sums = a.sb("sums", [P, NT, D])
            rest = a.sb("rest", [P, NT, D])
            with ExitStack() as pctx:
                per_node = Alloc(nc, pctx, "conv").sb("per_node", [P, NT, EDGE_F])
                clear(nc, [(per_node, 0.0)])
                segment_sum(nc, c, BY_SRC, hi2, EDGE_F, per_node, by_src)
                convolve_dense(nc, c, x, weights("L1_gnn_"), per_node, no_edges, dinv, sums, rest, conv_dram)
            segment_sum(nc, c, BY_DST, hi1, D, sums, conv_dram, src1, lo1)
            convolve_end(nc, x, dinv, sums, rest)
        w = weights("L1_ffn_")
        gate = keep.sb("gate", [P, NT, E3X])
        with ExitStack() as gctx:
            a = Alloc(nc, gctx, "gat")
            rows = a.sb("rows", [P, NT, KEPT])
            target = a.sb("target", [P, NB, H])
            top = a.sb("top", [P, NB, H])
            bounds = a.sb("bounds", [P, NB, 2 * H])
            acc = a.sb("acc", [P, NB, KEPT])
            source = a.sb("source", [P, GAT.tiles], I32)
            lo = a.sb("lo", [P, GAT.tiles])
            hi_row = a.sb("hi_row", [1, GAT.tiles + 2 * UNROLL], I32)
            router_rows(nc, c, x, w, rows, target, top, table_dram)
            load_edges(nc, GAT, by_gat, source, lo)
            copy(nc, hi_row[:], hi3_dram, "hi3_in")
            edge = a.sb("edge", [P, GAT.tiles, KEPT])
            edge_rows(nc, c, source, lo, hi_row, table_dram, edge, top)
            loops_to_self(nc, rows, target, top, bounds, acc)
            edge_sums(nc, c, lo, hi_row, edge, bounds, acc)
            gates(nc, w, acc, gate)
        experts(nc, c, x, w, gate, out)

def empty_slots(nc, ctx, st):
    a = Alloc(nc, ctx, f"empty_{st.name}")
    empty = a.sb("slots", [P, st.stride, 2], I32)
    with ExitStack() as bctx:
        zeroed = Alloc(nc, bctx, f"empty_{st.name}_now").sem("zeroed")
        block = bctx.enter_context(nc.Block())

        @block.vector
        def _(v):
            nc.vector.memset(empty[:], 0).then_inc(zeroed, 1)
            v.wait_ge(zeroed, 1)
            nc.vector.memset(empty[:, :, 1], PAD_LO)
    return empty


def copy(nc, to, from_, name):
    with ExitStack() as ctx:
        copied = Alloc(nc, ctx, name).sem("copied")
        block = ctx.enter_context(nc.Block())

        @block.sync
        def _(sp):
            sp.dma_start(to, from_).then_inc(copied, 16)
            sp.wait_ge(copied, 16)


def clear(nc, what):
    with nc.Block() as block:
        @block.vector
        def _(v):
            for tile, value in what:
                nc.vector.memset(tile[:], value)


def kernel(**inputs):
    import numpy as np
    import concourse.bacc as bacc
    from concourse.bass_utils import run_bass_kernel_spmd

    nc = bacc.Bacc("TRN2", target_bir_lowering=False, num_devices=1)
    arrays = {f"{name}_dram": np.ascontiguousarray(a) for name, a in inputs.items()}
    tensors = {name: nc.dram_tensor(f"{name}_dram", a.shape, mybir.dt.from_np(a.dtype), kind="ExternalInput").ap()
               for name, a in ((n, arrays[f"{n}_dram"]) for n in inputs)}
    out = nc.dram_tensor("out_dram", (N, D), F32, kind="ExternalOutput").ap()
    program(nc, tensors, out)
    result = run_bass_kernel_spmd(nc, [arrays], core_ids=[0])
    return result.results[0]["out_dram"]
```

```python
from contextlib import ExitStack

import concourse.bass as bass
from concourse import mybir

F32 = mybir.dt.float32
BF16 = mybir.dt.bfloat16
I32 = mybir.dt.int32
U16 = mybir.dt.uint16
ALU = mybir.AluOpType
ACT = mybir.ActivationFunctionType
AX = mybir.AxisListType
DVE = mybir.EngineType.DVE

P = 128
N = 6250
D = 256
NT = -(-N // P)
NP = NT * P
LAST = N - (NT - 1) * P
KC = D // P
NB = NT + 1
H = 4
DH = D // H
LN_EPS = 1e-5
PAD_LO = 999
UNROLL = 8


class Stream:

    def __init__(self, name, edges, parts, buckets, tiles, room=0):
        self.name = name
        self.edges = edges
        self.buckets = buckets
        self.parts = parts
        self.cols = edges // parts
        self.tiles = tiles
        self.stride = max(room, -(-(edges // P + buckets) // UNROLL) * UNROLL)
        assert parts * self.cols == edges and tiles <= self.stride


E1 = 100000
E3 = 131072
BY_DST = Stream("dst", E1, 125, NT, 832)
BY_SRC = Stream("src", E1, 125, NT, 840, room=840)
GAT = Stream("gat", E3, 128, NB, 1072)
for s in (BY_DST, BY_SRC):
    assert s.tiles >= (s.edges + NT * (P - 1)) // P
assert GAT.tiles >= (E3 + NT * (P - 1)) // P


class Alloc:

    def __init__(self, nc, ctx, stage):
        self.nc, self.ctx, self.stage = nc, ctx, stage
        self.own = []
        ctx.callback(self.give_back)

    def give_back(self):
        if self.own:
            self.nc.clear_and_free_semaphores(self.own)
            self.nc.all_engine_barrier()

    def sb(self, name, shape, dt=F32):
        return self.ctx.enter_context(self.nc.sbuf_tensor(f"{self.stage}_{name}", shape, dt))

    def ps(self, name, shape, dt=F32):
        return self.ctx.enter_context(self.nc.psum_tensor(f"{self.stage}_{name}", shape, dt))

    def sem(self, name):
        self.own.append(self.nc.alloc_semaphore(f"{self.stage}_{name}"))
        return self.own[-1]

    def sems(self, name, n):
        return [self.sem(f"{name}{i}") for i in range(n)]


def wait(eng, sem, value):
    if not isinstance(value, int) or value > 0:
        eng.wait_ge(sem, value)


def wait_alone(eng, sem, value, passed):
    wait(eng, sem, value)
    if not isinstance(value, int):
        eng.sem_inc(passed, 1)


def pipelined(eng, tiles, unroll, stages, top=None, peel=1):
    assert tiles % unroll == 0
    last = max(lag for lag, _ in stages)
    rounds = tiles // unroll
    assert last <= unroll * peel and peel <= rounds

    def steps(i, u):
        for lag, stage in stages:
            if not isinstance(i, int):
                back = -((u - lag) // unroll)
                stage(i * unroll + (u - lag), (u - lag) % unroll, i - back if back else i)
            elif 0 <= i * unroll + u - lag < tiles:
                t = i * unroll + u - lag
                stage(t, t % unroll, t // unroll)
    for i in range(peel):
        if top:
            top(i)
        for u in range(unroll):
            steps(i, u)
    if rounds > peel:
        with eng.Fori(peel, rounds) as i:
            if top:
                top(i)
            for u in range(unroll):
                steps(i, u)
    for k in range(last):
        if k % unroll == 0 and top:
            top(rounds + k // unroll)
        steps(rounds + k // unroll, k % unroll)


def cols(ap, start, n=1):
    return ap[:, bass.ds(start, n)]

def constants(nc, keep):
    c = {}
    c["ident"] = keep.sb("ident", [P, P])
    c["ident_bf"] = keep.sb("ident_bf", [P, P], BF16)
    c["drop4"] = keep.sb("drop4", [P, H * P], BF16)
    c["ones"] = keep.sb("ones", [P, P])
    c["ones_bf"] = keep.sb("ones_bf", [P, P], BF16)
    c["before"] = keep.sb("before", [P, P])
    c["upto"] = keep.sb("upto", [P, P])
    c["iota"] = keep.sb("iota", [P, P])
    c["iota_bf"] = keep.sb("iota_bf", [P, P], BF16)
    with ExitStack() as ctx:
        a = Alloc(nc, ctx, "const")
        filled, made = a.sem("filled"), a.sem("made")
        block = ctx.enter_context(nc.Block())

        @block.gpsimd
        def _(pool):
            for name, value in (("ident", 0.0), ("ident_bf", 0.0), ("drop4", 0.0), ("ones", 1.0), ("ones_bf", 1.0),
                                ("before", 1.0), ("upto", 1.0)):
                nc.gpsimd.memset(c[name][:], value).then_inc(filled, 1)
            pool.wait_ge(filled, 7)
            for name, copies, fill in (("ident", 1, 1.0), ("ident_bf", 1, 1.0), ("drop4", H, 1e30)):
                m = c[name][:].rearrange("p (h n) -> p h n", h=copies)
                nc.gpsimd.affine_select(m, m, [[0, copies], [-1, P]], ALU.not_equal, fill, base=0,
                                        channel_multiplier=1).then_inc(made, 1)
            for name, compare in (("before", ALU.is_gt), ("upto", ALU.is_ge)):
                nc.gpsimd.affine_select(c[name][:], c[name][:], [[1, P]], compare, 0.0, base=0,
                                        channel_multiplier=-1).then_inc(made, 1)
            for name in ("iota", "iota_bf"):
                nc.gpsimd.iota(c[name][:], pattern=[[1, P]], base=0, channel_multiplier=0,
                               allow_small_or_imprecise_dtypes=True).then_inc(made, 1)
            pool.wait_ge(made, 7)
    return c


class PlaceScratch:

    def __init__(self, nc, a, edges_wide, tiles):
        self.nc, C = nc, edges_wide
        self.key, self.lo_i = a.sb("key", [P, C], I32), a.sb("lo_i", [P, C], I32)
        self.hi = a.sb("hi", [P, C], BF16)
        self.mask = a.sb("mask", [P, C], U16)
        self.rank, self.pos = a.sb("rank", [P, max(C, tiles)]), a.sb("pos", [P, C])
        self.tile_no = a.sb("tile_no", [NB, tiles])
        self.small = a.ps("small", [P, 512])
        self.listing = a.ps("listing", [P, 512])
        self.numbered = a.sem("numbered")

    def on_gpsimd(self, pool):
        self.nc.gpsimd.iota(self.tile_no[:], pattern=[[1, self.tile_no.shape[1]]], base=0, channel_multiplier=0,
                            allow_small_or_imprecise_dtypes=True).then_inc(self.numbered, 1)


class Place:

    def __init__(self, nc, c, a, w, st, key_dram, hi_row, slot_row, lo, src_dram=None, payload=None,
                 earlier=None):
        self.nc, self.c, self.w, self.st = nc, c, w, st
        self.key_dram, self.hi_row, self.slot_row, self.lo = key_dram, hi_row, slot_row, lo
        self.src_dram, self.payload, self.earlier = src_dram, payload, earlier
        R, C, T = st.parts, st.cols, st.tiles
        self.key, self.lo_i, self.hi, self.mask, self.rank, self.pos = (
            t[0:R, 0:C] for t in (w.key, w.lo_i, w.hi, w.mask, w.rank, w.pos))
        self.tile_no, self.ended = w.tile_no[:, 0:T], w.rank[0:NB, 0:T]
        self.cnt, self.tot, self.n_tiles, self.end, self.first, self.start = (
            a.sb(n, [P, NB]) for n in ("cnt", "tot", "n_tiles", "end", "first", "start"))
        self.tot_i = a.sb("tot_i", [P, NB], I32)
        self.ctot, self.ctiles, self.cend = (a.sb(n, [NB, 2]) for n in ("ctot", "ctiles", "cend"))
        self.ctot_i = a.sb("ctot_i", [NB, 2], I32)
        self.p_off, self.p_tot = w.small[:, 0:NB], w.small[:, NB:2 * NB]
        self.p_col, self.p_end = w.small[0:NB, 2 * NB:2 * NB + 2], w.listing[0:NB, 0:2]
        self.chunks = [(k, min(512, T - k)) for k in range(0, T, 512)]
        (self.loaded, self.counted, self.tiled, self.summed, self.ends, self.listed,
         self.listing_read, self.marked, self.v_done, self.loops, self.passed, self.placed) = (a.sem(n) for n in (
             "loaded", "counted", "tiled", "summed", "ends", "listed", "listing_read",
             "marked", "v_done", "loops", "passed", "placed"))

    def on_sync(self, sp):
        R = self.st.parts
        if self.earlier:
            sp.wait_ge(self.earlier.placed, 1)
        sp.dma_start(self.key, self.key_dram.rearrange("(p c) -> p c", p=R)).then_inc(self.loaded, 16)
        if self.src_dram is not None:
            sp.dma_start(self.slot_row[:], self.src_dram.rearrange("(p c) -> p c", p=R)).then_inc(self.loaded, 16)

    def on_tensor(self, pe):
        nc, c = self.nc, self.c
        pe.wait_ge(self.counted, 1)
        nc.tensor.matmul(self.p_off, c["before"][:], self.cnt[:], start=True, stop=True)
        nc.tensor.matmul(self.p_tot, c["ones"][:], self.cnt[:], start=True, stop=True)
        nc.tensor.matmul(self.p_col, self.cnt[:], c["ones"][:, 0:2], start=True, stop=True).then_inc(self.summed, 1)
        pe.wait_ge(self.tiled, 1)
        nc.tensor.matmul(self.p_end, c["upto"][0:NB, 0:NB], self.ctiles[:], start=True, stop=True).then_inc(self.ends, 1)
        pe.wait_ge(self.marked, 1)
        for i, (k, n) in enumerate(self.chunks):
            wait(pe, self.listing_read, i)
            nc.tensor.matmul(self.w.listing[0:1, 0:n], c["ones"][0:NB, 0:1], self.ended[:, k:k + n],
                             start=True, stop=True).then_inc(self.listed, 1)

    def on_vector(self, v):
        nc, c, st = self.nc, self.c, self.st
        R = st.parts
        key, lo_i, pos, hi, mask = self.key, self.lo_i, self.pos, self.hi, self.mask
        tot_i, ctot_i, n_tiles, start = self.tot_i, self.ctot_i, self.n_tiles, self.start
        done = [0]

        def step(ins):
            done[0] += 1
            ins.then_inc(self.v_done, 1)
            v.wait_ge(self.v_done, done[0])

        step(nc.vector.memset(self.cnt[:], 0.0))
        step(nc.vector.memset(pos, 0.0))
        step(nc.vector.memset(self.hi_row[:], 0))
        v.wait_ge(self.loaded, 16 if self.src_dram is None else 32)
        step(nc.vector.tensor_scalar(lo_i, key, 7, None, ALU.arith_shift_right))
        step(nc.vector.tensor_scalar(hi, lo_i, float(NT), None, ALU.min))
        step(nc.vector.tensor_scalar(lo_i, key, P - 1, None, ALU.bitwise_and))
        if self.lo is not None:
            step(nc.vector.tensor_copy(self.lo[:], lo_i))
        if self.payload is not None:
            step(nc.vector.tensor_scalar(self.payload[:, :, 0], self.slot_row[:], float(N - 1), None, ALU.min))
            step(nc.vector.tensor_copy(self.payload[:, :, 1], lo_i))
        with v.Fori(0, NB) as b:
            nc.vector.tensor_scalar(mask, hi, cols(c["iota"][0:R, :], b), 0.0, ALU.is_equal, ALU.add,
                                    accum_out=cols(self.cnt[0:R, :], b)).then_inc(self.loops, 1)
            v.wait_ge(self.loops, b + 1)
        nc.vector.memset(self.ctot[:], 0.0).then_inc(self.counted, 1)
        v.wait_ge(self.summed, 1)
        step(nc.vector.tensor_copy(self.ctot[:], self.p_col))
        step(nc.vector.tensor_scalar(ctot_i[:], self.ctot[:], float(P - 1), None, ALU.add))
        step(nc.vector.tensor_scalar(ctot_i[:], ctot_i[:], 7, None, ALU.arith_shift_right))
        nc.vector.tensor_copy(self.ctiles[:], ctot_i[:]).then_inc(self.tiled, 1)
        step(nc.vector.tensor_scalar(tot_i[:], self.p_tot, float(P - 1), None, ALU.add))
        step(nc.vector.tensor_scalar(tot_i[:], tot_i[:], 7, None, ALU.arith_shift_right))
        step(nc.vector.tensor_copy(n_tiles[:], tot_i[:]))
        step(nc.vector.tensor_tensor_scan(self.end[:], c["ones"][:, 0:NB], n_tiles[:], 0.0, ALU.mult, ALU.add))
        step(nc.vector.tensor_tensor(self.first[:], self.end[:], n_tiles[:], ALU.subtract))
        step(nc.vector.scalar_tensor_tensor(start[:], self.first[:], float(P), self.p_off, ALU.mult, ALU.add))
        step(nc.vector.tensor_scalar(start[:], start[:], -1.0, None, ALU.add))
        v.wait_ge(self.ends, 1)
        v.wait_ge(self.w.numbered, 1)
        step(nc.vector.tensor_copy(self.cend[:], self.p_end))
        nc.vector.tensor_scalar(self.ended, self.tile_no, self.cend[:, 0:1], None, ALU.is_ge).then_inc(self.marked, 1)
        for i, (k, n) in enumerate(self.chunks):
            v.wait_ge(self.listed, i + 1)
            nc.vector.tensor_scalar(self.hi_row[0:1, UNROLL + k:UNROLL + k + n], self.w.listing[0:1, 0:n],
                                    float(st.buckets - 1), None, ALU.min).then_inc(self.listing_read, 1)
        with v.Fori(0, NB) as b:
            nc.vector.tensor_scalar(mask, hi, cols(c["iota"][0:R, :], b), None,
                                    ALU.is_equal).then_inc(self.loops, 1)
            v.wait_ge(self.loops, b * 3 + (NB + 1))
            nc.vector.tensor_tensor_scan(self.rank, c["ones_bf"][0:R, 0:1].to_broadcast([R, st.cols]), mask, cols(start[0:R, :], b), ALU.mult,
                                         ALU.add).then_inc(self.loops, 1)
            wait_alone(v, self.loops, b * 3 + (NB + 2), self.passed)
            nc.vector.copy_predicated(pos, mask, self.rank).then_inc(self.loops, 1)
            v.wait_ge(self.loops, b * 3 + (NB + 3))
        step(nc.vector.tensor_copy(key, pos))
        step(nc.vector.tensor_scalar(lo_i, key, P - 1, None, ALU.bitwise_and))
        step(nc.vector.tensor_scalar(key, key, 7, None, ALU.arith_shift_right))
        v.wait_ge(self.listing_read, len(self.chunks))
        nc.vector.scalar_tensor_tensor(self.slot_row[:], lo_i, float(st.stride), key, ALU.mult,
                                       ALU.add).then_inc(self.placed, 1)
        v.wait_ge(self.placed, 1)


def place_edges(nc, c, st, key_dram, hi_row, slot_row, lo, src_dram, payload, fill, x, x_dram):
    with ExitStack() as ctx:
        a = Alloc(nc, ctx, f"place_{st.name}")
        scratch = PlaceScratch(nc, a, st.cols, st.tiles)
        place = Place(nc, c, a, scratch, st, key_dram, hi_row, slot_row, lo, src_dram,
                      payload)
        filled, cleared, x_loaded = a.sem("filled"), a.sem("cleared"), a.sem("x_loaded")
        block = ctx.enter_context(nc.Block())

        @block.sync
        def _(sp):
            place.on_sync(sp)
            full = (NT - 1) * P
            sp.dma_start(x[:, 0:NT - 1, :], x_dram[0:full, :].rearrange("(t p) d -> p t d", p=P)).then_inc(x_loaded, 16)
            sp.wait_ge(cleared, 1)
            sp.dma_start(x[0:LAST, NT - 1, :], x_dram[full:N, :]).then_inc(x_loaded, 16)
            for to, from_ in fill:
                sp.dma_start(to, from_).then_inc(filled, 16)
            sp.wait_ge(x_loaded, 32)
            sp.wait_ge(filled, 16 * len(fill))

        @block.gpsimd
        def _(pool):
            scratch.on_gpsimd(pool)

        @block.tensor
        def _(pe):
            place.on_tensor(pe)

        @block.vector
        def _(v):
            nc.vector.memset(x[:, NT - 1, :], 0.0).then_inc(cleared, 1)
            place.on_vector(v)


SCATTER = 16


class Scatter:

    def __init__(self, nc, a, st, slot_row, out, width, dt, column, source, loads, wide=SCATTER):
        self.nc, self.st, self.slot_row, self.out, self.width, self.wide = nc, st, slot_row, out, width, wide
        self.column, self.source, self.loads = column, source, loads
        self.rows = a.sb(f"{st.name}_rows", [st.parts, 2, wide], I32)
        self.data = a.sb(f"{st.name}_data", [st.parts, 2, wide * width], dt)
        self.copied = a.sem(f"{st.name}_copied")
        self.loaded = a.sems(f"{st.name}_loaded", 2)
        self.landed = a.sems(f"{st.name}_landed", 2)
        self.passed = a.sem(f"{st.name}_passed")
        self.chunks = st.cols // wide

    def chunk(self, pool, t, u, r):
        nc, wide = self.nc, self.wide
        wait(pool, self.landed[u], r * (16 * wide))
        nc.gpsimd.tensor_copy(self.rows[:, u, :], cols(self.slot_row, t * wide, wide)).then_inc(self.copied, 1)
        data = self.data[:, u, :].rearrange("p (c w) -> p c w", w=self.width)
        to = self.data[:, u, self.column::self.width] if self.column else data
        nc.gpsimd.tensor_copy(to, cols(self.source, t * wide, wide)).then_inc(self.copied, 1)
        wait_alone(pool, self.copied, t * 2 + 2, self.passed)
        if self.loads:
            wait_alone(pool, self.loaded[u], r * 16 + 16, self.passed)
        for c in range(wide):
            nc.gpsimd.indirect_dma_start(self.out, bass.IndirectOffsetOnAxis(self.rows[:, u, c:c + 1], 0),
                                         data[:, c, :], None).then_inc(self.landed[u], 16)

    def on_gpsimd(self, pool):
        pipelined(pool, self.chunks, 2, [(0, lambda t, u, r: self.chunk(pool, t, u, r))])
        self.drain(pool)

    def drain(self, eng):
        for u in range(2):
            eng.wait_ge(self.landed[u], self.chunks // 2 * 16 * self.wide)


def gat_payload(nc, st, src_dram, key_dram, payload):
    with ExitStack() as ctx:
        a = Alloc(nc, ctx, "payload")
        ends = a.sb("ends", [st.parts, 2, st.cols], I32)
        loaded = a.sem("loaded")
        block = ctx.enter_context(nc.Block())

        @block.sync
        def _(sp):
            for i, rows in enumerate((src_dram, key_dram)):
                sp.dma_start(ends[:, i, :], rows.rearrange("(p c) -> p c", p=st.parts)).then_inc(loaded, 16)

        @block.vector
        def _(v):
            v.wait_ge(loaded, 32)
            nc.vector.tensor_scalar(payload[:, :, 0], ends[:, 0, :], float(N - 1), None, ALU.min)
            nc.vector.tensor_scalar(payload[:, :, 1], ends[:, 1, :], P - 1, None, ALU.bitwise_and)

GROUP = 7
GROUPS = NT // GROUP
GW = GROUP * P
HALF = GW // 2
assert GROUPS * GROUP == NT and HALF <= 512
VW = DH + 1
KVW = D + H * VW


class Normed:

    def __init__(self, a, gamma=None, beta=None, turned=True):
        self.gamma, self.beta = gamma, beta
        self.steps = GROUP * (1 if gamma is None else 3)
        self.stats = a.sb("stats", [P, GROUP, 6])
        self.mv = a.sb("mv", [P, GROUP, 2])
        self.var = a.sb("var", [P, GROUP])
        self.inv = a.sb("inv", [P, GROUP])
        self.rstd = a.sb("rstd", [P, GROUP])
        self.xn = a.sb("xn", [P, GROUP, D])
        if turned:
            self.xnT = a.sb("xnT", [P, KC, GW])
            self.banks = [a.ps(f"turn{b}", [P, 512]) for b in range(2)]
        self.passed = a.sem("passed")
        names = ("counted", "averaged", "added", "inverted", "rooted", "normed", "turned", "copied")
        (self.counted, self.averaged, self.added, self.inverted, self.rooted, self.normed, self.turned,
         self.copied) = (a.sem(n) for n in names)

    BATCHES = [(c, k0, min(4, GROUP - k0)) for c in range(KC) for k0 in range(0, GROUP, 4)]

    def on_vector(self, nc, v, g, x):
        for k in range(GROUP):
            nc.vector.bn_stats(self.stats[:, k, :], x(k)).then_inc(self.counted, 1)
        wait_alone(v, self.counted, g * GROUP + GROUP, self.passed)
        for k in range(GROUP):
            nc.vector.bn_aggr(self.mv[:, k, :], self.stats[:, k, :]).then_inc(self.averaged, 1)
        v.wait_ge(self.averaged, g * GROUP + GROUP)
        nc.vector.tensor_scalar(self.var[:], self.mv[:, :, 1], LN_EPS, None, ALU.add).then_inc(self.added, 1)
        v.wait_ge(self.added, g + 1)
        nc.vector.reciprocal(self.inv[:], self.var[:]).then_inc(self.inverted, 1)
        v.wait_ge(self.rooted, g + 1)
        for k in range(GROUP):
            nc.vector.tensor_scalar(self.xn[:, k, :], x(k), self.mv[:, k, 0:1], self.rstd[:, k:k + 1],
                                    ALU.subtract, ALU.mult).then_inc(self.normed, 1)
        if self.gamma is not None:
            for i, (row, op) in enumerate(((self.gamma, ALU.mult), (self.beta, ALU.add))):
                for k in range(GROUP):
                    v.wait_ge(self.normed, g * self.steps + (i * GROUP + k + 1))
                    nc.vector.tensor_tensor(self.xn[:, k, :], self.xn[:, k, :], row[:], op).then_inc(self.normed, 1)

    def on_scalar(self, nc, act, g):
        act.wait_ge(self.inverted, g + 1)
        nc.scalar.activation(self.rstd[:], self.inv[:], ACT.Sqrt).then_inc(self.rooted, 1)

    def turn(self, nc, pe, g, ident):
        pe.wait_ge(self.normed, g * self.steps + self.steps)
        for b, (c, k0, n) in enumerate(self.BATCHES):
            wait(pe, self.copied, g * len(self.BATCHES) + (b - 1))
            for k in range(n):
                last = nc.tensor.transpose(self.banks[b % 2][:, k * P:k * P + P],
                                           self.xn[:, k0 + k, c * P:c * P + P], ident[:])
            last.then_inc(self.turned, 1)

    def copy(self, nc, act, g):
        for b, (c, k0, n) in enumerate(self.BATCHES):
            act.wait_ge(self.turned, g * len(self.BATCHES) + b + 1)
            nc.scalar.activation(self.xnT[:, c, k0 * P:(k0 + n) * P], self.banks[b % 2][:, 0:n * P],
                                 ACT.Copy).then_inc(self.copied, 1)


def groups(eng, stages):
    pipelined(eng, GROUPS, 1, stages)


def tiled(rows):
    return rows.rearrange("(t p) w -> p t w", p=P)


def tile_of(x, t):
    return x[:, bass.ds(t, 1), :].rearrange("p a d -> p (a d)")


def chunked(w):
    return w.rearrange("(c p) n -> p c n", p=P)


def project(nc, c, x, w, qT, skip_dram, kv_dram, scatter, places):
    with ExitStack() as ctx:
        a = Alloc(nc, ctx, "project")
        norm = Normed(Alloc(nc, ctx, f"{a.stage}_n"))
        wq, wk, wv, ws = (a.sb(n, [P, KC, D]) for n in ("wq", "wk", "wv", "ws"))
        bq = a.sb("bq", [P, KC])
        bk, bv, bs = (a.sb(n, [P, D]) for n in ("bk", "bv", "bs"))
        kv = a.sb("kv", [P, GROUP, KVW])
        p_q = [a.ps(f"q{i}", [P, 512]) for i in range(2)]
        p_kv = a.ps("p_kv", [P, 512])
        p_s = a.ps("p_s", [P, 512])
        loaded, ones = a.sem("loaded"), a.sem("ones")
        q_made, q_read = a.sem("q_made"), a.sem("q_read")
        kvs_made, kv_read, s_read, stored = a.sem("kvs_made"), a.sem("kv_read"), a.sem("s_read"), a.sem("stored")
        loads = [(wq, chunked(w["Wq"])), (wk, chunked(w["Wk"])), (wv, chunked(w["Wv"])), (ws, chunked(w["Wskip"])),
                 (bq, w["bq"].rearrange("(c p) -> p c", p=P)), (bk, w["bk"].partition_broadcast(P)),
                 (bv, w["bv"].partition_broadcast(P)), (bs, w["bskip"].partition_broadcast(P))]
        block = ctx.enter_context(nc.Block())

        @block.sync
        def _(sp):
            for to, from_ in loads:
                sp.dma_start(to[:], from_, allow_slow_non_contiguous=True).then_inc(loaded, 16)
            places[0].on_sync(sp)

            def store(g, u, r):
                sp.wait_ge(kv_read, g * 3 * GROUP + 3 * GROUP)
                sp.dma_start(tiled(kv_dram)[:, bass.ds(g * GROUP, GROUP), :],
                             kv[:]).then_inc(stored, 16)
                sp.wait_ge(s_read, g * GROUP + GROUP)
                sp.dma_start(tiled(skip_dram)[:, bass.ds(g * GROUP, GROUP), :],
                             norm.xn[:]).then_inc(stored, 16)
            groups(sp, [(0, store)])
            sp.wait_ge(stored, 32 * GROUPS)
            for place in places[1:]:
                place.on_sync(sp)

        @block.gpsimd
        def _(pool):
            nc.gpsimd.memset(kv[:], 1.0).then_inc(ones, 1)
            places[0].w.on_gpsimd(pool)
            scatter.on_gpsimd(pool)

        @block.tensor
        def _(pe):
            pe.wait_ge(loaded, 16 * len(loads))

            def group(g, u, r):
                norm.turn(nc, pe, g, c["ident"])
                pe.wait_ge(norm.copied, g * len(norm.BATCHES) + len(norm.BATCHES))
                for m in range(KC):
                    for h in range(2):
                        i = 2 * m + h
                        wait(pe, q_read, g * 4 + (i - 1))
                        for k in range(KC):
                            mm = nc.tensor.matmul(p_q[i % 2][:, 0:HALF], wq[:, k, m * P:m * P + P],
                                                  norm.xnT[:, k, h * HALF:(h + 1) * HALF],
                                                  start=(k == 0), stop=(k == KC - 1))
                        mm.then_inc(q_made, 1)
                for t in range(GROUP):
                    wait(pe, s_read, g * GROUP + t)
                    for out, ww in ((p_kv[:, 0:D], wk), (p_kv[:, D:2 * D], wv), (p_s[:, 0:D], ws)):
                        for k in range(KC):
                            mm = nc.tensor.matmul(out, norm.xnT[:, k, t * P:t * P + P], ww[:, k, :],
                                                  start=(k == 0), stop=(k == KC - 1))
                    mm.then_inc(kvs_made, 1)
            groups(pe, [(0, group)])
            for place in places:
                place.on_tensor(pe)

        @block.scalar
        def _(act):
            act.wait_ge(loaded, 16 * len(loads))

            def group(g, u, r):
                norm.on_scalar(nc, act, g)
                norm.copy(nc, act, g)
                for m in range(KC):
                    for h in range(2):
                        i = 2 * m + h
                        act.wait_ge(q_made, g * 4 + i + 1)
                        nc.scalar.activation(qT[:, m, bass.ds(g * GW + h * HALF, HALF)], p_q[i % 2][:, 0:HALF],
                                             ACT.Identity, bias=bq[:, m:m + 1]).then_inc(q_read, 1)
            groups(act, [(0, group)])

        @block.vector
        def _(v):
            v.wait_ge(loaded, 16 * len(loads))
            v.wait_ge(ones, 1)

            def group(g, u, r):
                wait(v, stored, g * 32)
                norm.on_vector(nc, v, g, lambda k: tile_of(x, g * GROUP + k))
                for t in range(GROUP):
                    v.wait_ge(kvs_made, g * GROUP + t + 1)
                    nc.vector.tensor_tensor(kv[:, t, 0:D], p_kv[:, 0:D], bk[:], ALU.add).then_inc(kv_read, 1)
                    values = kv[:, t, D:].rearrange("p (h w) -> p h w", w=VW)[:, :, 0:DH]
                    nc.vector.tensor_tensor(values, p_kv[:, D:2 * D].rearrange("p (h w) -> p h w", w=DH),
                                            bv[:].rearrange("p (h w) -> p h w", w=DH), ALU.add).then_inc(kv_read, 1)
                    nc.vector.tensor_tensor(norm.xn[:, t, :], p_s[:, 0:D], norm.xn[:, t, :],
                                            ALU.add).then_inc(kv_read, 1)
                    v.wait_ge(kv_read, (g * GROUP + t) * 3 + 3)
                    nc.vector.tensor_tensor(norm.xn[:, t, :], norm.xn[:, t, :], bs[:], ALU.add).then_inc(s_read, 1)
                v.wait_ge(s_read, g * GROUP + GROUP)
            groups(v, [(0, group)])
            for place in places:
                place.on_vector(v)

def load_edges(nc, st, rows_dram, source, lo, clear=()):
    with ExitStack() as ctx:
        a = Alloc(nc, ctx, f"load_{st.name}")
        both = a.sb("both", [P, st.tiles, 2], I32)
        loaded = a.sem("loaded")
        block = ctx.enter_context(nc.Block())

        @block.sync
        def _(sp):
            sp.dma_start(both[:], rows_dram.rearrange("(p t) w -> p t w", p=P)[:, 0:st.tiles, :]).then_inc(loaded, 16)

        @block.gpsimd
        def _(pool):
            for tile, value in clear:
                nc.gpsimd.memset(tile[:], value)

        @block.vector
        def _(v):
            v.wait_ge(loaded, 16)
            nc.vector.tensor_copy(source[:], both[:, :, 0])
            nc.vector.tensor_copy(lo[:], both[:, :, 1])


RING = UNROLL


def gather_loop(nc, pool, tiles, source, index, staged, passed, rows_dram, ring, gathered, freed, side=None):
    def gather(t, u, r):
        if u % UNROLL == 0:
            wait(pool, freed, t - UNROLL)
            nc.gpsimd.tensor_copy(index[:, u // UNROLL, :], cols(source, t, UNROLL)).then_inc(staged, 1)
            wait_alone(pool, staged, r * 2 + (u // UNROLL + 1), passed)
            if isinstance(t, int):
                pool.sem_inc(passed, 1)
        wait_alone(pool, freed, t - (RING - 1), passed)
        pool.indirect_dma_start(ring[:, u % RING, :], None, rows_dram,
                                bass.IndirectOffsetOnAxis(index[:, u // UNROLL, u % UNROLL:u % UNROLL + 1], 0)
                                ).then_inc(gathered[u % RING], 16)
        if beside and (u + 1) % UNROLL == 0:
            side.chunk(pool, r * 2 + u // UNROLL, u // UNROLL, r)
    beside = side is not None
    together = side.chunks * UNROLL if side else tiles
    pipelined(pool, together, 2 * UNROLL, [(0, gather)])
    beside = False
    for t in range(together, tiles):
        gather(t, t % (2 * UNROLL), t // (2 * UNROLL))


def node_tiles(nc, st, hi_row, i, behind, engine=DVE):
    start = i * UNROLL + (UNROLL - behind)
    _, values = nc.values_load_multi_w_load_instructions(
        hi_row[0:1, bass.ds(start, UNROLL + behind)], (engine,), min_val=0, max_val=st.buckets - 1,
        skip_runtime_bounds_check_because="the row is clamped to the last bucket")
    return values


def attend(nc, c, source, lo, hi_row, qT, kv_dram, acc, top_score, no_edges, acc_dram, scatter, attr_dram):
    with ExitStack() as ctx:
        a = Alloc(nc, ctx, "attend")
        index = a.sb("index", [P, 2, UNROLL], I32)
        kv = a.sb("kv", [P, RING, KVW])
        kT = a.sb("kT", [P, 2, H, P])
        qs = a.sb("qs", [P, 4, KC, P])
        other = a.sb("other", [P, UNROLL, P], BF16)
        least = a.sb("least", [P, 2, H])
        minus = a.sb("minus", [P, 4, H])
        drop = a.sb("drop", [P, 4, H])
        shrink = a.sb("shrink", [P, UNROLL, H])
        prob = a.sb("prob", [P, 2, H, P])
        probT = a.sb("probT", [P, 2, H, P])
        p_k = [a.ps(f"k{i}", [P, 512]) for i in range(2)]
        p_s = [a.ps(f"s{i}", [P, 512]) for i in range(2)]
        p_t = [a.ps(f"t{i}", [P, 512]) for i in range(2)]
        p_v = [a.ps(f"v{i}", [P, 512]) for i in range(2)]
        gathered, fetched = a.sems("gathered", RING), a.sems("fetched", 4)
        staged, passed = a.sem("staged"), a.sem("passed")
        k_turned, k_copied, prepared, scored = a.sem("k_turned"), a.sem("k_copied"), a.sem("prepared"), a.sem("scored")
        reduced, raised, lowered, kept = a.sem("reduced"), a.sem("raised"), a.sem("lowered"), a.sem("kept")
        exped, shrunk, p_turned, p_copied = a.sem("exped"), a.sem("shrunk"), a.sem("p_turned"), a.sem("p_copied")
        valued, summed, zeroed = a.sem("valued"), a.sem("summed"), a.sem("zeroed")
        stored = a.sem("stored")
        block = ctx.enter_context(nc.Block())
        T = BY_DST.tiles
        TURN, SCORE, PTURN, VALUE = 0, 1, 2, 3

        @block.sync
        def _(sp):
            tile_regs = [None]

            def load_tiles(i):
                tile_regs[0] = node_tiles(nc, BY_DST, hi_row, i, 0, mybir.EngineType.SP)

            def queries(t, u, r):
                wait(sp, scored, t - 3)
                sp.dma_start(qs[:, u % 4, :, :], qT[:, :, bass.ds(tile_regs[0][u] * P, P)]).then_inc(fetched[u % 4], 16)

            def attributes(t, u, r):
                if u % UNROLL == 0:
                    load_attributes(sp, scatter, attr_dram, r * 2 + u // UNROLL, u // UNROLL, r)

            def queries_of_half(t, u, r):
                if u % UNROLL == 0:
                    load_tiles(r * 2 + u // UNROLL)
                queries(t, u % UNROLL, r * 2 + u // UNROLL)
            pipelined(sp, scatter.chunks * UNROLL, 2 * UNROLL, [(0, attributes), (0, queries_of_half)])
            for t in range(scatter.chunks * UNROLL, T):
                queries_of_half(t, t % (2 * UNROLL), t // (2 * UNROLL))
            sp.wait_ge(summed, T * 5)
            sp.dma_start(acc_dram, acc[:, 0:NT, :]).then_inc(stored, 16)
            sp.wait_ge(stored, 16)

        @block.gpsimd
        def _(pool):
            nc.gpsimd.memset(kT[:], 0.0).then_inc(zeroed, 1)
            gather_loop(nc, pool, T, source, index, staged, passed, kv_dram, kv, gathered, valued,
                        scatter)
            scatter.drain(pool)

        @block.tensor
        def _(pe):
            def turn_keys(t, u, r):
                pe.wait_ge(gathered[u], r * 16 + 16)
                wait(pe, k_copied, t * 2 - 2)
                for k in range(KC):
                    mm = nc.tensor.transpose(p_k[u % 2][:, k * P:k * P + P], kv[:, u, k * P:k * P + P], c["ident"][:])
                mm.then_inc(k_turned, 1)

            def score(t, u, r):
                pe.wait_ge(prepared, t + 1)
                pe.wait_ge(fetched[u % 4], r * 32 + (16 + u // 4 * 16))
                pe.wait_ge(k_copied, t * 2 + 2)
                wait(pe, exped, t - 1)
                s = p_s[u % 2]
                nc.tensor.matmul(s[:, :], other[:, u, :], c["drop4"][:], start=True, stop=False,
                                 skip_group_check=True)
                for h in range(H):
                    mm = nc.tensor.matmul(s[:, h * P:h * P + P], qs[:, u % 4, h * DH // P, :], kT[:, u % 2, h, :],
                                          start=False, stop=True, skip_group_check=True)
                mm.then_inc(scored, 1)

            def turn_probs(t, u, r):
                pe.wait_ge(exped, t + 1)
                wait(pe, p_copied, t - 1)
                for h in range(H):
                    mm = nc.tensor.transpose(p_t[u % 2][:, h * P:h * P + P], prob[:, u % 2, h, :], c["ident"][:])
                mm.then_inc(p_turned, 1)

            def value(t, u, r):
                pe.wait_ge(p_copied, t + 1)
                wait(pe, summed, t * 5 - 5)
                for h in range(H):
                    nc.tensor.matmul(p_v[u % 2][:, h * VW:h * VW + VW], probT[:, u % 2, h, :],
                                     kv[:, u, D + h * VW:D + h * VW + VW], start=True, stop=True)
                nc.tensor.matmul(p_v[u % 2][:, H * VW:H * VW + 2], other[:, u, :], c["ones_bf"][:, 0:2],
                                 start=True, stop=True).then_inc(valued, 1)
            pipelined(pe, T, UNROLL, [(TURN, turn_keys), (SCORE, score), (PTURN, turn_probs), (VALUE, value)])

        @block.scalar
        def _(act):
            act.wait_ge(zeroed, 1)

            def copy_keys(t, u, r):
                act.wait_ge(k_turned, t + 1)
                wait(act, scored, t - 1)
                for half in range(P // DH):
                    rows = slice(half * DH, half * DH + DH)
                    nc.scalar.activation(kT[rows, u % 2, half::P // DH, :],
                                         p_k[u % 2][rows, 0:D].rearrange("p (c e) -> p c e", e=P),
                                         ACT.Copy, scale=-(DH ** -0.5)).then_inc(k_copied, 1)

            def exponentials(t, u, r):
                act.wait_ge(lowered, t + 1)
                wait(act, p_turned, t - 1)
                for h in range(H):
                    e = nc.scalar.activation(prob[:, u % 2, h, :], p_s[u % 2][:, h * P:h * P + P], ACT.Exp,
                                             bias=minus[:, u % 4, h:h + 1], scale=-1.0)
                e.then_inc(exped, 1)
                wait(act, summed, t * 5 - 35)
                nc.scalar.activation(shrink[:, u, :], drop[:, u % 4, :], ACT.Exp).then_inc(shrunk, 1)

            def copy_probs(t, u, r):
                act.wait_ge(p_turned, t + 1)
                wait(act, valued, t - 1)
                nc.scalar.activation(probT[:, u % 2, :, :].rearrange("p h n -> p (h n)"), p_t[u % 2][:, :],
                                     ACT.Copy).then_inc(p_copied, 1)
            pipelined(act, T, UNROLL, [(TURN, copy_keys), (SCORE, exponentials), (PTURN, copy_probs)])

        @block.vector
        def _(v):
            tile_regs = [None]

            def load_tiles(i):
                tile_regs[0] = node_tiles(nc, BY_DST, hi_row, i, VALUE)

            def node_tile(u, lag):
                return tile_regs[0][VALUE + (u if u < UNROLL - lag else u - UNROLL)]

            def prepare(t, u, r):
                if u % 4 == 0:
                    wait(v, valued, t - 4)
                    nc.vector.tensor_tensor(other[:, u:u + 4, :], c["iota"][:].unsqueeze(1).to_broadcast([P, 4, P]),
                                            cols(lo, t, 4).unsqueeze(2).to_broadcast([P, 4, P]),
                                            ALU.not_equal).then_inc(prepared, 4)

            def maxima(t, u, r):
                n = node_tile(u, SCORE)
                top = tile_of(top_score, n)
                v.wait_ge(scored, t + 1)
                nc.vector.tensor_reduce(least[:, u % 2, :], p_s[u % 2][:, :].rearrange("p (h e) -> p h e", h=H), AX.X,
                                        ALU.min).then_inc(reduced, 1)
                v.wait_ge(reduced, t + 1)
                wait(v, kept, t)
                nc.vector.tensor_tensor(minus[:, u % 4, :], least[:, u % 2, :], top, ALU.min).then_inc(raised, 1)
                v.wait_ge(raised, t + 1)
                nc.vector.tensor_tensor(drop[:, u % 4, :], minus[:, u % 4, :], top, ALU.subtract).then_inc(lowered, 1)
                v.wait_ge(lowered, t + 1)
                nc.vector.tensor_scalar(top, minus[:, u % 4, :], 1.0, None, ALU.mult).then_inc(kept, 1)

            def add_up(t, u, r):
                n = node_tile(u, VALUE)
                v.wait_ge(valued, t + 1)
                v.wait_ge(shrunk, t + 1)
                wait(v, summed, t * 5)
                sums = tile_of(acc, n)
                for h in range(H):
                    part = sums[:, h * VW:h * VW + VW]
                    nc.vector.scalar_tensor_tensor(part, part, shrink[:, u, h:h + 1],
                                                   p_v[u % 2][:, h * VW:h * VW + VW], ALU.mult, ALU.add).then_inc(summed, 1)
                count = cols(no_edges, n)
                nc.vector.scalar_tensor_tensor(count, p_v[u % 2][:, H * VW:H * VW + 1], -float(P), count, ALU.add,
                                               ALU.add).then_inc(summed, 1)
            pipelined(v, T, UNROLL, [(TURN, prepare), (SCORE, maxima), (VALUE, add_up)], top=load_tiles)

FF = 4 * D
FC = FF // P
EXPERTS = 8
BN_EPS = 1e-3


def feed_forward(nc, c, x, w, acc_dram, skip_dram):
    with ExitStack() as ctx:
        a = Alloc(nc, ctx, "ff")
        rows = {n: a.sb(n, [P, D]) for n in ("ln1_g", "ln1_b", "ln2_g", "ln2_b", "b2")}
        w1 = a.sb("w1", [P, KC, FF])
        w2 = a.sb("w2", [P, FC, D])
        b1 = a.sb("b1", [P, FC])
        norm1 = Normed(Alloc(nc, ctx, "ff_n1"), rows["ln1_g"], rows["ln1_b"])
        norm2 = Normed(Alloc(nc, ctx, "ff_n2"), rows["ln2_g"], rows["ln2_b"], turned=False)
        sums = a.sb("sums", [P, GROUP, H * VW])
        skip = a.sb("skip", [P, GROUP, D])
        weight = a.sb("weight", [P, GROUP, H])
        y = a.sb("y", [P, GROUP, D])
        h_b2 = a.sb("h_b2", [P, GROUP, D])
        z = a.sb("z", [P, GROUP, D])
        hidden = a.sb("hidden", [P, FC, GW])
        p_1 = [a.ps(f"p1{i}", [P, 512]) for i in range(3)]
        p_2 = [a.ps(f"p2{i}", [P, 512]) for i in range(3)]
        loaded, fetched, used = a.sem("loaded"), a.sem("fetched"), a.sem("used")
        den, inv, att, biased = a.sem("den"), a.sem("inv"), a.sem("att"), a.sem("biased")
        up, gelued, down, evacuated, added = a.sem("up"), a.sem("gelued"), a.sem("down"), a.sem("evacuated"), a.sem("added")
        loads = [(w1, chunked(w["W1"])), (w2, chunked(w["W2"])), (b1, w["b1"].rearrange("(c p) -> p c", p=P))]
        loads += [(t, w[n].partition_broadcast(P)) for n, t in rows.items()]
        block = ctx.enter_context(nc.Block())

        @block.sync
        def _(sp):
            for to, from_ in loads:
                sp.dma_start(to[:], from_, allow_slow_non_contiguous=True).then_inc(loaded, 16)

            def fetch(g, u, r):
                wait(sp, used, g * GROUP)
                sp.dma_start(sums[:], acc_dram[:, bass.ds(g * GROUP, GROUP), :]).then_inc(fetched, 16)
                sp.dma_start(skip[:], tiled(skip_dram)[:, bass.ds(g * GROUP, GROUP), :]).then_inc(fetched, 16)
            groups(sp, [(0, fetch)])

        @block.tensor
        def _(pe):
            pe.wait_ge(loaded, 16 * len(loads))

            def group(g, u, r):
                norm1.turn(nc, pe, g, c["ident"])
                pe.wait_ge(norm1.copied, g * len(norm1.BATCHES) + len(norm1.BATCHES))
                for m in range(FC):
                    for h in range(2):
                        i = 2 * m + h
                        wait(pe, gelued, g * 2 * FC + (i - 2))
                        for k in range(KC):
                            mm = nc.tensor.matmul(p_1[i % 3][:, 0:HALF], w1[:, k, m * P:m * P + P],
                                                  norm1.xnT[:, k, h * HALF:(h + 1) * HALF],
                                                  start=(k == 0), stop=(k == KC - 1))
                        mm.then_inc(up, 1)
                pe.wait_ge(gelued, g * 2 * FC + 2 * FC)
                for t in range(GROUP):
                    if t < 3:
                        wait(pe, evacuated, g * GROUP)
                    else:
                        pe.wait_ge(evacuated, g * GROUP + (t - 2))
                    for m in range(FC):
                        mm = nc.tensor.matmul(p_2[t % 3][:, 0:D], hidden[:, m, t * P:t * P + P], w2[:, m, :],
                                              start=(m == 0), stop=(m == FC - 1))
                    mm.then_inc(down, 1)
            groups(pe, [(0, group)])

        @block.scalar
        def _(act):
            act.wait_ge(loaded, 16 * len(loads))

            def first(g, u, r):
                norm1.on_scalar(nc, act, g)
                norm1.copy(nc, act, g)

            def gelu(g, u, r):
                wait(act, down, g * GROUP)
                for m in range(FC):
                    for h in range(2):
                        i = 2 * m + h
                        act.wait_ge(up, g * 2 * FC + i + 1)
                        nc.scalar.activation(hidden[:, m, h * HALF:(h + 1) * HALF], p_1[i % 3][:, 0:HALF], ACT.Gelu,
                                             bias=b1[:, m:m + 1]).then_inc(gelued, 1)

            def second(g, u, r):
                norm2.on_scalar(nc, act, g)
            pipelined(act, GROUPS, 1, [(0, first), (1, second), (0, gelu)])

        @block.vector
        def _(v):
            v.wait_ge(loaded, 16 * len(loads))

            def attention(g, u, r):
                v.wait_ge(fetched, g * 32 + 32)
                heads = [sums[:, t, :].rearrange("p (h w) -> p h w", w=VW) for t in range(GROUP)]
                for t in range(GROUP):
                    nc.vector.tensor_scalar(weight[:, t, :], heads[t][:, :, DH], 1e-16, None, ALU.add).then_inc(den, 1)
                v.wait_ge(den, g * GROUP + GROUP)
                nc.vector.reciprocal(weight[:], weight[:]).then_inc(inv, 1)
                v.wait_ge(inv, g + 1)
                for t in range(GROUP):
                    nc.vector.tensor_tensor(y[:, t, :].rearrange("p (h w) -> p h w", w=DH), heads[t][:, :, 0:DH],
                                            weight[:, t, :].unsqueeze(2).to_broadcast([P, H, DH]),
                                            ALU.mult).then_inc(att, 1)
                for t in range(GROUP):
                    v.wait_ge(att, g * GROUP + t + 1)
                    nc.vector.tensor_tensor(y[:, t, :], y[:, t, :], skip[:, t, :], ALU.add).then_inc(used, 1)
                v.wait_ge(used, g * GROUP + GROUP)
                norm1.on_vector(nc, v, g, lambda k: y[:, k, :])

            def output(g, u, r):
                for t in range(GROUP):
                    v.wait_ge(down, g * GROUP + t + 1)
                    nc.vector.tensor_tensor(z[:, t, :], p_2[t % 3][:, 0:D], h_b2[:, t, :], ALU.add).then_inc(evacuated, 1)
                v.wait_ge(evacuated, g * GROUP + GROUP)
                norm2.on_vector(nc, v, g, lambda k: z[:, k, :])
                v.wait_ge(norm2.normed, g * norm2.steps + norm2.steps)
                for t in range(GROUP):
                    rows_of_x = tile_of(x, g * GROUP + t)
                    nc.vector.tensor_tensor(rows_of_x, rows_of_x, norm2.xn[:, t, :], ALU.add).then_inc(added, 1)

            def keep_h(g, u, r):
                v.wait_ge(norm1.normed, g * norm1.steps + norm1.steps)
                wait(v, evacuated, g * GROUP)
                for t in range(GROUP):
                    nc.vector.tensor_tensor(h_b2[:, t, :], norm1.xn[:, t, :], rows["b2"][:], ALU.add).then_inc(biased, 1)
                wait(v, added, g * GROUP)
                v.wait_ge(biased, g * GROUP + GROUP)
                v.wait_ge(norm1.turned, g * len(norm1.BATCHES) + len(norm1.BATCHES))
            pipelined(v, GROUPS, 1, [(0, attention), (1, output), (0, keep_h)])


def mixture(nc, c, x, w, scatter, hi2, per_node, by_src):
    E = EXPERTS
    with ExitStack() as ctx:
        a = Alloc(nc, ctx, "moe")
        norm = Normed(Alloc(nc, ctx, f"{a.stage}_n"))
        layers = [a.sb(n, [P, E, KC, D]) for n in ("W1", "W2", "Wo")]
        wr = a.sb("Wr", [P, KC, E])
        br = a.sb("br", [P, E])
        bo = a.sb("bo", [E, D])
        bn = {n: a.sb(n, [P, E, KC]) for i in "12" for n in (f"b{i}", f"g{i}", f"be{i}", f"m{i}", f"v{i}")}
        logits = a.sb("logits", [P, GROUP, E])
        top = a.sb("top", [P, GROUP])
        total = a.sb("total", [P, GROUP])
        share = a.sb("share", [P, GROUP, E])
        shareT = a.sb("shareT", [E, GW])
        h1 = a.sb("h1", [P, KC, GW])
        h2 = a.sb("h2", [P, 2, KC, GW])
        p_r = a.ps("r", [P, 512])
        p_1 = [a.ps(f"p1{i}", [P, 512]) for i in range(3)]
        p_o = [a.ps(f"po{i}", [P, 512]) for i in range(2)]
        beside = AttributeSums(nc, c, Alloc(nc, ctx, "attribute_sums"), hi2, per_node, by_src, norm.banks)
        loaded, folded, rooted, ready = a.sem("loaded"), a.sem("folded"), a.sem("rooted"), a.sem("ready")
        routed, gated, exped, shared = a.sem("routed"), a.sem("gated"), a.sem("exped"), a.sem("shared")
        folding, summed = a.sem("folding"), a.sem("summed")
        share_turned, share_copied = a.sem("share_turned"), a.sem("share_copied")
        made, activated, out, added = a.sem("made"), a.sem("activated"), a.sem("out"), a.sem("added")
        loads = [(wr[:], chunked(w["Wr"])), (br[:], w["br"].partition_broadcast(P)), (bo[:], w["bo"])]
        loads += [(tile[:, e, :, :], chunked(w[n][e])) for n, tile in zip(("W1", "W2", "Wo"), layers) for e in range(E)]
        loads += [(tile[:, :, k], w[n][:, k * P:k * P + P].rearrange("e p -> p e")) for n, tile in bn.items()
                  for k in range(KC)]
        PER = 2 * 2 * KC * E
        OUT = (E + 1) * GROUP
        block = ctx.enter_context(nc.Block())

        @block.gpsimd
        def _(pool):
            scatter.on_gpsimd(pool)

        @block.sync
        def _(sp):
            for to, from_ in loads:
                sp.dma_start(to, from_, allow_slow_non_contiguous=True).then_inc(loaded, 16)
            beside.on_sync(sp)

        @block.tensor
        def _(pe):
            pe.wait_ge(loaded, 16 * len(loads))

            def hidden(g, i, weight, moving):
                for m in range(KC):
                    for h in range(2):
                        wait(pe, activated, g * PER + (i - 2))
                        for k in range(KC):
                            mm = nc.tensor.matmul(p_1[i % 3][:, 0:HALF], weight[:, k, m * P:m * P + P],
                                                  moving[:, k, h * HALF:(h + 1) * HALF],
                                                  start=(k == 0), stop=(k == KC - 1))
                        mm.then_inc(made, 1)
                        i += 1
                return i

            def group(g, u, r):
                wait(pe, beside.summed, g * (beside.PER_GROUP * UNROLL))
                norm.turn(nc, pe, g, c["ident"])
                pe.wait_ge(norm.copied, g * len(norm.BATCHES) + len(norm.BATCHES))
                wait(pe, share_copied, g * 2)
                for t in range(GROUP):
                    for k in range(KC):
                        mm = nc.tensor.matmul(p_r[:, t * E:t * E + E], norm.xnT[:, k, t * P:t * P + P], wr[:, k, :],
                                              start=(k == 0), stop=(k == KC - 1))
                mm.then_inc(routed, 1)
                i, o = 0, 0

                def output(lhsTs, rhss):
                    nonlocal o
                    for t in range(GROUP):
                        wait(pe, added, g * OUT + (o - 1))
                        for k, rhs in enumerate(rhss):
                            mm = nc.tensor.matmul(p_o[o % 2][:, 0:D], lhsTs[k][:, t * P:t * P + P], rhs,
                                                  start=(k == 0), stop=(k == len(rhss) - 1))
                        mm.then_inc(out, 1)
                        o += 1
                for e in range(E):
                    i = hidden(g, i, layers[0][:, e], norm.xnT)
                    beside.product(pe, g, 2 * e)
                    if e == 0:
                        pe.wait_ge(shared, g + 1)
                        for b, (k0, n) in enumerate(((0, 4), (4, GROUP - 4))):
                            wait(pe, share_copied, g * 2 + b)
                            for t in range(n):
                                mm = nc.tensor.transpose(p_r[0:E, t * P:t * P + P], share[:, k0 + t, :], c["ident"][:])
                            mm.then_inc(share_turned, 1)
                    else:
                        output([h2[:, (e - 1) % 2, k, :] for k in range(KC)],
                               [layers[2][:, e - 1, k, :] for k in range(KC)])
                    pe.wait_ge(activated, g * PER + i)
                    i = hidden(g, i, layers[1][:, e], h1)
                    if 2 * e + 1 < beside.PER_GROUP:
                        beside.product(pe, g, 2 * e + 1)
                    if e == 0:
                        pe.wait_ge(share_copied, g * 2 + 2)
                        output([shareT], [bo[:]])
                pe.wait_ge(activated, g * PER + i)
                output([h2[:, (E - 1) % 2, k, :] for k in range(KC)], [layers[2][:, E - 1, k, :] for k in range(KC)])
            groups(pe, [(0, group)])

        @block.scalar
        def _(act):
            act.wait_ge(folded, 2)
            for i in "12":
                nc.scalar.activation(bn[f"v{i}"][:], bn[f"v{i}"][:], ACT.Sqrt).then_inc(rooted, 1)
            act.wait_ge(ready, 2)

            def group(g, u, r):
                norm.on_scalar(nc, act, g)
                norm.copy(nc, act, g)
                act.wait_ge(gated, g * (2 + GROUP) + 2 + GROUP)
                nc.scalar.activation(share[:], logits[:], ACT.Exp).then_inc(exped, 1)
                i = 0
                for e in range(E):
                    for n, to in (("1", h1), ("2", h2[:, e % 2])):
                        if n == "2" and e == 0:
                            for b, (k0, c0) in enumerate(((0, 4), (4, GROUP - 4))):
                                act.wait_ge(share_turned, g * 2 + b + 1)
                                nc.scalar.activation(shareT[:, k0 * P:(k0 + c0) * P], p_r[0:E, 0:c0 * P],
                                                     ACT.Copy).then_inc(share_copied, 1)
                        if n == "2" and e >= 2:
                            act.wait_ge(out, g * OUT + e * GROUP)
                        elif n == "2":
                            wait(act, out, g * OUT)
                        for m in range(KC):
                            for h in range(2):
                                act.wait_ge(made, g * PER + i + 1)
                                nc.scalar.activation(to[:, m, h * HALF:(h + 1) * HALF], p_1[i % 3][:, 0:HALF], ACT.Relu,
                                                     bias=bn[f"b{n}"][:, e, m:m + 1],
                                                     scale=bn[f"g{n}"][:, e, m:m + 1]).then_inc(activated, 1)
                                i += 1
            groups(act, [(0, group)])

        @block.vector
        def _(v):
            v.wait_ge(loaded, 16 * len(loads))
            done = [0]

            def step(ins):
                done[0] += 1
                ins.then_inc(folding, 1)
                v.wait_ge(folding, done[0])
            for i in "12":
                var = bn[f"v{i}"][:]
                step(nc.vector.tensor_scalar(var, var, BN_EPS, None, ALU.add))
                nc.vector.reciprocal(var, var).then_inc(folded, 1)
            v.wait_ge(rooted, 2)
            for i in "12":
                scale, shift = bn[f"g{i}"][:], bn[f"b{i}"][:]
                step(nc.vector.tensor_tensor(scale, scale, bn[f"v{i}"][:], ALU.mult))
                step(nc.vector.tensor_tensor(shift, shift, bn[f"m{i}"][:], ALU.subtract))
                step(nc.vector.tensor_tensor(shift, shift, scale, ALU.mult))
                nc.vector.tensor_tensor(shift, shift, bn[f"be{i}"][:], ALU.add).then_inc(ready, 1)

            def group(g, u, r):
                wait(v, added, g * OUT)
                beside.mark(v, g, 0)
                norm.on_vector(nc, v, g, lambda k: tile_of(x, g * GROUP + k))
                v.wait_ge(routed, g + 1)
                v.wait_ge(norm.turned, g * len(norm.BATCHES) + len(norm.BATCHES))
                for t in range(GROUP):
                    nc.vector.tensor_tensor(logits[:, t, :], p_r[:, t * E:t * E + E], br[:], ALU.add).then_inc(gated, 1)
                v.wait_ge(gated, g * (2 + GROUP) + GROUP)
                nc.vector.tensor_reduce(top[:], logits[:], AX.X, ALU.max).then_inc(gated, 1)
                v.wait_ge(gated, g * (2 + GROUP) + 1 + GROUP)
                nc.vector.tensor_tensor(logits[:], logits[:], top[:].unsqueeze(2).to_broadcast([P, GROUP, E]),
                                        ALU.subtract).then_inc(gated, 1)
                v.wait_ge(exped, g + 1)
                nc.vector.tensor_reduce(total[:], share[:], AX.X, ALU.add).then_inc(summed, 1)
                v.wait_ge(summed, g * 2 + 1)
                nc.vector.reciprocal(total[:], total[:]).then_inc(summed, 1)
                v.wait_ge(summed, g * 2 + 2)
                nc.vector.tensor_tensor(share[:], share[:], total[:].unsqueeze(2).to_broadcast([P, GROUP, E]),
                                        ALU.mult).then_inc(shared, 1)
                v.wait_ge(shared, g + 1)
                rounds = 0

                def attributes(n):
                    nonlocal rounds
                    while rounds < min(n, beside.PER_GROUP):
                        if rounds + 1 < beside.PER_GROUP:
                            beside.mark(v, g, rounds + 1)
                        beside.add(v, g, rounds)
                        rounds += 1
                for o in range(OUT):
                    e, t = o // GROUP - 1, o % GROUP
                    if t == 0:
                        attributes(max(1, 2 * (o // GROUP)))
                    v.wait_ge(out, g * OUT + o + 1)
                    if o >= GROUP:
                        v.wait_ge(added, g * OUT + (o + 1 - GROUP))
                    rows_of_x = tile_of(x, g * GROUP + t)
                    if e < 0:
                        nc.vector.tensor_tensor(rows_of_x, p_o[o % 2][:, 0:D], rows_of_x, ALU.add).then_inc(added, 1)
                    else:
                        nc.vector.scalar_tensor_tensor(rows_of_x, p_o[o % 2][:, 0:D], share[:, t, e:e + 1], rows_of_x,
                                                       ALU.mult, ALU.add).then_inc(added, 1)
                attributes(beside.PER_GROUP)
            groups(v, [(0, group)])

EDGE_F = 64
HALF_F = 128
ATTR_W = EDGE_F + 1
CHUNK = UNROLL // 2


def empty_attributes(nc, ctx, st, n):
    empty = Alloc(nc, ctx, "empty_attr").sb("slots", [P, n, ATTR_W])
    with ExitStack() as bctx:
        zeroed = Alloc(nc, bctx, "empty_attr_zeroed").sem("zeroed")
        block = bctx.enter_context(nc.Block())

        @block.vector
        def _(v):
            nc.vector.memset(empty[:], 0.0).then_inc(zeroed, 1)
            v.wait_ge(zeroed, 1)
            nc.vector.memset(empty[:, :, EDGE_F], float(PAD_LO))
    return empty


def load_attributes(sp, scatter, attr_dram, t, u, r):
    wait(sp, scatter.landed[u], r * (16 * scatter.wide))
    attr = attr_dram.rearrange("(p c) f -> p c f", p=scatter.st.parts)
    data = scatter.data[:, u, :].rearrange("p (c w) -> p c w", w=ATTR_W)
    sp.dma_start(data[:, :, 0:EDGE_F], attr[:, bass.ds(t * scatter.wide, scatter.wide), :]).then_inc(scatter.loaded[u], 16)


class AttributeSums:
    RINGS = 3
    PER_GROUP = BY_SRC.tiles // UNROLL // GROUPS

    def __init__(self, nc, c, a, hi_row, sums, rows_dram, banks):
        assert self.PER_GROUP * GROUPS * UNROLL == BY_SRC.tiles and self.PER_GROUP % self.RINGS == 0
        self.nc, self.c, self.hi_row, self.sums, self.rows_dram, self.banks = nc, c, hi_row, sums, rows_dram, banks
        self.ring = a.sb("ring", [P, self.RINGS, UNROLL, ATTR_W])
        self.mine = a.sb("mine", [P, self.RINGS, UNROLL, P])
        self.arrived = a.sems("arrived", self.RINGS)
        self.marked, self.multiplied, self.summed = a.sem("marked"), a.sem("multiplied"), a.sem("summed")

    def on_sync(self, sp):
        rows = self.rows_dram.rearrange("(p t) w -> p t w", p=P)

        def load(t, u, r):
            wait(sp, self.multiplied, t - (self.RINGS - 1))
            sp.dma_start(self.ring[:, u, :, :], rows[:, bass.ds(t * UNROLL, UNROLL), :]).then_inc(self.arrived[u], 16)
        pipelined(sp, self.PER_GROUP * GROUPS, self.RINGS, [(0, load)])

    def mark(self, v, g, k):
        u = k % self.RINGS
        here = g * (self.PER_GROUP // self.RINGS * 16) + (k // self.RINGS * 16 + 16)
        v.wait_ge(self.arrived[u], here)
        wait(v, self.multiplied, g * self.PER_GROUP + (k - self.RINGS + 1))
        for half in range(0, UNROLL, 4):
            at = self.ring[:, u, half:half + 4, EDGE_F:ATTR_W]
            self.nc.vector.tensor_tensor(self.mine[:, u, half:half + 4, :],
                                         self.c["iota"][:].unsqueeze(1).to_broadcast([P, 4, P]),
                                         at.to_broadcast([P, 4, P]), ALU.is_equal).then_inc(self.marked, 1)

    def product(self, pe, g, k):
        u = k % self.RINGS
        pe.wait_ge(self.marked, g * (2 * self.PER_GROUP) + (2 * k + 2))
        wait(pe, self.summed, g * (self.PER_GROUP * UNROLL) + max(0, k - 1) * UNROLL)
        for t in range(UNROLL):
            mm = self.nc.tensor.matmul(self.banks[k % 2][:, t * EDGE_F:(t + 1) * EDGE_F], self.mine[:, u, t, :],
                                       self.ring[:, u, t, 0:EDGE_F], start=True, stop=True)
        mm.then_inc(self.multiplied, 1)

    def add(self, v, g, k):
        tiles = node_tiles(self.nc, BY_SRC, self.hi_row, g * self.PER_GROUP + k, 0)
        v.wait_ge(self.multiplied, g * self.PER_GROUP + (k + 1))
        for t in range(UNROLL):
            wait(v, self.summed, g * (self.PER_GROUP * UNROLL) + (k * UNROLL + t))
            part = tile_of(self.sums, tiles[t])
            self.nc.vector.tensor_tensor(part, part, self.banks[k % 2][:, t * EDGE_F:(t + 1) * EDGE_F],
                                         ALU.add).then_inc(self.summed, 1)


def segment_sum(nc, c, st, hi_row, width, sums, rows_dram, source, lo):
    with ExitStack() as ctx:
        a = Alloc(nc, ctx, f"sum_{st.name}_{width}")
        ring = a.sb("ring", [P, UNROLL, width])
        mine = a.sb("mine", [P, UNROLL, P])
        p_sum = [a.ps(f"sum{i}", [P, 512]) for i in range(4)]
        index = a.sb("index", [P, 2, UNROLL], I32)
        arrived = a.sems("arrived", UNROLL)
        staged, passed = a.sem("staged"), a.sem("passed")
        marked, multiplied, summed = a.sem("marked"), a.sem("multiplied"), a.sem("summed")
        block = ctx.enter_context(nc.Block())
        LAG = 2

        @block.gpsimd
        def _(pool):
            gather_loop(nc, pool, st.tiles, source, index, staged, passed, rows_dram, ring, arrived, multiplied)

        @block.tensor
        def _(pe):
            def product(t, u, r):
                pe.wait_ge(arrived[u], r * 16 + 16)
                pe.wait_ge(marked, t + 1)
                wait(pe, summed, t - 3)
                nc.tensor.matmul(p_sum[u % 4][:, 0:width], mine[:, u, :], ring[:, u, 0:width], start=True,
                                 stop=True).then_inc(multiplied, 1)
            pipelined(pe, st.tiles, UNROLL, [(0, product)])

        @block.vector
        def _(v):
            tile_regs = [None]

            def load_tiles(i):
                tile_regs[0] = node_tiles(nc, st, hi_row, i, LAG)

            def mark(t, u, r):
                if u % CHUNK:
                    return
                wait(v, multiplied, t - CHUNK)
                at = cols(lo, t, CHUNK).unsqueeze(2)
                nc.vector.tensor_tensor(mine[:, u:u + CHUNK, :], c["iota"][:].unsqueeze(1).to_broadcast([P, CHUNK, P]),
                                        at.to_broadcast([P, CHUNK, P]), ALU.is_equal).then_inc(marked, CHUNK)

            def add_up(t, u, r):
                n = tile_regs[0][LAG + (u if u < UNROLL - LAG else u - UNROLL)]
                v.wait_ge(multiplied, t + 1)
                wait(v, summed, t)
                part = tile_of(sums, n)
                nc.vector.tensor_tensor(part, part, p_sum[u % 4][:, 0:width], ALU.add).then_inc(summed, 1)
            pipelined(v, st.tiles, UNROLL, [(0, mark), (LAG, add_up)], top=load_tiles)


def convolve_dense(nc, c, x, w, per_node, no_edges, dinv, sums, rest, conv_dram):
    with ExitStack() as ctx:
        a = Alloc(nc, ctx, "conv")
        norm = Normed(Alloc(nc, ctx, "conv_n"))
        HC3 = KC + HALF_F // P
        we = a.sb("W_edge", [EDGE_F, HALF_F])
        be = a.sb("b_edge", [P, 1])
        both = a.sb("both", [P, HC3, 2 * D])
        bias = a.sb("bias", [P, D])
        bias2 = a.sb("bias2", [P, D])
        per = a.sb("per", [P, GROUP, EDGE_F])
        pnT = a.sb("pnT", [P, GW])
        perT, z = pnT[0:EDGE_F, :], pnT
        p_e = [a.ps(f"e{i}", [P, 512]) for i in range(2)]
        p_c = [a.ps(f"c{i}", [P, 512]) for i in range(3)]
        loaded, prepared, rooted, ready = a.sem("loaded"), a.sem("prepared"), a.sem("rooted"), a.sem("ready")
        per_staged, passed = a.sem("per_staged"), a.sem("passed")
        per_turned, per_copied, edged, z_made, leaked = (a.sem(n) for n in (
            "per_turned", "per_copied", "edged", "z_made", "leaked"))
        made, scaled, rested, stored = a.sem("made"), a.sem("scaled"), a.sem("rested"), a.sem("stored")
        loads = [(we[:], w["W_edge"]), (be[:], w["b_edge"].rearrange("(p a) -> p a", a=1)),
                 (both[:, :, 0:D], chunked(w["W_conv"])), (both[:, :, D:], chunked(w["W_res"])),
                 (bias[:], w["b_conv"].partition_broadcast(P)), (bias2[:], w["b_res"].partition_broadcast(P))]
        block = ctx.enter_context(nc.Block())
        BATCH = ((0, 4), (4, GROUP - 4))

        @block.sync
        def _(sp):
            for to, from_ in loads:
                sp.dma_start(to, from_, allow_slow_non_contiguous=True).then_inc(loaded, 16)

            def store(g, u, r):
                sp.wait_ge(scaled, g * GROUP + GROUP)
                sp.dma_start(tiled(conv_dram)[:, bass.ds(g * GROUP, GROUP), :],
                             sums[:, bass.ds(g * GROUP, GROUP), :]).then_inc(stored, 16)
            groups(sp, [(0, store)])
            sp.wait_ge(stored, 16 * GROUPS)

        @block.tensor
        def _(pe):
            pe.wait_ge(loaded, 16 * len(loads))

            def group(g, u, r):
                wait(pe, z_made, g * 2)
                wait_alone(pe, per_staged, g + 1, passed)
                for b, (k0, n) in enumerate(BATCH):
                    for t in range(n):
                        mm = nc.tensor.transpose(p_e[b][0:EDGE_F, t * P:t * P + P], per[:, k0 + t, :], c["ident"][:])
                    mm.then_inc(per_turned, 1)
                norm.turn(nc, pe, g, c["ident"])
                pe.wait_ge(per_copied, g * 2 + 2)
                for h in range(2):
                    nc.tensor.matmul(p_e[h][:, 0:HALF], we[:], perT[:, h * HALF:(h + 1) * HALF], start=True,
                                     stop=True).then_inc(edged, 1)
                pe.wait_ge(norm.copied, g * len(norm.BATCHES) + len(norm.BATCHES))
                pe.wait_ge(leaked, g + 1)
                for t in range(GROUP):
                    if t < 3:
                        wait(pe, rested, g * 2 * GROUP)
                    else:
                        pe.wait_ge(rested, g * 2 * GROUP + (t - 2) * 2)
                    for k in range(HC3):
                        lhsT = norm.xnT[:, k, t * P:t * P + P] if k < KC else pnT[:, t * P:t * P + P]
                        mm = nc.tensor.matmul(p_c[t % 3][:, :], lhsT, both[:, k, :], start=(k == 0), stop=(k == HC3 - 1))
                    mm.then_inc(made, 1)
            groups(pe, [(0, group)])

        @block.scalar
        def _(act):
            act.wait_ge(prepared, 3)
            nc.scalar.activation(dinv[:], dinv[:], ACT.Sqrt).then_inc(rooted, 1)

            def group(g, u, r):
                for b, (k0, n) in enumerate(BATCH):
                    act.wait_ge(per_turned, g * 2 + b + 1)
                    nc.scalar.activation(perT[:, k0 * P:(k0 + n) * P], p_e[b][0:EDGE_F, 0:n * P], ACT.Copy).then_inc(per_copied, 1)
                norm.on_scalar(nc, act, g)
                norm.copy(nc, act, g)
            groups(act, [(0, group)])

        @block.vector
        def _(v):
            v.wait_ge(loaded, 16 * len(loads))
            nc.vector.tensor_tensor(bias[:], bias[:], bias2[:], ALU.add).then_inc(prepared, 1)
            nc.vector.tensor_scalar(dinv[:], no_edges[:, 0:NT], -1.0, 1.0, ALU.mult, ALU.add).then_inc(prepared, 1)
            v.wait_ge(prepared, 2)
            nc.vector.reciprocal(dinv[:], dinv[:]).then_inc(prepared, 1)
            v.wait_ge(rooted, 1)

            def group(g, u, r):
                wait(v, per_turned, g * 2)
                nc.vector.tensor_scalar(per[:], per_node[:, bass.ds(g * GROUP, GROUP), :], 1.0, None,
                                        ALU.mult).then_inc(per_staged, 1)
                norm.on_vector(nc, v, g, lambda k: tile_of(x, g * GROUP + k))
                wait(v, made, g * GROUP)
                for h in range(2):
                    v.wait_ge(edged, g * 2 + h + 1)
                    nc.vector.tensor_scalar(z[:, h * HALF:(h + 1) * HALF], p_e[h][:, 0:HALF], be[:, 0:1], None,
                                            ALU.add).then_inc(z_made, 1)
                v.wait_ge(z_made, g * 2 + 2)
                nc.vector.scalar_tensor_tensor(pnT[:], pnT[:], 0.01, pnT[:], ALU.mult, ALU.max).then_inc(leaked, 1)
                v.wait_ge(leaked, g + 1)
                for t in range(GROUP):
                    n = g * GROUP + t
                    v.wait_ge(made, g * GROUP + t + 1)
                    nc.vector.tensor_scalar(tile_of(sums, n), p_c[t % 3][:, 0:D], cols(dinv, n), None,
                                            ALU.mult).then_inc(scaled, 1)
                    nc.vector.tensor_tensor(tile_of(rest, n), p_c[t % 3][:, D:2 * D], bias[:], ALU.add).then_inc(rested, 2)
                v.wait_ge(rested, g * 2 * GROUP + 2 * GROUP)
            groups(v, [(0, group)])


def convolve_end(nc, x, dinv, sums, rest):
    with ExitStack() as ctx:
        a = Alloc(nc, ctx, "conv_end")
        scaled, added = a.sem("scaled"), a.sem("added")
        block = ctx.enter_context(nc.Block())

        @block.vector
        def _(v):
            def scale(t, u, r):
                nc.vector.scalar_tensor_tensor(tile_of(rest, t), tile_of(sums, t), cols(dinv, t), tile_of(rest, t),
                                               ALU.mult, ALU.add).then_inc(scaled, 1)

            def add(t, u, r):
                v.wait_ge(scaled, t + 1)
                nc.vector.scalar_tensor_tensor(tile_of(x, t), tile_of(rest, t), 0.0, tile_of(x, t), ALU.max,
                                               ALU.add).then_inc(added, 1)
            pipelined(v, NT, GROUP, [(0, scale), (1, add)])

E3X = 4
HEADW = H * E3X
SCORES, VECTORS, PARTS = slice(0, H), slice(H, H + HEADW), slice(H + HEADW, H + HEADW + 3 * H)
KEPT = H + HEADW
ROWW = KEPT + 3 * H


def router_rows(nc, c, x, w, rows, target, top, table_dram):
    with ExitStack() as ctx:
        a = Alloc(nc, ctx, "router")
        norm = Normed(Alloc(nc, ctx, "router_n"))
        wg = a.sb("wg", [P, KC, HEADW])
        att = [a.sb(n, [P, HEADW]) for n in ("att_src", "att_dst")]
        row = a.sb("row", [P, GROUP, ROWW])
        prod = [a.sb(f"prod{i}", [P, GROUP, HEADW]) for i in range(2)]
        part = a.sb("part", [P, GROUP, H], BF16)
        left = a.sb("left", [P, GROUP, H])
        p_h = a.ps("h", [P, 512])
        loaded, cleared, made = a.sem("loaded"), a.sem("cleared"), a.sem("made")
        stepped, stored = a.sem("stepped"), a.sem("stored")
        loads = [(wg[:], chunked(w["W_gat"]))]
        loads += [(tile[:], w[n].rearrange("h e -> (h e)").partition_broadcast(P))
                  for n, tile in zip(("att_src", "att_dst"), att)]
        STEPS = 15
        block = ctx.enter_context(nc.Block())

        @block.gpsimd
        def _(pool):
            nc.gpsimd.memset(target[:], 0.0).then_inc(cleared, 1)
            nc.gpsimd.memset(top[:], 0.0).then_inc(cleared, 1)

        @block.sync
        def _(sp):
            for to, from_ in loads:
                sp.dma_start(to, from_, allow_slow_non_contiguous=True).then_inc(loaded, 16)

            def store(g, u, r):
                sp.wait_ge(stepped, g * STEPS + STEPS)
                sp.dma_start(tiled(table_dram)[:, bass.ds(g * GROUP, GROUP), :], row[:]).then_inc(stored, 16)
            groups(sp, [(0, store)])
            sp.wait_ge(stored, 16 * GROUPS)

        @block.tensor
        def _(pe):
            pe.wait_ge(loaded, 16 * len(loads))

            def group(g, u, r):
                norm.turn(nc, pe, g, c["ident"])
                pe.wait_ge(norm.copied, g * len(norm.BATCHES) + len(norm.BATCHES))
                wait(pe, stepped, g * STEPS)
                for t in range(GROUP):
                    for k in range(KC):
                        mm = nc.tensor.matmul(p_h[:, t * HEADW:(t + 1) * HEADW], norm.xnT[:, k, t * P:t * P + P],
                                              wg[:, k, :], start=(k == 0), stop=(k == KC - 1))
                mm.then_inc(made, 1)
            groups(pe, [(0, group)])

        @block.scalar
        def _(act):
            def group(g, u, r):
                norm.on_scalar(nc, act, g)
                norm.copy(nc, act, g)
            groups(act, [(0, group)])

        @block.vector
        def _(v):
            v.wait_ge(loaded, 16 * len(loads))
            v.wait_ge(cleared, 2)

            def group(g, u, r):
                norm.on_vector(nc, v, g, lambda k: tile_of(x, g * GROUP + k))
                done = [0]

                def step(ins):
                    done[0] += 1
                    ins.then_inc(stepped, 1)
                    v.wait_ge(stepped, g * STEPS + done[0])
                here = bass.ds(g * GROUP, GROUP)
                v.wait_ge(norm.turned, g * len(norm.BATCHES) + len(norm.BATCHES))
                wait(v, stored, g * 16)
                v.wait_ge(made, g + 1)
                step(nc.vector.tensor_scalar(row[:, :, VECTORS], p_h[:, 0:GROUP * HEADW].rearrange("p (t w) -> p t w", w=HEADW),
                                             1.0, None, ALU.mult))
                for i in range(2):
                    step(nc.vector.tensor_tensor(prod[i][:], row[:, :, VECTORS],
                                                 att[i][:].unsqueeze(1).to_broadcast([P, GROUP, HEADW]), ALU.mult))
                heads = [p[:].rearrange("p t (h e) -> p t h e", e=E3X) for p in prod]
                step(nc.vector.tensor_reduce(row[:, :, SCORES], heads[0], AX.X, ALU.add))
                step(nc.vector.tensor_reduce(target[:, here, :], heads[1], AX.X, ALU.add))
                step(nc.vector.tensor_scalar(top[:, here, :], row[:, :, SCORES], -1.0, None, ALU.mult))
                parts = row[:, :, PARTS].rearrange("p t (h i) -> p t h i", i=3)
                rest = row[:, :, SCORES]
                for i in range(3):
                    step(nc.vector.tensor_scalar(part[:], rest, 1.0, None, ALU.mult))
                    step(nc.vector.tensor_scalar(parts[:, :, :, i], part[:], 1.0, None, ALU.mult))
                    if i < 2:
                        step(nc.vector.tensor_tensor(left[:], rest, part[:], ALU.subtract))
                        rest = left[:]
                step(nc.vector.tensor_scalar(rows[:, here, :], row[:, :, 0:KEPT], 1.0, None, ALU.mult))
                assert done[0] == STEPS
            groups(v, [(0, group)])


def gather_batches(nc, pool, tiles, source, index, staged, passed, rows_dram, ring, arrived, freed):
    def batch(b, u, r):
        wait(pool, freed, b * 2 - 2)
        nc.gpsimd.tensor_copy(index[:, u, :], cols(source, b * UNROLL, UNROLL)).then_inc(staged, 1)
        wait_alone(pool, staged, b + 1, passed)
        for k in range(UNROLL):
            pool.indirect_dma_start(ring[:, u, k, :], None, rows_dram,
                                    bass.IndirectOffsetOnAxis(index[:, u, k:k + 1], 0)).then_inc(arrived[u], 16)
    pipelined(pool, tiles // UNROLL, 2, [(0, batch)])


def edge_rows(nc, c, source, lo, hi_row, table_dram, edge, top):
    st = GAT
    with ExitStack() as ctx:
        a = Alloc(nc, ctx, "edge_rows")
        W = UNROLL * 3 * H
        index = a.sb("index", [P, 2, UNROLL], I32)
        ring = a.sb("ring", [P, 2, UNROLL, ROWW])
        parts = a.sb("parts", [P, 2, W])
        partsT = a.sb("partsT", [W, 2, P], BF16)
        select = a.sb("select", [W, UNROLL * H, P], BF16)
        other = a.sb("other", [P, UNROLL, P], BF16)
        least = a.sb("least", [P, 4, H])
        p_t = [a.ps(f"t{i}", [P, 512]) for i in range(2)]
        p_s = [a.ps(f"s{i}", [P, 512]) for i in range(4)]
        arrived = a.sems("arrived", 2)
        staged, passed, freed = a.sem("staged"), a.sem("passed"), a.sem("freed")
        ones_made, selected = a.sem("ones_made"), a.sem("selected")
        turned, copied = a.sem("turned"), a.sem("copied")
        marked, scored, reduced, kept = a.sem("marked"), a.sem("scored"), a.sem("reduced"), a.sem("kept")
        block = ctx.enter_context(nc.Block())
        BATCHES = st.tiles // UNROLL

        @block.gpsimd
        def _(pool):
            nc.gpsimd.memset(select[:], 1.0).then_inc(ones_made, 1)
            pool.wait_ge(ones_made, 1)
            nc.gpsimd.affine_select(select[:], select[:], [[-3, UNROLL * H], [0, P]], ALU.is_ge, 0.0, base=0,
                                    channel_multiplier=1).then_inc(ones_made, 1)
            pool.wait_ge(ones_made, 2)
            nc.gpsimd.affine_select(select[:], select[:], [[3, UNROLL * H], [0, P]], ALU.is_ge, 0.0, base=2,
                                    channel_multiplier=-1).then_inc(selected, 1)
            gather_batches(nc, pool, st.tiles, source, index, staged, passed, table_dram, ring, arrived, freed)

        @block.scalar
        def _(act):
            def take(b, u, r):
                act.wait_ge(arrived[u], r * (16 * UNROLL) + 16 * UNROLL)
                wait(act, turned, b - 1)
                nc.scalar.activation(parts[:, u, :].rearrange("p (t w) -> p t w", w=3 * H), ring[:, u, :, PARTS],
                                     ACT.Copy).then_inc(freed, 1)
                nc.scalar.activation(edge[:, bass.ds(b * UNROLL, UNROLL), :], ring[:, u, :, 0:KEPT],
                                     ACT.Copy).then_inc(freed, 1)

            def copy(b, u, r):
                act.wait_ge(turned, b + 1)
                wait(act, scored, b * UNROLL - UNROLL)
                nc.scalar.activation(partsT[:, u, :], p_t[u][0:W, 0:P], ACT.Copy, scale=-1.0).then_inc(copied, 1)
            pipelined(act, BATCHES, 2, [(0, take), (0, copy)])

        @block.tensor
        def _(pe):
            pe.wait_ge(selected, 1)

            def turn(b, u, r):
                pe.wait_ge(freed, b * 2 + 2)
                wait(pe, copied, b - 1)
                nc.tensor.transpose(p_t[u][0:W, 0:P], parts[:, u, :], c["ident"][:]).then_inc(turned, 1)

            def score(b, u, r):
                pe.wait_ge(copied, b + 1)
                for k in range(UNROLL):
                    pe.wait_ge(marked, b * UNROLL + k + 1)
                    if isinstance(b, int):
                        wait(pe, reduced, b * UNROLL + k - 3)
                    else:
                        pe.wait_ge(reduced, b * UNROLL + (k - 3))
                    s = p_s[k % 4]
                    nc.tensor.matmul(s[:, :], other[:, k, :], c["drop4"][:], start=True, stop=False,
                                     skip_group_check=True)
                    for h in range(H):
                        mm = nc.tensor.matmul(s[:, h * P:h * P + P], select[:, k * H + h, :], partsT[:, u, :],
                                              start=False, stop=True, skip_group_check=True)
                    mm.then_inc(scored, 1)
            pipelined(pe, BATCHES, 2, [(0, turn), (1, score)])

        @block.vector
        def _(v):
            tile_regs = [None]
            MAXIMA, KEEP = 2, 3

            def load_tiles(i):
                tile_regs[0] = node_tiles(nc, st, hi_row, i, KEEP)

            def mark(t, u, r):
                if u % 4 == 0:
                    wait(v, scored, t - 4)
                    nc.vector.tensor_tensor(other[:, u:u + 4, :], c["iota"][:].unsqueeze(1).to_broadcast([P, 4, P]),
                                            cols(lo, t, 4).unsqueeze(2).to_broadcast([P, 4, P]),
                                            ALU.not_equal).then_inc(marked, 4)

            def maxima(t, u, r):
                v.wait_ge(scored, t + 1)
                wait(v, kept, t - 3)
                nc.vector.tensor_reduce(least[:, u % 4, :], p_s[u % 4][:, :].rearrange("p (h e) -> p h e", h=H), AX.X,
                                        ALU.min).then_inc(reduced, 1)

            def keep(t, u, r):
                n = tile_regs[0][KEEP + (u if u < UNROLL - KEEP else u - UNROLL)]
                v.wait_ge(reduced, t + 1)
                wait(v, kept, t)
                nc.vector.tensor_tensor(tile_of(top, n), least[:, u % 4, :], tile_of(top, n), ALU.min).then_inc(kept, 1)
            pipelined(v, st.tiles, UNROLL, [(0, mark), (MAXIMA, maxima), (KEEP, keep)], top=load_tiles)


def leaky(nc, out, z, slope):
    return nc.vector.scalar_tensor_tensor(out, z, slope, z, ALU.mult, ALU.max)


def loops_to_self(nc, rows, target, top, bounds, acc):
    with ExitStack() as ctx:
        a = Alloc(nc, ctx, "self")
        z = a.sb("z", [P, NB, H])
        whole = a.sb("whole", [P, NB, 2 * H])
        left = a.sb("left", [P, NB, 2 * H])
        stepped, exped = a.sem("stepped"), a.sem("exped")
        block = ctx.enter_context(nc.Block())
        nodes = slice(0, NT)

        @block.vector
        def _(v):
            done = [0]

            def step(ins):
                done[0] += 1
                ins.then_inc(stepped, 1)
                v.wait_ge(stepped, done[0])
            nc.vector.memset(acc[:], 0.0).then_inc(stepped, 1)
            done[0] += 1
            step(nc.vector.tensor_scalar(whole[:, :, 0:H], target[:], 1.0, None, ALU.mult))
            step(nc.vector.tensor_tensor(z[:], target[:], top[:], ALU.subtract))
            step(leaky(nc, whole[:, :, H:2 * H], z[:], 0.2))
            step(nc.vector.tensor_tensor(z[:, nodes, :], target[:, nodes, :], rows[:, :, SCORES], ALU.add))
            step(leaky(nc, top[:, nodes, :], z[:, nodes, :], 0.2))
            step(nc.vector.tensor_tensor(z[:, nodes, :], top[:, nodes, :], whole[:, nodes, H:2 * H], ALU.subtract))
            parts = [bounds[:, :, i * 2 * H:(i + 1) * 2 * H] for i in range(3)]
            step(nc.vector.tensor_scalar(parts[0], whole[:], 1.0, None, ALU.mult))
            step(nc.vector.tensor_tensor(left[:], whole[:], parts[0], ALU.subtract))
            step(nc.vector.tensor_scalar(parts[1], left[:], 1.0, None, ALU.mult))
            step(nc.vector.tensor_tensor(parts[2], left[:], parts[1], ALU.subtract))
            v.wait_ge(exped, 1)
            for h in range(H):
                vectors = acc[:, nodes, h * E3X:(h + 1) * E3X]
                nc.vector.tensor_tensor(vectors, rows[:, :, H + h * E3X:H + (h + 1) * E3X],
                                        acc[:, nodes, HEADW + h:HEADW + h + 1].to_broadcast([P, NT, E3X]), ALU.mult)

        @block.scalar
        def _(act):
            act.wait_ge(stepped, 7)
            nc.scalar.activation(acc[:, nodes, HEADW:], z[:, nodes, :], ACT.Exp).then_inc(exped, 1)


def edge_sums(nc, c, lo, hi_row, edge, bounds, acc):
    st = GAT
    with ExitStack() as ctx:
        a = Alloc(nc, ctx, "edge_sums")
        mine = a.sb("mine", [P, 2, UNROLL, P], BF16)
        mineT = a.sb("mineT", [P, 2, UNROLL, P], BF16)
        bound = a.sb("bound", [P, 2, UNROLL, 3 * 2 * H], BF16)
        z = a.sb("z", [P, 2, UNROLL, H])
        y = a.sb("y", [P, 2, UNROLL, H])
        msg = a.sb("msg", [P, 2, UNROLL, KEPT])
        left = a.sb("left", [P, 2, UNROLL, KEPT])
        split = a.sb("split", [P, 2, 3, UNROLL, KEPT], BF16)
        part = a.sb("part", [P, 2, UNROLL, KEPT])
        p_t = [a.ps(f"t{i}", [P, 512], BF16) for i in range(4)]
        p_b = [a.ps(f"b{i}", [P, 512]) for i in range(2)]
        p_a = [a.ps(f"a{i}", [P, 512]) for i in range(2)]
        marked, bounded, turned, copied = a.sem("marked"), a.sem("bounded"), a.sem("turned"), a.sem("copied")
        spread, zed, exped, sent = a.sem("spread"), a.sem("zed"), a.sem("exped"), a.sem("sent")
        multiplied, taken, summed = a.sem("multiplied"), a.sem("taken"), a.sem("summed")
        block = ctx.enter_context(nc.Block())
        BATCHES = st.tiles // UNROLL

        @block.gpsimd
        def _(pool):
            def bounds_of(b, u, r):
                regs = node_tiles(nc, st, hi_row, b, 0, mybir.EngineType.Pool)
                wait(pool, spread, b - 1)
                for k in range(UNROLL):
                    nc.gpsimd.tensor_copy(bound[:, u, k, :], tile_of(bounds, regs[k])).then_inc(bounded, 1)

            def add_up(b, u, r):
                regs = node_tiles(nc, st, hi_row, b, 0, mybir.EngineType.Pool)
                pool.wait_ge(taken, b + 1)
                for k in range(UNROLL):
                    wait(pool, summed, b * UNROLL + k)
                    nc.gpsimd.tensor_tensor(tile_of(acc, regs[k]), tile_of(acc, regs[k]), part[:, u, k, :],
                                            ALU.add).then_inc(summed, 1)
            pipelined(pool, BATCHES, 2, [(0, bounds_of), (2, add_up)], peel=2)

        @block.tensor
        def _(pe):
            def sum_up(b, u, r):
                pe.wait_ge(sent, b * 5 + 5)
                wait(pe, taken, b - 1)
                for k in range(UNROLL):
                    for i in range(3):
                        mm = nc.tensor.matmul(p_a[u][:, k * KEPT:(k + 1) * KEPT], mine[:, u, k, :],
                                              split[:, u, i, k, :], start=(i == 0), stop=(i == 2))
                mm.then_inc(multiplied, 1)

            def spread_bounds(b, u, r):
                pe.wait_ge(bounded, b * UNROLL + UNROLL)
                wait(pe, copied, b * 2 + 2)
                wait(pe, zed, b * 4 - 4)
                for k in range(UNROLL):
                    for i in range(3):
                        mm = nc.tensor.matmul(p_b[u][:, k * 2 * H:(k + 1) * 2 * H], mineT[:, u, k, :],
                                              bound[:, u, k, i * 2 * H:(i + 1) * 2 * H], start=(i == 0), stop=(i == 2))
                mm.then_inc(spread, 1)

            def turn(b, u, r):
                for half in range(2):
                    wait(pe, copied, b * 2 - 3 + half)
                    pe.wait_ge(marked, b * 2 + half + 1)
                    for k in range(4 * half, 4 * half + 4):
                        mm = nc.tensor.transpose(p_t[2 * u + half][:, k % 4 * P:k % 4 * P + P], mine[:, u, k, :],
                                                 c["ident_bf"][:])
                    mm.then_inc(turned, 1)
            pipelined(pe, BATCHES, 2, [(2, sum_up), (1, spread_bounds), (0, turn)], peel=2)

        @block.scalar
        def _(act):
            def copy(b, u, r):
                wait(act, spread, b - 1)
                for half in range(2):
                    act.wait_ge(turned, b * 2 + half + 1)
                    nc.scalar.activation(mineT[:, u, 4 * half:4 * half + 4, :].rearrange("p k n -> p (k n)"),
                                         p_t[2 * u + half][:, :], ACT.Copy).then_inc(copied, 1)

            def weigh(b, u, r):
                act.wait_ge(zed, b * 4 + 4)
                wait(act, sent, b * 5 - 5)
                nc.scalar.activation(msg[:, u, :, HEADW:], z[:, u, :, :], ACT.Exp).then_inc(exped, 1)

            def take(b, u, r):
                act.wait_ge(multiplied, b + 1)
                wait(act, summed, (b - 1) * UNROLL)
                nc.scalar.activation(part[:, u, :, :].rearrange("p k w -> p (k w)"), p_a[u][:, 0:UNROLL * KEPT],
                                     ACT.Copy).then_inc(taken, 1)
            pipelined(act, BATCHES, 2, [(1, weigh), (2, take), (0, copy)], peel=2)

        @block.vector
        def _(v):
            def mark(b, u, r):
                wait(v, multiplied, b - 1)
                for k in range(0, UNROLL, 4):
                    nc.vector.tensor_tensor(mine[:, u, k:k + 4, :], c["iota"][:].unsqueeze(1).to_broadcast([P, 4, P]),
                                            cols(lo, b * UNROLL + k, 4).unsqueeze(2).to_broadcast([P, 4, P]),
                                            ALU.is_equal).then_inc(marked, 1)

            def exponents(b, u, r):
                v.wait_ge(spread, b + 1)
                wait(v, exped, b - 1)
                bd = p_b[u][:, 0:UNROLL * 2 * H].rearrange("p (k w) -> p k w", w=2 * H)
                here = bass.ds(b * UNROLL, UNROLL)
                nc.vector.tensor_tensor(z[:, u, :, :], edge[:, here, SCORES], bd[:, :, 0:H], ALU.add).then_inc(zed, 1)
                v.wait_ge(zed, b * 4 + 1)
                leaky(nc, y[:, u, :, :], z[:, u, :, :], 0.2).then_inc(zed, 1)
                v.wait_ge(zed, b * 4 + 2)
                nc.vector.tensor_tensor(z[:, u, :, :], y[:, u, :, :], bd[:, :, H:2 * H], ALU.subtract).then_inc(zed, 1)
                v.wait_ge(zed, b * 4 + 3)
                nc.vector.tensor_scalar(z[:, u, :, :], z[:, u, :, :], 0.0, None, ALU.min).then_inc(zed, 1)

            def message(b, u, r):
                here = bass.ds(b * UNROLL, UNROLL)
                wait(v, multiplied, b - 1)
                v.wait_ge(exped, b + 1)
                nc.vector.tensor_tensor(msg[:, u, :, 0:HEADW].rearrange("p k (h e) -> p k h e", e=E3X),
                                        edge[:, here, VECTORS].rearrange("p k (h e) -> p k h e", e=E3X),
                                        msg[:, u, :, HEADW:].unsqueeze(3).to_broadcast([P, UNROLL, H, E3X]),
                                        ALU.mult).then_inc(sent, 1)
                m, rest = msg[:, u, :, :], left[:, u, :, :]
                v.wait_ge(sent, b * 5 + 1)
                nc.vector.tensor_scalar(split[:, u, 0, :, :], m, 1.0, None, ALU.mult).then_inc(sent, 1)
                v.wait_ge(sent, b * 5 + 2)
                nc.vector.tensor_tensor(rest, m, split[:, u, 0, :, :], ALU.subtract).then_inc(sent, 1)
                v.wait_ge(sent, b * 5 + 3)
                nc.vector.tensor_scalar(split[:, u, 1, :, :], rest, 1.0, None, ALU.mult).then_inc(sent, 1)
                v.wait_ge(sent, b * 5 + 4)
                nc.vector.tensor_tensor(split[:, u, 2, :, :], rest, split[:, u, 1, :, :], ALU.subtract).then_inc(sent, 1)

            pipelined(v, BATCHES, 2, [(1, exponents), (0, mark), (1, message)], peel=2)


def gates(nc, w, acc, gate):
    with ExitStack() as ctx:
        a = Alloc(nc, ctx, "gates")
        vecs = {n: a.sb(n, [P, HEADW]) for n in ("b_gat", "ln_gamma", "ln_beta")}
        agg = a.sb("agg", [P, NT, HEADW])
        sq = a.sb("sq", [P, NT, HEADW])
        weight = a.sb("weight", [P, NT, H])
        mean = a.sb("mean", [P, NT])
        rstd = a.sb("rstd", [P, NT])
        score = a.sb("score", [P, NT, E3X])
        over = a.sb("over", [P, NT])
        rank = a.sb("rank", [P, NT, E3X])
        best = a.sb("best", [P, NT])
        loaded, stepped, inverted, rooted = a.sem("loaded"), a.sem("stepped"), a.sem("inverted"), a.sem("rooted")
        lowered, exped = a.sem("lowered"), a.sem("exped")
        block = ctx.enter_context(nc.Block())

        @block.sync
        def _(sp):
            for n, tile in vecs.items():
                sp.dma_start(tile[:], w[n].partition_broadcast(P)).then_inc(loaded, 16)

        @block.scalar
        def _(act):
            act.wait_ge(inverted, 1)
            nc.scalar.activation(rstd[:], mean[:], ACT.Sqrt).then_inc(rooted, 1)
            act.wait_ge(lowered, 1)
            nc.scalar.activation(gate[:], score[:], ACT.Exp).then_inc(exped, 1)

        @block.vector
        def _(v):
            done = [0]

            def step(ins):
                done[0] += 1
                ins.then_inc(stepped, 1)
                v.wait_ge(stepped, done[0])

            def per_node(tile, n):
                return tile[:].unsqueeze(2).to_broadcast([P, NT, n])

            def per_feature(name):
                return vecs[name][:].unsqueeze(1).to_broadcast([P, NT, HEADW])
            nodes = slice(0, NT)
            v.wait_ge(loaded, 16 * len(vecs))
            step(nc.vector.tensor_scalar(weight[:], acc[:, nodes, HEADW:], 1e-16, None, ALU.add))
            step(nc.vector.reciprocal(weight[:], weight[:]))
            for h in range(H):
                part = slice(h * E3X, (h + 1) * E3X)
                step(nc.vector.tensor_tensor(agg[:, :, part], acc[:, nodes, part],
                                             weight[:, :, h:h + 1].to_broadcast([P, NT, E3X]), ALU.mult))
            step(nc.vector.tensor_tensor(agg[:], agg[:], per_feature("b_gat"), ALU.add))
            step(nc.vector.tensor_reduce(mean[:], agg[:], AX.X, ALU.add))
            step(nc.vector.tensor_scalar(mean[:], mean[:], 1.0 / HEADW, None, ALU.mult))
            step(nc.vector.tensor_tensor(agg[:], agg[:], per_node(mean, HEADW), ALU.subtract))
            step(nc.vector.tensor_tensor(sq[:], agg[:], agg[:], ALU.mult))
            step(nc.vector.tensor_reduce(mean[:], sq[:], AX.X, ALU.add))
            step(nc.vector.tensor_scalar(mean[:], mean[:], 1.0 / HEADW, LN_EPS, ALU.mult, ALU.add))
            nc.vector.reciprocal(mean[:], mean[:]).then_inc(inverted, 1)
            v.wait_ge(rooted, 1)
            step(nc.vector.tensor_tensor(agg[:], agg[:], per_node(rstd, HEADW), ALU.mult))
            step(nc.vector.tensor_tensor(agg[:], agg[:], per_feature("ln_gamma"), ALU.mult))
            step(nc.vector.tensor_tensor(agg[:], agg[:], per_feature("ln_beta"), ALU.add))
            step(nc.vector.tensor_reduce(score[:], agg[:].rearrange("p t (h e) -> p t e h", e=E3X), AX.X, ALU.add))
            step(nc.vector.tensor_scalar(score[:], score[:], 1.0 / H, None, ALU.mult))
            step(nc.vector.memset(rank[:], 0.0))
            for e in range(E3X):
                for f in range(E3X):
                    if f != e:
                        step(nc.vector.tensor_tensor(over[:], score[:, :, f], score[:, :, e],
                                                     ALU.is_ge if f < e else ALU.is_gt))
                        step(nc.vector.tensor_tensor(rank[:, :, e], rank[:, :, e], over[:], ALU.add))
            step(nc.vector.tensor_scalar(rank[:], rank[:], 2.0, None, ALU.is_lt))
            step(nc.vector.tensor_reduce(best[:], score[:], AX.X, ALU.max))
            nc.vector.tensor_tensor(score[:], score[:], per_node(best, E3X), ALU.subtract).then_inc(lowered, 1)
            v.wait_ge(exped, 1)
            step(nc.vector.tensor_tensor(gate[:], gate[:], rank[:], ALU.mult))
            step(nc.vector.tensor_reduce(best[:], gate[:], AX.X, ALU.add))
            step(nc.vector.reciprocal(best[:], best[:]))
            nc.vector.tensor_tensor(gate[:], gate[:], per_node(best, E3X), ALU.mult)


def experts(nc, c, x, w, gate, out):
    E = E3X
    HID = 2 * D
    FC = HID // P
    with ExitStack() as ctx:
        a = Alloc(nc, ctx, "experts")
        norm = Normed(Alloc(nc, ctx, "experts_n"))
        w1 = a.sb("w1", [P, E, KC, HID])
        w2 = a.sb("w2", [P, E, FC, D])
        b1 = a.sb("b1", [P, E, FC])
        b2 = a.sb("b2", [E, D])
        share = a.sb("share", [P, GROUP, E])
        shareT = a.sb("shareT", [E, GW])
        hidden = a.sb("hidden", [P, 2, FC, GW])
        p_r = a.ps("r", [P, 512])
        p_1 = [a.ps(f"p1{i}", [P, 512]) for i in range(3)]
        p_o = [a.ps(f"po{i}", [P, 512]) for i in range(2)]
        loaded, shared = a.sem("loaded"), a.sem("shared")
        share_turned, share_copied = a.sem("share_turned"), a.sem("share_copied")
        made, activated, down, added, stored = (a.sem(n) for n in ("made", "activated", "down", "added", "stored"))
        loads = [(b2[:], w["b2"])]
        for e in range(E):
            loads += [(w1[:, e], chunked(w["W1"][e])), (w2[:, e], chunked(w["W2"][e])),
                      (b1[:, e, :], w["b1"][e].rearrange("(m p) -> p m", p=P))]
        PER = 2 * FC * E
        OUT = (E + 1) * GROUP
        block = ctx.enter_context(nc.Block())

        @block.sync
        def _(sp):
            for to, from_ in loads:
                sp.dma_start(to, from_, allow_slow_non_contiguous=True).then_inc(loaded, 16)
            for g in range(GROUPS):
                sp.wait_ge(added, g * OUT + OUT)
                full = min(GROUP, NT - 1 - g * GROUP)
                sp.dma_start(out[g * GW:g * GW + full * P, :].rearrange("(t p) d -> p t d", p=P),
                             x[:, g * GROUP:g * GROUP + full, :]).then_inc(stored, 16)
            sp.dma_start(out[(NT - 1) * P:N, :], x[0:LAST, NT - 1, :]).then_inc(stored, 16)
            sp.wait_ge(stored, 16 * (GROUPS + 1))

        @block.tensor
        def _(pe):
            pe.wait_ge(loaded, 16 * len(loads))

            def group(g, u, r):
                norm.turn(nc, pe, g, c["ident"])
                pe.wait_ge(shared, g + 1)
                for b, (k0, n) in enumerate(((0, 4), (4, GROUP - 4))):
                    wait(pe, share_copied, g * 2 + b)
                    for t in range(n):
                        mm = nc.tensor.transpose(p_r[0:E, t * P:t * P + P], share[:, k0 + t, :], c["ident"][:])
                    mm.then_inc(share_turned, 1)
                pe.wait_ge(norm.copied, g * len(norm.BATCHES) + len(norm.BATCHES))
                i, o = 0, 0

                def output(lhsTs, rhss):
                    nonlocal o
                    for t in range(GROUP):
                        wait(pe, added, g * OUT + (o - 1))
                        for k, rhs in enumerate(rhss):
                            mm = nc.tensor.matmul(p_o[o % 2][:, 0:D], lhsTs[k][:, t * P:t * P + P], rhs,
                                                  start=(k == 0), stop=(k == len(rhss) - 1))
                        mm.then_inc(down, 1)
                        o += 1

                def expert_output(e):
                    pe.wait_ge(activated, g * PER + (e + 1) * 2 * FC)
                    output([hidden[:, e % 2, k, :] for k in range(FC)], [w2[:, e, k, :] for k in range(FC)])
                for e in range(E):
                    for m in range(FC):
                        for h in range(2):
                            wait(pe, activated, g * PER + (i - 2))
                            for k in range(KC):
                                mm = nc.tensor.matmul(p_1[i % 3][:, 0:HALF], w1[:, e, k, m * P:m * P + P],
                                                      norm.xnT[:, k, h * HALF:(h + 1) * HALF],
                                                      start=(k == 0), stop=(k == KC - 1))
                            mm.then_inc(made, 1)
                            i += 1
                    if e == 0:
                        pe.wait_ge(share_copied, g * 2 + 2)
                        output([shareT], [b2[:]])
                    else:
                        expert_output(e - 1)
                expert_output(E - 1)
            groups(pe, [(0, group)])

        @block.scalar
        def _(act):
            act.wait_ge(loaded, 16 * len(loads))

            def group(g, u, r):
                norm.on_scalar(nc, act, g)
                norm.copy(nc, act, g)
                for b, (k0, n) in enumerate(((0, 4), (4, GROUP - 4))):
                    act.wait_ge(share_turned, g * 2 + b + 1)
                    wait(act, down, g * OUT)
                    nc.scalar.activation(shareT[:, k0 * P:(k0 + n) * P], p_r[0:E, 0:n * P],
                                         ACT.Copy).then_inc(share_copied, 1)
                i = 0
                for e in range(E):
                    wait(act, down, g * OUT + (e * GROUP if e >= 2 else 0))
                    for m in range(FC):
                        for h in range(2):
                            act.wait_ge(made, g * PER + i + 1)
                            nc.scalar.activation(hidden[:, e % 2, m, h * HALF:(h + 1) * HALF], p_1[i % 3][:, 0:HALF],
                                                 ACT.Gelu, bias=b1[:, e, m:m + 1]).then_inc(activated, 1)
                            i += 1
            groups(act, [(0, group)])

        @block.vector
        def _(v):
            def group(g, u, r):
                wait(v, added, g * OUT)
                nc.vector.tensor_scalar(share[:], gate[:, bass.ds(g * GROUP, GROUP), :], 1.0, None,
                                        ALU.mult).then_inc(shared, 1)
                norm.on_vector(nc, v, g, lambda k: tile_of(x, g * GROUP + k))
                v.wait_ge(shared, g + 1)
                v.wait_ge(norm.turned, g * len(norm.BATCHES) + len(norm.BATCHES))
                v.wait_ge(norm.normed, g * norm.steps + norm.steps)
                for o in range(OUT):
                    e, t = o // GROUP - 1, o % GROUP
                    v.wait_ge(down, g * OUT + o + 1)
                    if o >= GROUP:
                        v.wait_ge(added, g * OUT + (o + 1 - GROUP))
                    rows_of_x = tile_of(x, g * GROUP + t)
                    if e < 0:
                        nc.vector.tensor_tensor(rows_of_x, p_o[o % 2][:, 0:D], rows_of_x, ALU.add).then_inc(added, 1)
                    else:
                        nc.vector.scalar_tensor_tensor(rows_of_x, p_o[o % 2][:, 0:D], share[:, t, e:e + 1], rows_of_x,
                                                       ALU.mult, ALU.add).then_inc(added, 1)
            groups(v, [(0, group)])

def program(nc, t, out):
    def dram(name, shape, dt=F32):
        return nc.dram_tensor(name, shape, dt, kind="Internal").ap()

    def weights(prefix):
        return {n[len(prefix):]: ap for n, ap in t.items() if n.startswith(prefix)}

    kv_dram = dram("kv_rows", (NP, KVW))
    skip_dram = dram("skip_rows", (NP, D))
    sums_dram = dram("attention_sums", (P, NT, H * VW))
    by_src = dram("attributes_by_src", (P * BY_SRC.stride, ATTR_W))
    by_gat = dram("gat_edges_by_dst", (P * GAT.stride, 2), I32)
    hi2_dram = dram("attribute_node_tiles", (1, BY_SRC.tiles + 2 * UNROLL), I32)
    hi3_dram = dram("gat_node_tiles", (1, GAT.tiles + 2 * UNROLL), I32)
    slot3_dram = dram("gat_slots", (GAT.parts, GAT.cols), I32)
    conv_dram = dram("conv_rows", (NP, D))
    by_dst = dram("edges_by_dst", (P * BY_DST.stride, 2), I32)
    table_dram = dram("router_rows", (NP, ROWW))
    with ExitStack() as ctx:
        keep = Alloc(nc, ctx, "keep")
        c = constants(nc, keep)
        hi1 = keep.sb("hi1", [1, BY_DST.tiles + 2 * UNROLL], I32)
        x = keep.sb("x", [P, NT, D])
        src1 = keep.sb("src1", [P, BY_DST.tiles], I32)
        lo1 = keep.sb("lo1", [P, BY_DST.tiles])
        no_edges = keep.sb("no_edges", [P, NB])
        with ExitStack() as actx:
            b = Alloc(nc, actx, "by_src")
            slot = b.sb("slot", [BY_SRC.parts, BY_SRC.cols], I32)
            lo = b.sb("lo", [BY_SRC.parts, BY_SRC.cols], BF16)
            qT = Alloc(nc, actx, "attend").sb("qT", [P, KC, NP])
            with ExitStack() as sctx:
                b1 = Alloc(nc, sctx, "by_dst")
                slot1 = b1.sb("slot", [BY_DST.parts, BY_DST.cols], I32)
                pay1 = b1.sb("pay", [BY_DST.parts, BY_DST.cols, 2], I32)
                with ExitStack() as fctx:
                    empty = empty_slots(nc, fctx, GAT)
                    more = empty_attributes(nc, fctx, BY_SRC, BY_SRC.stride // 28)
                    fill = [(slots(by_dst), empty[:, 0:BY_DST.stride, :]), (slots(by_gat), empty[:])]
                    fill += [(part, more[:]) for part in parts_of(slots(by_src), 28)]
                    place_edges(nc, c, BY_DST, t["dst"], hi1, slot1, None, t["src"], pay1, fill, x, t["x"])
                scatter1 = Scatter(nc, b1, BY_DST, slot1, by_dst, 2, I32, 0, pay1, False)
                b3 = Alloc(nc, sctx, "place_gat")
                slot3 = b3.sb("slot", [GAT.parts, GAT.cols], I32)
                hi2 = b3.sb("hi2", [1, BY_SRC.tiles + 2 * UNROLL], I32)
                hi3 = b3.sb("hi3", [1, GAT.tiles + 2 * UNROLL], I32)
                with ExitStack() as pctx:
                    a2, a3 = Alloc(nc, pctx, "place_src"), Alloc(nc, pctx, "place_gat_now")
                    scratch = PlaceScratch(nc, a3, GAT.cols, GAT.tiles)
                    place2 = Place(nc, c, a2, scratch, BY_SRC, t["src"], hi2, slot, lo)
                    place3 = Place(nc, c, a3, scratch, GAT, t["L1_ffn_edge_index"][1], hi3, slot3, None, earlier=place2)
                    project(nc, c, x, weights("L0_gnn_"), qT, skip_dram, kv_dram, scatter1, [place2, place3])
                copy(nc, [(hi2_dram, hi2), (hi3_dram, hi3), (slot3_dram, slot3)], "gat_out")
            a = Alloc(nc, actx, "sums")
            acc = a.sb("acc", [P, NB, H * VW])
            top_score = a.sb("top_score", [P, NB, H])
            load_edges(nc, BY_DST, by_dst, src1, lo1, [(acc, 0.0), (top_score, 1e20), (no_edges, 0.0)])
            scatter2 = Scatter(nc, b, BY_SRC, slot, by_src, ATTR_W, F32, EDGE_F, lo, True, SCATTER // 2)
            attend(nc, c, src1, lo1, hi1, qT, kv_dram, acc, top_score, no_edges, sums_dram, scatter2,
                   t["edge_attr_64"])
        feed_forward(nc, c, x, weights("L0_gnn_"), sums_dram, skip_dram)
        gcn_ctx = ctx.enter_context(ExitStack())
        per_node = Alloc(nc, gcn_ctx, "gcn").sb("per_node", [P, NT, EDGE_F])
        with ExitStack() as sctx:
            b = Alloc(nc, sctx, "by_gat")
            hi2 = b.sb("hi2", [1, BY_SRC.tiles + 2 * UNROLL], I32)
            slot = b.sb("slot", [GAT.parts, GAT.cols], I32)
            pay = b.sb("pay", [GAT.parts, GAT.cols, 2], I32)
            copy(nc, [(slot, slot3_dram), (hi2, hi2_dram)], "gat_in")
            clear(nc, [(per_node, 0.0)])
            gat_payload(nc, GAT, t["L1_ffn_edge_index"][0], t["L1_ffn_edge_index"][1], pay)
            mixture(nc, c, x, weights("L0_ffn_"), Scatter(nc, b, GAT, slot, by_gat, 2, I32, 0, pay, False),
                    hi2, per_node, by_src)
        with ExitStack() as cctx:
            a = Alloc(nc, cctx, "conv")
            dinv = a.sb("dinv", [P, NT])
            sums = a.sb("sums", [P, NT, D])
            rest = a.sb("rest", [P, NT, D])
            convolve_dense(nc, c, x, weights("L1_gnn_"), per_node, no_edges, dinv, sums, rest, conv_dram)
            segment_sum(nc, c, BY_DST, hi1, D, sums, conv_dram, src1, lo1)
            convolve_end(nc, x, dinv, sums, rest)
        gcn_ctx.close()
        w = weights("L1_ffn_")
        gate = keep.sb("gate", [P, NT, E3X])
        with ExitStack() as gctx:
            a = Alloc(nc, gctx, "gat")
            rows = a.sb("rows", [P, NT, KEPT])
            target = a.sb("target", [P, NB, H])
            top = a.sb("top", [P, NB, H])
            bounds = a.sb("bounds", [P, NB, 3 * 2 * H], BF16)
            acc = a.sb("acc", [P, NB, KEPT])
            source = a.sb("source", [P, GAT.tiles], I32)
            lo = a.sb("lo", [P, GAT.tiles])
            hi_row = a.sb("hi_row", [1, GAT.tiles + 2 * UNROLL], I32)
            router_rows(nc, c, x, w, rows, target, top, table_dram)
            load_edges(nc, GAT, by_gat, source, lo)
            copy(nc, [(hi_row, hi3_dram)], "hi3_in")
            edge = a.sb("edge", [P, GAT.tiles, KEPT])
            edge_rows(nc, c, source, lo, hi_row, table_dram, edge, top)
            loops_to_self(nc, rows, target, top, bounds, acc)
            edge_sums(nc, c, lo, hi_row, edge, bounds, acc)
            gates(nc, w, acc, gate)
        experts(nc, c, x, w, gate, out)

def empty_slots(nc, ctx, st):
    a = Alloc(nc, ctx, f"empty_{st.name}")
    empty = a.sb("slots", [P, st.stride, 2], I32)
    with ExitStack() as bctx:
        zeroed = Alloc(nc, bctx, f"empty_{st.name}_now").sem("zeroed")
        block = bctx.enter_context(nc.Block())

        @block.vector
        def _(v):
            nc.vector.memset(empty[:], 0).then_inc(zeroed, 1)
            v.wait_ge(zeroed, 1)
            nc.vector.memset(empty[:, :, 1], PAD_LO)
    return empty


def copy(nc, what, name):
    with ExitStack() as ctx:
        copied = Alloc(nc, ctx, name).sem("copied")
        block = ctx.enter_context(nc.Block())

        @block.sync
        def _(sp):
            for to, from_ in what:
                sp.dma_start(to[:], from_[:]).then_inc(copied, 16)
            sp.wait_ge(copied, 16 * len(what))


def slots(rows_dram):
    return rows_dram.rearrange("(p t) w -> p t w", p=P)


def parts_of(slot_rows, n):
    wide = slot_rows.shape[1] // n
    return [slot_rows[:, i * wide:(i + 1) * wide, :] for i in range(n)]


def clear(nc, what):
    with nc.Block() as block:
        @block.vector
        def _(v):
            for tile, value in what:
                nc.vector.memset(tile[:], value)


def kernel(**inputs):
    import numpy as np
    import concourse.bacc as bacc
    from concourse.bass_utils import run_bass_kernel_spmd

    nc = bacc.Bacc("TRN2", target_bir_lowering=False, num_devices=1)
    arrays = {f"{name}_dram": np.ascontiguousarray(a) for name, a in inputs.items()}
    tensors = {name: nc.dram_tensor(f"{name}_dram", a.shape, mybir.dt.from_np(a.dtype), kind="ExternalInput").ap()
               for name, a in ((n, arrays[f"{n}_dram"]) for n in inputs)}
    out = nc.dram_tensor("out_dram", (N, D), F32, kind="ExternalOutput").ap()
    program(nc, tensors, out)
    result = run_bass_kernel_spmd(nc, [arrays], core_ids=[0])
    return result.results[0]["out_dram"]
```
